# Optimizing a Trainium2 kernel written in Bass

```python
import numpy as np
import jax
import jax.numpy as jnp

def _softmax(x, axis=-1):
    return jax.nn.softmax(x, axis=axis)

def _gelu(x):
    return jax.nn.gelu(x, approximate=True)

def _silu(x):
    return jax.nn.silu(x)

def _sigmoid(x):
    return jax.nn.sigmoid(x)

def _layernorm(x, axis=-1, eps=1e-05):
    m = jnp.mean(x, axis=axis, keepdims=True)
    v = jnp.var(x, axis=axis, keepdims=True)
    return (x - m) / jnp.sqrt(v + eps)

def _scatter_add(tgt, idx, src, axis=0):
    return tgt.at[idx].add(src)

def _segment_sum(src, seg, n):
    return jax.ops.segment_sum(src, seg, n)
kernel_name = 'mk_gnn_ffn_d4_gnn_r32_554b62'

def setup_inputs(seed: int=0):
    np.random.seed(seed)
    _w = jnp.asarray

    def _rec_inputs():
        import jax
        import jax.numpy as jnp
        _gk = jax.random.key(seed)
        x = -0.0003713 + 1 * jax.random.normal(jax.random.fold_in(_gk, 1), (3125, 256), jnp.float32)
        src = jax.random.randint(jax.random.fold_in(_gk, 2), (50000,), 0, 3125, jnp.int32)
        dst = jax.random.randint(jax.random.fold_in(_gk, 3), (50000,), 0, 3125, jnp.int32)
        _o = jnp.argsort(dst, stable=True)
        src = src[_o]
        dst = dst[_o]
        edge_attr_64 = 1.36993e-05 + 0.999972 * jax.random.normal(jax.random.fold_in(_gk, 11), (50000, 64), jnp.float32)
        edge_weight = jax.random.uniform(jax.random.fold_in(_gk, 13), (50000,), jnp.float32, 0.0, 0.999998)
        edge_weight1 = jax.random.uniform(jax.random.fold_in(_gk, 14), (50000, 1), jnp.float32, 0.0, 0.999998)
        return (x, src, dst, edge_attr_64, edge_weight, edge_weight1)
    x, src, dst, edge_attr_64, edge_weight, edge_weight1 = _rec_inputs()

    def _L0_gnn_setup():
        import jax, jax.numpy as jnp
        import numpy as np
        N_NODES = 50000
        DIM_H = 256
        N_EDGES = 25000
        LN_EPS = 1e-05

        def _layer_norm(x, g, b):
            mu = jnp.mean(x, axis=-1, keepdims=True)
            var = jnp.mean(jnp.square(x - mu), axis=-1, keepdims=True)
            return (x - mu) * jax.lax.rsqrt(var + LN_EPS) * g + b
        key = jax.random.key(seed)
        ks = jax.random.split(key, 12)
        d = DIM_H

        def lin(k, fan_in, fan_out):
            lim = 1.0 / np.sqrt(fan_in)
            kw, kb = jax.random.split(k)
            W = jax.random.uniform(kw, (fan_in, fan_out), jnp.float32, -lim, lim)
            b = jax.random.uniform(kb, (fan_out,), jnp.float32, -lim, lim)
            return (W, b)
        h = jax.random.normal(ks[0], (N_NODES, d), jnp.float32)
        e = jax.random.randint(ks[1], (2, N_EDGES), 0, N_NODES, jnp.int64)
        d2 = jax.random.uniform(ks[2], (N_EDGES, 1), jnp.float32)
        mW1, mb1 = lin(ks[3], 2 * d + 1, d)
        mW2, mb2 = lin(ks[4], d, d)
        ln_g = jnp.ones((d,), jnp.float32)
        ln_b = jnp.zeros((d,), jnp.float32)
        uW1, ub1 = lin(ks[5], 2 * d, d)
        uW2, ub2 = lin(ks[6], d, d)
        return {'h': h, 'e': e, 'd2': d2, 'mW1': mW1, 'mb1': mb1, 'ln_g': ln_g, 'ln_b': ln_b, 'mW2': mW2, 'mb2': mb2, 'uW1': uW1, 'ub1': ub1, 'uW2': uW2, 'ub2': ub2}
    _L0_gnn_all = _L0_gnn_setup()
    _L0_gnn_in = {k: v for k, v in _L0_gnn_all.items() if k in ('mW1', 'mb1', 'ln_g', 'ln_b', 'mW2', 'mb2', 'uW1', 'ub1', 'uW2', 'ub2')}
    del _L0_gnn_all

    def _L0_ffn_setup():
        import jax, jax.numpy as jnp
        import numpy as np
        E = 8
        K = 2
        D = 256
        H = 512
        DOUT = 256
        EPS = 1e-05
        key = jax.random.key(seed)
        ks = jax.random.split(key, 9)
        s = 0.02
        return {'x': jax.random.normal(ks[0], (4, 256, D), jnp.float32), 'gamma': 1.0 + 0.05 * jax.random.normal(ks[1], (D,), jnp.float32), 'beta': 0.05 * jax.random.normal(ks[2], (D,), jnp.float32), 'Wr': 0.01 * jax.random.normal(ks[3], (D, E), jnp.float32), 'br': jnp.zeros((E,), jnp.float32), 'W1': s * jax.random.normal(ks[4], (E, D, H), jnp.float32), 'b1': s * jax.random.normal(ks[5], (E, H), jnp.float32), 'W2': s * jax.random.normal(ks[6], (E, H, DOUT), jnp.float32), 'b2': s * jax.random.normal(ks[7], (E, DOUT), jnp.float32)}
    _L0_ffn_all = _L0_ffn_setup()
    _L0_ffn_in = {k: v for k, v in _L0_ffn_all.items() if k in ('gamma', 'beta', 'Wr', 'br', 'W1', 'b1', 'W2', 'b2')}
    del _L0_ffn_all

    def _L1_gnn_setup():
        import jax, jax.numpy as jnp
        import numpy as np
        N = 625
        E = 10000
        D = 256
        H = 8
        DH = D // H
        ED = 64
        FF = 4 * D
        EPS = 1e-05

        def _layernorm(x, g, b):
            m = jnp.mean(x, axis=-1, keepdims=True)
            v = jnp.var(x, axis=-1, keepdims=True)
            return (x - m) * jax.lax.rsqrt(v + EPS) * g + b

        def _edge_attention(xn, edge_index, ef, ew, Wq, bq, Wk, bk, Wv, bv, We, be, Wo, bo):
            n = xn.shape[0]
            scale = DH ** (-0.5)
            q = (xn @ Wq + bq).reshape(n, H, DH)
            k = (xn @ Wk + bk).reshape(n, H, DH)
            v = (xn @ Wv + bv).reshape(n, H, DH)
            src, dst = (edge_index[0], edge_index[1])
            ep = ef @ We + be
            scores = jnp.einsum('ehd,ehd->eh', q[dst], k[src] + ep[:, None, :]) * scale
            scores = scores * ew[:, None]
            m = jax.ops.segment_max(scores, dst, num_segments=n)
            m = jnp.where(jnp.isfinite(m), m, 0.0)
            ex = jnp.exp(scores - m[dst])
            s = jax.ops.segment_sum(ex, dst, num_segments=n)
            attn = ex / s[dst]
            out = jax.ops.segment_sum(attn[:, :, None] * v[src], dst, num_segments=n)
            out = out.reshape(n, D) @ Wo + bo
            return out
        key = jax.random.key(seed)
        ks = jax.random.split(key, 32)

        def lin_w(k, i, o):
            return (jax.random.normal(k, (i, o), jnp.float32) / np.sqrt(i)).astype(jnp.float32)
        return {'x': jax.random.normal(ks[0], (N, D), jnp.float32), 'edge_features': jax.random.normal(ks[1], (E, ED), jnp.float32), 'edge_weights': jax.random.uniform(ks[2], (E,), jnp.float32), 'edge_index': jax.random.randint(ks[3], (2, E), 0, N, dtype=jnp.int32), 'Wq': lin_w(ks[4], D, D), 'bq': jnp.zeros((D,), jnp.float32), 'Wk': lin_w(ks[5], D, D), 'bk': jnp.zeros((D,), jnp.float32), 'Wv': lin_w(ks[6], D, D), 'bv': jnp.zeros((D,), jnp.float32), 'We': lin_w(ks[7], ED, DH), 'be': jnp.zeros((DH,), jnp.float32), 'Wo': lin_w(ks[8], D, D), 'bo': jnp.zeros((D,), jnp.float32), 'ln1_g': jnp.ones((D,), jnp.float32), 'ln1_b': jnp.zeros((D,), jnp.float32), 'ln2_g': jnp.ones((D,), jnp.float32), 'ln2_b': jnp.zeros((D,), jnp.float32), 'W1': lin_w(ks[9], D, FF), 'b1': jnp.zeros((FF,), jnp.float32), 'W2': lin_w(ks[10], FF, D), 'b2': jnp.zeros((D,), jnp.float32), 'alpha': jnp.ones((1,), jnp.float32), 'beta': jnp.ones((1,), jnp.float32)}
    _L1_gnn_all = _L1_gnn_setup()
    _L1_gnn_in = {k: v for k, v in _L1_gnn_all.items() if k in ('Wq', 'bq', 'Wk', 'bk', 'Wv', 'bv', 'We', 'be', 'Wo', 'bo', 'ln1_g', 'ln1_b', 'ln2_g', 'ln2_b', 'W1', 'b1', 'W2', 'b2', 'alpha', 'beta')}
    del _L1_gnn_all

    def _L1_ffn_setup():
        import math
        import jax, jax.numpy as jnp
        import numpy as np
        CAPACITY_FACTOR = 1.25
        key = jax.random.key(seed)
        ks = jax.random.split(key, 5)
        B, L, D, F, E = (8, 256, 256, 1024, 8)
        h = jax.random.normal(ks[0], (B, L, D), dtype=jnp.float32)
        gate_w = jax.random.normal(ks[1], (D, E), dtype=jnp.float32) * 0.02
        gate_b = jnp.zeros((E,), dtype=jnp.float32)
        w1 = jax.random.normal(ks[2], (E, D, F), dtype=jnp.float32) * (1.0 / math.sqrt(D))
        b1 = jnp.zeros((E, F), dtype=jnp.float32)
        w2 = jax.random.normal(ks[3], (E, F, D), dtype=jnp.float32) * (1.0 / math.sqrt(F))
        b2 = jnp.zeros((E, D), dtype=jnp.float32)
        return {'h': h, 'gate_w': gate_w, 'gate_b': gate_b, 'w1': w1, 'b1': b1, 'w2': w2, 'b2': b2}
    _L1_ffn_all = _L1_ffn_setup()
    _L1_ffn_in = {k: v for k, v in _L1_ffn_all.items() if k in ('gate_w', 'gate_b', 'w1', 'b1', 'w2', 'b2')}
    del _L1_ffn_all

    def _L2_gnn_setup():
        import jax, jax.numpy as jnp
        import numpy as np
        N = 3125
        D = 256
        E_RAND = 100000
        NEG_SLOPE = 0.2

        def gat_layer(h, W, a, src, dst):
            h2 = h @ W
            s_src = h2 @ a[:D]
            s_dst = h2 @ a[D:]
            score = s_src[src] + s_dst[dst]
            e = jnp.exp(-jax.nn.leaky_relu(score, NEG_SLOPE))
            denom = jax.ops.segment_sum(e, src, num_segments=h.shape[0])
            num = jax.ops.segment_sum(e[:, None] * h2[dst], src, num_segments=h.shape[0])
            return jax.nn.elu(num / denom[:, None])
        key = jax.random.key(seed)
        k0, k1, k2, k3, k4, k5 = jax.random.split(key, 6)
        edges_rand = jax.random.randint(k0, (2, E_RAND), 0, N, dtype=jnp.int32)
        self_loops = jnp.tile(jnp.arange(N, dtype=jnp.int32)[None, :], (2, 1))
        edges = jnp.concatenate([edges_rand, self_loops], axis=1)
        scale_w = 1.0 / np.sqrt(D).astype(np.float32)
        scale_a = 0.1 / np.sqrt(D).astype(np.float32)
        emb = jax.random.normal(k1, (N, D), jnp.float32)
        W1 = jax.random.normal(k2, (D, D), jnp.float32) * scale_w
        a1 = jax.random.normal(k3, (2 * D,), jnp.float32) * scale_a
        W2 = jax.random.normal(k4, (D, D), jnp.float32) * scale_w
        a2 = jax.random.normal(k5, (2 * D,), jnp.float32) * scale_a
        return {'emb': emb, 'W1': W1, 'a1': a1, 'W2': W2, 'a2': a2, 'edges': edges}
    _L2_gnn_all = _L2_gnn_setup()
    _L2_gnn_in = {k: v for k, v in _L2_gnn_all.items() if k in ('W1', 'a1', 'W2', 'a2')}
    del _L2_gnn_all

    def _L2_ffn_setup():
        import jax, jax.numpy as jnp
        import numpy as np
        B, S, D = (8, 128, 256)
        H = 4 * D
        CAPACITY = 0.5
        key = jax.random.key(seed)
        ks = jax.random.split(key, 6)
        x = jax.random.normal(ks[0], (B, S, D), dtype=jnp.float32)
        attention_mask = jnp.zeros((B, 1, 1, S), dtype=jnp.float32)
        wr = jax.random.normal(ks[1], (D, 1), dtype=jnp.float32) * 0.02
        br = jnp.zeros((1,), dtype=jnp.float32)
        w1 = jax.random.normal(ks[2], (D, H), dtype=jnp.float32) * 0.02
        b1 = jnp.zeros((H,), dtype=jnp.float32)
        w2 = jax.random.normal(ks[3], (H, D), dtype=jnp.float32) * 0.02
        b2 = jnp.zeros((D,), dtype=jnp.float32)
        return {'x': x, 'attention_mask': attention_mask, 'wr': wr, 'br': br, 'w1': w1, 'b1': b1, 'w2': w2, 'b2': b2}
    _L2_ffn_all = _L2_ffn_setup()
    _L2_ffn_in = {k: v for k, v in _L2_ffn_all.items() if k in ('attention_mask', 'wr', 'br', 'w1', 'b1', 'w2', 'b2')}
    del _L2_ffn_all

    def _L3_gnn_setup():
        import jax, jax.numpy as jnp
        import numpy as np
        N_NODES = 3125
        N_EDGES = 50000
        IN_DIM = 256
        OUT_DIM = 256
        key = jax.random.key(seed)
        k1, k2, k3 = jax.random.split(key, 3)
        x = jax.random.normal(k1, (N_NODES, IN_DIM), dtype=jnp.float32)
        limit = 0.1 * np.sqrt(6.0 / (IN_DIM + OUT_DIM))
        W = jax.random.uniform(k2, (OUT_DIM, IN_DIM), dtype=jnp.float32, minval=-limit, maxval=limit)
        b = jnp.zeros((OUT_DIM,), dtype=jnp.float32)
        edge_index = jax.random.randint(k3, (2, N_EDGES), 0, N_NODES, dtype=jnp.int64)
        return {'x': x, 'W': W, 'b': b, 'edge_index': edge_index}
    _L3_gnn_all = _L3_gnn_setup()
    _L3_gnn_in = {k: v for k, v in _L3_gnn_all.items() if k in ('W', 'b')}
    del _L3_gnn_all

    def _L3_ffn_setup():
        import math
        import jax, jax.numpy as jnp
        import numpy as np
        CAPACITY_FACTOR = 1.25
        TOP_K = 2
        LN_EPS = 1e-05

        def _layer_norm(x, gamma, beta):
            mu = jnp.mean(x, axis=-1, keepdims=True)
            var = jnp.var(x, axis=-1, keepdims=True)
            return (x - mu) * jax.lax.rsqrt(var + LN_EPS) * gamma + beta
        key = jax.random.key(seed)
        ks = jax.random.split(key, 4)
        B, S, D, F, E = (8, 128, 256, 512, 8)
        x = jax.random.normal(ks[0], (B, S, D), dtype=jnp.float32)
        Wr = jax.random.normal(ks[1], (D, E), dtype=jnp.float32) / np.sqrt(D)
        br = jnp.zeros((E,), jnp.float32)
        W1 = jax.random.normal(ks[2], (E, D, F), dtype=jnp.float32) / np.sqrt(D)
        b1 = jnp.zeros((E, F), jnp.float32)
        W2 = jax.random.normal(ks[3], (E, F, D), dtype=jnp.float32) / np.sqrt(F)
        b2 = jnp.zeros((E, D), jnp.float32)
        gamma = jnp.ones((D,), jnp.float32)
        beta = jnp.zeros((D,), jnp.float32)
        return {'x': x, 'Wr': Wr, 'br': br, 'W1': W1, 'b1': b1, 'W2': W2, 'b2': b2, 'gamma': gamma, 'beta': beta}
    _L3_ffn_all = _L3_ffn_setup()
    _L3_ffn_in = {k: v for k, v in _L3_ffn_all.items() if k in ('Wr', 'br', 'W1', 'b1', 'W2', 'b2', 'gamma', 'beta')}
    del _L3_ffn_all
    return {'x': x, 'src': src, 'dst': dst, 'edge_attr_64': edge_attr_64, 'edge_weight': edge_weight, 'edge_weight1': edge_weight1, 'L0_gnn_mW1': _L0_gnn_in['mW1'], 'L0_gnn_mb1': _L0_gnn_in['mb1'], 'L0_gnn_ln_g': _L0_gnn_in['ln_g'], 'L0_gnn_ln_b': _L0_gnn_in['ln_b'], 'L0_gnn_mW2': _L0_gnn_in['mW2'], 'L0_gnn_mb2': _L0_gnn_in['mb2'], 'L0_gnn_uW1': _L0_gnn_in['uW1'], 'L0_gnn_ub1': _L0_gnn_in['ub1'], 'L0_gnn_uW2': _L0_gnn_in['uW2'], 'L0_gnn_ub2': _L0_gnn_in['ub2'], 'L0_ffn_gamma': _L0_ffn_in['gamma'], 'L0_ffn_beta': _L0_ffn_in['beta'], 'L0_ffn_Wr': _L0_ffn_in['Wr'], 'L0_ffn_br': _L0_ffn_in['br'], 'L0_ffn_W1': _L0_ffn_in['W1'], 'L0_ffn_b1': _L0_ffn_in['b1'], 'L0_ffn_W2': _L0_ffn_in['W2'], 'L0_ffn_b2': _L0_ffn_in['b2'], 'L1_gnn_Wq': _L1_gnn_in['Wq'], 'L1_gnn_bq': _L1_gnn_in['bq'], 'L1_gnn_Wk': _L1_gnn_in['Wk'], 'L1_gnn_bk': _L1_gnn_in['bk'], 'L1_gnn_Wv': _L1_gnn_in['Wv'], 'L1_gnn_bv': _L1_gnn_in['bv'], 'L1_gnn_We': _L1_gnn_in['We'], 'L1_gnn_be': _L1_gnn_in['be'], 'L1_gnn_Wo': _L1_gnn_in['Wo'], 'L1_gnn_bo': _L1_gnn_in['bo'], 'L1_gnn_ln1_g': _L1_gnn_in['ln1_g'], 'L1_gnn_ln1_b': _L1_gnn_in['ln1_b'], 'L1_gnn_ln2_g': _L1_gnn_in['ln2_g'], 'L1_gnn_ln2_b': _L1_gnn_in['ln2_b'], 'L1_gnn_W1': _L1_gnn_in['W1'], 'L1_gnn_b1': _L1_gnn_in['b1'], 'L1_gnn_W2': _L1_gnn_in['W2'], 'L1_gnn_b2': _L1_gnn_in['b2'], 'L1_gnn_alpha': _L1_gnn_in['alpha'], 'L1_gnn_beta': _L1_gnn_in['beta'], 'L1_ffn_gate_w': _L1_ffn_in['gate_w'], 'L1_ffn_gate_b': _L1_ffn_in['gate_b'], 'L1_ffn_w1': _L1_ffn_in['w1'], 'L1_ffn_b1': _L1_ffn_in['b1'], 'L1_ffn_w2': _L1_ffn_in['w2'], 'L1_ffn_b2': _L1_ffn_in['b2'], 'L2_gnn_W1': _L2_gnn_in['W1'], 'L2_gnn_a1': _L2_gnn_in['a1'], 'L2_gnn_W2': _L2_gnn_in['W2'], 'L2_gnn_a2': _L2_gnn_in['a2'], 'L2_ffn_attention_mask': _L2_ffn_in['attention_mask'], 'L2_ffn_wr': _L2_ffn_in['wr'], 'L2_ffn_br': _L2_ffn_in['br'], 'L2_ffn_w1': _L2_ffn_in['w1'], 'L2_ffn_b1': _L2_ffn_in['b1'], 'L2_ffn_w2': _L2_ffn_in['w2'], 'L2_ffn_b2': _L2_ffn_in['b2'], 'L3_gnn_W': _L3_gnn_in['W'], 'L3_gnn_b': _L3_gnn_in['b'], 'L3_ffn_Wr': _L3_ffn_in['Wr'], 'L3_ffn_br': _L3_ffn_in['br'], 'L3_ffn_W1': _L3_ffn_in['W1'], 'L3_ffn_b1': _L3_ffn_in['b1'], 'L3_ffn_W2': _L3_ffn_in['W2'], 'L3_ffn_b2': _L3_ffn_in['b2'], 'L3_ffn_gamma': _L3_ffn_in['gamma'], 'L3_ffn_beta': _L3_ffn_in['beta']}

def reference(x, src, dst, edge_attr_64, edge_weight, edge_weight1, L0_gnn_mW1, L0_gnn_mb1, L0_gnn_ln_g, L0_gnn_ln_b, L0_gnn_mW2, L0_gnn_mb2, L0_gnn_uW1, L0_gnn_ub1, L0_gnn_uW2, L0_gnn_ub2, L0_ffn_gamma, L0_ffn_beta, L0_ffn_Wr, L0_ffn_br, L0_ffn_W1, L0_ffn_b1, L0_ffn_W2, L0_ffn_b2, L1_gnn_Wq, L1_gnn_bq, L1_gnn_Wk, L1_gnn_bk, L1_gnn_Wv, L1_gnn_bv, L1_gnn_We, L1_gnn_be, L1_gnn_Wo, L1_gnn_bo, L1_gnn_ln1_g, L1_gnn_ln1_b, L1_gnn_ln2_g, L1_gnn_ln2_b, L1_gnn_W1, L1_gnn_b1, L1_gnn_W2, L1_gnn_b2, L1_gnn_alpha, L1_gnn_beta, L1_ffn_gate_w, L1_ffn_gate_b, L1_ffn_w1, L1_ffn_b1, L1_ffn_w2, L1_ffn_b2, L2_gnn_W1, L2_gnn_a1, L2_gnn_W2, L2_gnn_a2, L2_ffn_attention_mask, L2_ffn_wr, L2_ffn_br, L2_ffn_w1, L2_ffn_b1, L2_ffn_w2, L2_ffn_b2, L3_gnn_W, L3_gnn_b, L3_ffn_Wr, L3_ffn_br, L3_ffn_W1, L3_ffn_b1, L3_ffn_W2, L3_ffn_b2, L3_ffn_gamma, L3_ffn_beta):
    import jax
    import jax.numpy as jnp

    def _L0_gnn_ref(h, e, d2, mW1, mb1, ln_g, ln_b, mW2, mb2, uW1, ub1, uW2, ub2):
        import jax, jax.numpy as jnp
        import numpy as np
        N_NODES = 50000
        DIM_H = 256
        N_EDGES = 25000
        LN_EPS = 1e-05

        def _layer_norm(x, g, b):
            mu = jnp.mean(x, axis=-1, keepdims=True)
            var = jnp.mean(jnp.square(x - mu), axis=-1, keepdims=True)
            return (x - mu) * jax.lax.rsqrt(var + LN_EPS) * g + b
        ei, ej = (e[0], e[1])
        hi = h[ei]
        hj = h[ej]
        x = jnp.concatenate((hi, hj, d2), axis=-1)
        msg = jax.nn.silu(x @ mW1 + mb1)
        msg = _layer_norm(msg, ln_g, ln_b)
        msg = jax.nn.silu(msg @ mW2 + mb2)
        agg = jax.ops.segment_sum(msg, ei, num_segments=h.shape[0])
        y = jnp.concatenate((h, agg), axis=-1)
        y = jax.nn.silu(y @ uW1 + ub1) @ uW2 + ub2
        return h + y

    def _L0_ffn_ref(x, gamma, beta, Wr, br, W1, b1, W2, b2):
        import jax, jax.numpy as jnp
        import numpy as np
        E = 8
        K = 2
        D = 256
        H = 512
        DOUT = 256
        EPS = 1e-05
        mu = jnp.mean(x, axis=-1, keepdims=True)
        var = jnp.mean(jnp.square(x - mu), axis=-1, keepdims=True)
        xn = (x - mu) * jax.lax.rsqrt(var + EPS) * gamma + beta
        logits = jnp.einsum('bsd,de->bse', xn, Wr) + br
        top_vals, top_idx = jax.lax.top_k(logits, K)
        w = jax.nn.softmax(top_vals, axis=-1)
        w_full = jnp.einsum('bsk,bske->bse', w, jax.nn.one_hot(top_idx, E, dtype=w.dtype))
        y = jnp.zeros(x.shape[:-1] + (DOUT,), x.dtype)
        for e in range(E):
            h = jax.nn.gelu(jnp.einsum('bsd,dh->bsh', xn, W1[e]) + b1[e], approximate=False)
            y_e = jnp.einsum('bsh,hd->bsd', h, W2[e]) + b2[e]
            y = y + y_e * w_full[..., e, None]
        return y

    def _L1_gnn_ref(x, edge_features, edge_weights, edge_index, Wq, bq, Wk, bk, Wv, bv, We, be, Wo, bo, ln1_g, ln1_b, ln2_g, ln2_b, W1, b1, W2, b2, alpha, beta):
        import jax, jax.numpy as jnp
        import numpy as np
        N = 625
        E = 10000
        D = 256
        H = 8
        DH = D // H
        ED = 64
        FF = 4 * D
        EPS = 1e-05

        def _layernorm(x, g, b):
            m = jnp.mean(x, axis=-1, keepdims=True)
            v = jnp.var(x, axis=-1, keepdims=True)
            return (x - m) * jax.lax.rsqrt(v + EPS) * g + b

        def _edge_attention(xn, edge_index, ef, ew, Wq, bq, Wk, bk, Wv, bv, We, be, Wo, bo):
            n = xn.shape[0]
            scale = DH ** (-0.5)
            q = (xn @ Wq + bq).reshape(n, H, DH)
            k = (xn @ Wk + bk).reshape(n, H, DH)
            v = (xn @ Wv + bv).reshape(n, H, DH)
            src, dst = (edge_index[0], edge_index[1])
            ep = ef @ We + be
            scores = jnp.einsum('ehd,ehd->eh', q[dst], k[src] + ep[:, None, :]) * scale
            scores = scores * ew[:, None]
            m = jax.ops.segment_max(scores, dst, num_segments=n)
            m = jnp.where(jnp.isfinite(m), m, 0.0)
            ex = jnp.exp(scores - m[dst])
            s = jax.ops.segment_sum(ex, dst, num_segments=n)
            attn = ex / s[dst]
            out = jax.ops.segment_sum(attn[:, :, None] * v[src], dst, num_segments=n)
            out = out.reshape(n, D) @ Wo + bo
            return out
        xn = _layernorm(x, ln1_g, ln1_b)
        attn_out = _edge_attention(xn, edge_index, edge_features, edge_weights, Wq, bq, Wk, bk, Wv, bv, We, be, Wo, bo)
        x = x + alpha * attn_out
        xn = _layernorm(x, ln2_g, ln2_b)
        ff = jax.nn.gelu(xn @ W1 + b1, approximate=False) @ W2 + b2
        x = x + beta * ff
        return x

    def _L1_ffn_ref(h, gate_w, gate_b, w1, b1, w2, b2):
        import math
        import jax, jax.numpy as jnp
        import numpy as np
        CAPACITY_FACTOR = 1.25
        B, L, D = h.shape
        E = gate_w.shape[1]
        T = B * L
        C = max(1, math.ceil(CAPACITY_FACTOR * T / E))
        x = h.reshape(T, D)
        logits = x @ gate_w + gate_b
        probs = jax.nn.softmax(logits, axis=-1)
        idx = jnp.argmax(probs, axis=-1)
        prb = jnp.take_along_axis(probs, idx[:, None], axis=1)[:, 0]
        one_hot = jax.nn.one_hot(idx, E, dtype=jnp.float32)
        pos = (jnp.cumsum(one_hot, axis=0) * one_hot).sum(-1).astype(jnp.int32) - 1
        kept = pos < C
        pos_safe = jnp.where(kept, pos, C)
        buf = jnp.zeros((E, C, D), dtype=h.dtype).at[idx, pos_safe].set(x, mode='drop')
        hmid = jax.nn.relu(jnp.einsum('ecd,edf->ecf', buf, w1) + b1[:, None, :])
        ybuf = jnp.einsum('ecf,efd->ecd', hmid, w2) + b2[:, None, :]
        pos_g = jnp.minimum(pos, C - 1)
        y_tok = ybuf[idx, pos_g] * (prb * kept)[:, None]
        y = y_tok.reshape(B, L, D)
        y = jnp.nan_to_num(y, nan=0.0, posinf=10000.0, neginf=-10000.0)
        return y

    def _L2_gnn_ref(emb, W1, a1, W2, a2, edges):
        import jax, jax.numpy as jnp
        import numpy as np
        N = 3125
        D = 256
        E_RAND = 100000
        NEG_SLOPE = 0.2

        def gat_layer(h, W, a, src, dst):
            h2 = h @ W
            s_src = h2 @ a[:D]
            s_dst = h2 @ a[D:]
            score = s_src[src] + s_dst[dst]
            e = jnp.exp(-jax.nn.leaky_relu(score, NEG_SLOPE))
            denom = jax.ops.segment_sum(e, src, num_segments=h.shape[0])
            num = jax.ops.segment_sum(e[:, None] * h2[dst], src, num_segments=h.shape[0])
            return jax.nn.elu(num / denom[:, None])
        src, dst = (edges[0], edges[1])
        h = gat_layer(emb, W1, a1, src, dst)
        h = gat_layer(h, W2, a2, src, dst)
        return h

    def _L2_ffn_ref(x, attention_mask, wr, br, w1, b1, w2, b2):
        import jax, jax.numpy as jnp
        import numpy as np
        B, S, D = (8, 128, 256)
        H = 4 * D
        CAPACITY = 0.5
        b, s, d = x.shape
        weights = (jnp.einsum('bsd,do->bso', x, wr) + br)[..., 0]
        k = max(1, int(CAPACITY * s))
        kk = k - 1 if k > 1 else 1
        _, idx = jax.lax.top_k(weights, k)
        sel_idx = idx[:, :kk]
        sel = jnp.take_along_axis(x, sel_idx[:, :, None], axis=1)
        h = jax.nn.gelu(jnp.einsum('bkd,dh->bkh', sel, w1) + b1)
        y = jnp.einsum('bkh,hd->bkd', h, w2) + b2
        w_sel = jnp.take_along_axis(weights, sel_idx, axis=1)
        y = y * w_sel[..., None]
        batch_idx = jnp.arange(b)[:, None]
        processed = jnp.zeros_like(x).at[batch_idx, sel_idx].set(y)
        return processed + x

    def _L3_gnn_ref(x, W, b, edge_index):
        import jax, jax.numpy as jnp
        import numpy as np
        N_NODES = 3125
        N_EDGES = 50000
        IN_DIM = 256
        OUT_DIM = 256
        num_nodes = x.shape[0]
        src, tgt = (edge_index[0], edge_index[1])
        xt = jnp.einsum('ni,oi->no', x, W) + b
        out = jax.ops.segment_sum(xt[src], tgt, num_segments=num_nodes)
        deg = jax.ops.segment_sum(jnp.ones_like(tgt, dtype=x.dtype), tgt, num_segments=num_nodes)
        out = out / (deg + 1.0)[:, None]
        return out

    def _L3_ffn_ref(x, Wr, br, W1, b1, W2, b2, gamma, beta):
        import math
        import jax, jax.numpy as jnp
        import numpy as np
        CAPACITY_FACTOR = 1.25
        TOP_K = 2
        LN_EPS = 1e-05

        def _layer_norm(x, gamma, beta):
            mu = jnp.mean(x, axis=-1, keepdims=True)
            var = jnp.var(x, axis=-1, keepdims=True)
            return (x - mu) * jax.lax.rsqrt(var + LN_EPS) * gamma + beta
        B, S, D = x.shape
        E = Wr.shape[1]
        N = B * S
        K = TOP_K
        logits = jnp.mean(x, axis=1) @ Wr + br
        routing_weights = jax.nn.softmax(logits, axis=-1)
        capacity = float(math.ceil(N * CAPACITY_FACTOR / E))
        expected_loads = routing_weights.sum(axis=0) * (N / B)
        scale = jnp.where(expected_loads > capacity, capacity / expected_loads, 1.0)
        routing_weights = jax.nn.softmax(routing_weights * scale, axis=-1)
        rw_tok = jnp.broadcast_to(routing_weights[:, None, :], (B, S, E)).reshape(N, E)
        top_w, top_i = jax.lax.top_k(rw_tok, K)
        top_w = jax.nn.softmax(top_w, axis=-1)
        xf = x.reshape(N, D)
        h = jax.nn.gelu(jnp.einsum('nd,edf->enf', xf, W1) + b1[:, None, :], approximate=False)
        y = jnp.einsum('enf,efd->end', h, W2) + b2[:, None, :]
        w_dense = jnp.zeros((N, E), x.dtype).at[jnp.arange(N)[:, None], top_i].add(top_w)
        out = jnp.einsum('ne,end->nd', w_dense, y).reshape(B, S, D)
        out = _layer_norm(out + x, gamma, beta)
        return out
    edge_index = jnp.stack([src, dst])
    x = x + _L0_gnn_ref(_layernorm(x, axis=-1), edge_index, edge_weight1, L0_gnn_mW1, L0_gnn_mb1, L0_gnn_ln_g, L0_gnn_ln_b, L0_gnn_mW2, L0_gnn_mb2, L0_gnn_uW1, L0_gnn_ub1, L0_gnn_uW2, L0_gnn_ub2)
    x = x + _L0_ffn_ref(_layernorm(x, axis=-1)[None], L0_ffn_gamma, L0_ffn_beta, L0_ffn_Wr, L0_ffn_br, L0_ffn_W1, L0_ffn_b1, L0_ffn_W2, L0_ffn_b2)[0]
    x = x + _L1_gnn_ref(_layernorm(x, axis=-1), edge_attr_64, edge_weight, edge_index, L1_gnn_Wq, L1_gnn_bq, L1_gnn_Wk, L1_gnn_bk, L1_gnn_Wv, L1_gnn_bv, L1_gnn_We, L1_gnn_be, L1_gnn_Wo, L1_gnn_bo, L1_gnn_ln1_g, L1_gnn_ln1_b, L1_gnn_ln2_g, L1_gnn_ln2_b, L1_gnn_W1, L1_gnn_b1, L1_gnn_W2, L1_gnn_b2, L1_gnn_alpha, L1_gnn_beta)
    x = x + _L1_ffn_ref(_layernorm(x, axis=-1)[None], L1_ffn_gate_w, L1_ffn_gate_b, L1_ffn_w1, L1_ffn_b1, L1_ffn_w2, L1_ffn_b2)[0]
    x = x + _L2_gnn_ref(_layernorm(x, axis=-1), L2_gnn_W1, L2_gnn_a1, L2_gnn_W2, L2_gnn_a2, edge_index)
    x = x + _L2_ffn_ref(_layernorm(x, axis=-1)[None], L2_ffn_attention_mask, L2_ffn_wr, L2_ffn_br, L2_ffn_w1, L2_ffn_b1, L2_ffn_w2, L2_ffn_b2)[0]
    x = x + _L3_gnn_ref(_layernorm(x, axis=-1), L3_gnn_W, L3_gnn_b, edge_index)
    x = x + _L3_ffn_ref(_layernorm(x, axis=-1)[None], L3_ffn_Wr, L3_ffn_br, L3_ffn_W1, L3_ffn_b1, L3_ffn_W2, L3_ffn_b2, L3_ffn_gamma, L3_ffn_beta)[0]
    return x

_drawn_inputs = setup_inputs


def setup_inputs(seed=0):
    import zlib

    import numpy as np

    out = dict(_drawn_inputs(seed))
    spreads = {'L0_gnn_ln_g': (1.0, 0.2),
     'L0_gnn_ln_b': (0.0, 0.1),
     'L0_ffn_br': (0.0, 0.295),
     'L1_gnn_bq': (0.0, 0.688),
     'L1_gnn_bk': (0.0, 0.8),
     'L1_gnn_bv': (0.0, 0.1),
     'L1_gnn_be': (0.0, 0.8),
     'L1_gnn_bo': (0.0, 0.1),
     'L1_gnn_ln1_g': (1.0, 0.2),
     'L1_gnn_ln1_b': (0.0, 0.1),
     'L1_gnn_ln2_g': (1.0, 0.2),
     'L1_gnn_ln2_b': (0.0, 0.353),
     'L1_gnn_b1': (0.0, 0.353),
     'L1_gnn_b2': (0.0, 0.1),
     'L1_ffn_gate_b': (0.0, 0.347),
     'L1_ffn_b1': (0.0, 0.8),
     'L1_ffn_b2': (0.0, 0.8),
     'L2_ffn_b1': (0.0, 0.8),
     'L2_ffn_b2': (0.0, 0.8),
     'L3_gnn_b': (0.0, 1.312),
     'L3_ffn_br': (0.0, 0.1),
     'L3_ffn_b1': (0.0, 2.0),
     'L3_ffn_b2': (0.0, 2.0),
     'L3_ffn_gamma': (1.0, 0.6),
     'L3_ffn_beta': (0.0, 1.403)}
    factors = {'edge_weight1': 8.0,
     'L0_gnn_mb1': 3.013,
     'L0_gnn_ub1': 8.0,
     'L0_gnn_ub2': 2.755,
     'L0_ffn_gamma': 8.0,
     'L0_ffn_beta': 8.0,
     'L0_ffn_Wr': 2.941,
     'L0_ffn_b1': 8.0,
     'L0_ffn_b2': 7.745,
     'L2_gnn_a1': 31.452,
     'L2_gnn_a2': 43.952,
     'L2_ffn_wr': 7.192,
     'L2_ffn_w1': 7.464,
     'L2_ffn_w2': 6.936,
     'L3_gnn_W': 20.88,
     'L3_ffn_W1': 2.676}
    for name, (base, spread) in spreads.items():
        noise = np.random.default_rng([zlib.crc32(name.encode()), seed]).standard_normal(out[name].shape)
        drawn = base * np.exp(spread * noise) if base else spread * noise
        out[name] = jnp.asarray(drawn.astype(out[name].dtype))
    for name, factor in factors.items():
        out[name] = (out[name] * factor).astype(out[name].dtype)
    return out
```

```python
import numpy as np
import concourse.bass as bass
from concourse import mybir
from contextlib import ExitStack

fp32 = mybir.dt.float32
bf16 = mybir.dt.bfloat16
i32 = mybir.dt.int32
u32 = mybir.dt.uint32
ALU = mybir.AluOpType
ACT = mybir.ActivationFunctionType
AX = mybir.AxisListType

N, D, E = 3125, 256, 50000
NT = 25
P = N // NT
ET = E // P
GT = 4
G = ET // GT
HEADS, DH = 8, 32
RADIX = 64
SORT_TILES = 8
SCAN = 16
FAR = 4096
CHUNK = 5
CW = CHUNK * 128
HW = CW // 2
EPS = 1e-5
BIG = 3.0e38
REC_W = (4, 68)
FLT_MAX = 3.4028234663852886e38


class Link:

    def __init__(self, eng, sem):
        self.eng, self.sem, self.n = eng, sem, 0

    def restart(self):
        self.eng.sem_clear(self.sem)
        self.n = 0

    def __call__(self, ins):
        self.mark(ins)
        self.eng.wait_ge(self.sem, self.n)

    def mark(self, ins):
        self.n += 1
        ins.then_inc(self.sem, 1)


class Stage:

    def __init__(self, K, name):
        self.K, self.name, self.ctx, self.sems, self.held = K, name, ExitStack(), ExitStack(), []
        self.ctx.push(self.give_back)

    def sb(self, name, shape, dt=fp32):
        return self.ctx.enter_context(self.K.nc.sbuf_tensor(self.name + name, shape, dt))

    def ps(self, name, shape, dt=fp32):
        return self.ctx.enter_context(self.K.nc.psum_tensor(self.name + name, shape, dt))

    def sem(self, name):
        self.held.append(self.sems.enter_context(self.K.nc.semaphore(self.name + name)))
        return self.held[-1]

    def indirect(self, name):
        return self.K.nc.alloc_semaphore(self.name + name)

    def link(self, eng, name):
        return Link(eng, self.sem(name))

    def give_back(self, failure, *_):
        if failure:
            return
        with self.K.nc.Block() as block:

            @block.sync
            def _(sp):
                for sem in self.held:
                    sp.sem_clear(sem)

        self.sems.close()


class Kernel:
    pass


def over(ap, shape):
    return ap.to_broadcast(shape)


def await_(eng, sem, value):
    if isinstance(value, int) and value <= 0:
        return
    eng.wait_ge(sem, value)


def hold(K, eng, sem, value):
    if isinstance(value, int) and value <= 0:
        return
    eng.wait_ge(sem, value)
    eng.sem_inc(K.tick)


def skewed(eng, total, phases):
    lag_max = max(lag for lag, _ in phases)
    start = 2 * ((lag_max + 3) // 2)
    end = total - total % 2
    for t in range(start):
        for lag, fn in phases:
            if t - lag >= 0:
                fn(t - lag, (t - lag) % 2, (t - lag) // 2)
    with eng.Fori(start // 2, end // 2) as i:
        for u in range(2):
            for lag, fn in phases:
                fn(2 * i + (u - lag), (u - lag) % 2, i + (u - lag) // 2)
    for t in range(end, total + lag_max):
        for lag, fn in phases:
            if t - lag < total:
                fn(t - lag, (t - lag) % 2, (t - lag) // 2)


def nodes(ap):
    return ap.rearrange("(p t) w -> p t w", t=NT)


def shared(K, dram):
    nc = K.nc

    def sb(name, shape, dt=fp32):
        return nc.alloc_sbuf_tensor(name, shape, dt)

    K.dram = dram
    K.tick = nc.alloc_semaphore("tick")
    K.X = sb("X", [P, NT, D])
    K.H = sb("H", [P, NT, D])
    K.ident = sb("ident", [128, 128])
    K.identb = sb("identb", [128, 128], bf16)
    K.before = sb("before", [128, 128])
    K.lower = sb("lower", [128, 128])
    K.ones = sb("ones", [128, 128])
    K.iota64 = sb("iota64", [128, RADIX], bf16)
    K.bounds = dram("bounds", (2, 2, RADIX * RADIX))
    K.idx = [sb(f"idx{k}", [P, ET, 2], i32) for k in range(2)]
    K.fk = [sb(f"fk{k}", [P, ET, 2]) for k in range(2)]
    K.runs_on = [sb(f"runs_on{k}", [128, ET]) for k in range(2)]
    K.ss = dram("ss", (N, 4))
    K.scores = sb("scores", [P, ET, HEADS])
    K.at = [sb(f"at{k}", [P, 2, NT], i32) for k in range(2)]
    K.sums = {w: dram(f"sums{w}", (E, w)) for w in (D, D + 1, D + HEADS)}
    K.running = {w: dram(f"running{w}", (ET, w)) for w in (D, D + 1, D + HEADS)}
    K.rec = [dram(f"rec{k}", (E + 1, w)) for k, w in enumerate(REC_W)]


def constants(K, a):
    nc = K.nc
    zeros_done, made, loaded = (nc.alloc_semaphore(x) for x in ("c_zeros", "c_made", "c_x"))
    with nc.Block() as block:

        @block.sync
        def _(sp):
            sp.dma_start(K.X[:, :, :], nodes(a["x"])).then_inc(loaded, 16)
            sp.wait_ge(loaded, 16)

        @block.gpsimd
        def _(pool):
            pool.memset(K.ident[:, :], 0.0).then_inc(zeros_done, 1)
            pool.memset(K.identb[:, :], 0.0).then_inc(zeros_done, 1)
            pool.memset(K.ones[:, :], 1.0).then_inc(zeros_done, 1)
            pool.memset(K.before[:, :], 1.0).then_inc(zeros_done, 1)
            pool.memset(K.lower[:, :], 1.0).then_inc(zeros_done, 1)
            pool.wait_ge(zeros_done, 5)
            for m in (K.ident, K.identb):
                pool.affine_select(out=m[:, :], in_=m[:, :], compare_op=ALU.not_equal, fill=1.0, base=0,
                                   pattern=[[-1, 128]], channel_multiplier=1).then_inc(made, 1)
            pool.affine_select(out=K.before[:, :], in_=K.before[:, :], compare_op=ALU.is_gt, fill=0.0, base=0,
                               pattern=[[1, 128]], channel_multiplier=-1).then_inc(made, 1)
            pool.affine_select(out=K.lower[:, :], in_=K.lower[:, :], compare_op=ALU.is_gt, fill=0.0, base=0,
                               pattern=[[-1, 128]], channel_multiplier=1).then_inc(made, 1)
            pool.iota(K.iota64[:, :], pattern=[[1, RADIX]], base=0, channel_multiplier=0,
                      allow_small_or_imprecise_dtypes=True).then_inc(made, 1)
            pool.wait_ge(made, 5)


def sort_edges(K, a):
    nc = K.nc
    S = Stage(K, "so_")
    B, NB = SORT_TILES, ET // SORT_TILES
    SIDE = [slice(0, RADIX), slice(RADIX, 2 * RADIX)]
    with S.ctx:
        ei = S.sb("ei", [P, 2, ET], i32)
        hl = S.sb("hl", [P, 2, 2, ET], i32)
        digit = S.sb("digit", [P, 2, 2, ET], bf16)
        ef = S.sb("ef", [P, 2, ET])
        ew = S.sb("ew", [P, 2, ET])
        hot = [S.sb(f"hot{i}", [P, 2, B, 2 * RADIX], bf16) for i in range(2)]
        hotT = [S.sb(f"hotT{i}", [128, 2, B, P], bf16) for i in range(2)]
        highf = [S.sb(f"highf{i}", [RADIX, 2, B, P]) for i in range(2)]
        base0 = S.sb("first", [RADIX, 2, RADIX])
        runs = S.sb("runs", [RADIX, 2, RADIX])
        tot = S.sb("tot", [RADIX, 2, RADIX])
        base = [S.sb(f"base{i}", [RADIX, 2, RADIX]) for i in range(2)]
        acc = [S.sb(f"acc{i}", [P, 4, B]) for i in range(2)]
        junk = S.sb("junk", [P, 2, 4, 128])
        zero = S.sb("zero", [P, 128], bf16)
        place = [S.sb(f"place{i}", [P, 2, B], i32) for i in range(2)]
        rec = [[S.sb(f"rec{k}{i}", [P, B, w]) for i in range(2)] for k, w in enumerate(REC_W)]
        tail = S.sb("tail", [1, 4])
        counts = S.ps("counts", [RADIX, 4, 2 * RADIX])
        transposed = S.ps("tr", [128, 2, B, 128], bf16)
        same = [S.ps(f"same{i}", [P, 2, 256]) for i in range(2)]
        before = [S.ps(f"below{i}", [P, 512]) for i in range(2)]
        loaded, hot_ready, counted, summed = S.sem("ld"), S.sem("hot"), S.sem("cnt"), S.sem("sum")
        tables_ready = S.sem("tables")
        offset_ready, tail_ready, stored = S.sem("offs"), S.sem("tail"), S.sem("st")
        attr = a["edge_attr_64"].rearrange("(p t) w -> p t w", t=ET)

        def one_hots(dve, b, slot):
            for h in range(2):
                for k in range(2):
                    ins = dve.tensor_tensor(
                        hot[slot][:, k, :, SIDE[h]],
                        over(digit[:, h, k, bass.ds(b * B, B)].unsqueeze(2), [P, B, RADIX]),
                        over(K.iota64[0:P, :].unsqueeze(1), [P, B, RADIX]), ALU.is_equal)
            return ins

        with nc.Block() as block:

            @block.sync
            def _(sp):
                for k, n in enumerate(("src", "dst")):
                    sp.dma_start(ei[:, k, :], a[n].rearrange("(p t) -> p t", t=ET)).then_inc(loaded, 16)
                sp.dma_start(ew[:, 0, :], a["edge_weight1"].rearrange("(p t) o -> p (t o)", t=ET)).then_inc(loaded, 16)
                sp.dma_start(ew[:, 1, :], a["edge_weight"].rearrange("(p t) -> p t", t=ET)).then_inc(loaded, 16)
                sp.wait_ge(tail_ready, 1)
                for k in range(2):
                    sp.dma_start(K.rec[k][E:E + 1, 0:4], tail[:, :]).then_inc(stored, 16)
                sp.wait_ge(tables_ready, 1)
                for k in range(2):
                    for c, table in enumerate((base0, tot)):
                        sp.dma_start(K.bounds[k, c, :].rearrange("(h l) -> h l", l=RADIX), table[:, k, :]).then_inc(stored, 16)
                sp.wait_ge(stored, 96)

            @block.vector
            def _(dve):
                link = S.link(dve, "l1")
                dve.memset(tail[:, :], -1.0).then_inc(tail_ready, 1)
                link(dve.memset(zero[:, :], 0.0))
                dve.wait_ge(loaded, 64)
                link(dve.tensor_single_scalar(hl[:, 0, :, :], ei[:, :, :], 6, ALU.logical_shift_right))
                link(dve.tensor_single_scalar(hl[:, 1, :, :], ei[:, :, :], RADIX - 1, ALU.bitwise_and))
                link(dve.tensor_copy(digit[:, :, :, :], hl[:, :, :, :]))
                link(dve.tensor_copy(ef[:, :, :], ei[:, :, :]))

                def hots(b, slot, turn):
                    await_(dve, counted, b - 1)
                    one_hots(dve, b, slot).then_inc(hot_ready, 1)

                skewed(dve, NB, [(0, hots)])
                dve.wait_ge(counted, NB)
                link(dve.tensor_copy(tot[:, :, :], counts[:, 0, :].rearrange("p (k l) -> p k l", k=2)))
                for k in range(2):
                    ins = dve.tensor_tensor_scan(runs[:, k, :], tot[:, k, :], tot[:, k, :], 0.0, ALU.add, ALU.bypass)
                ins.then_inc(summed, 1)
                dve.wait_ge(summed, 1)
                link(dve.tensor_tensor(base0[:, :, :], runs[:, :, :], tot[:, :, :], ALU.subtract))
                dve.wait_ge(offset_ready, 1)
                link(dve.tensor_tensor(base0[:, :, :], base0[:, :, :],
                                       over(counts[:, 1, 0:2].unsqueeze(2), [RADIX, 2, RADIX]), ALU.add))
                dve.tensor_copy(base[0][:, :, :], base0[:, :, :]).then_inc(tables_ready, 1)

            @block.tensor
            def _(pe):
                pe.wait_ge(hot_ready, 1)
                pe.matmul(counts[:, 0, :], zero[:, 0:RADIX], zero[:, :], start=True, stop=True)

                def count(b, slot, turn):
                    pe.wait_ge(hot_ready, b + 1)
                    for j in range(B):
                        for k in range(2):
                            ins = pe.matmul(counts[:, 0, SIDE[k]], hot[slot][:, k, j, SIDE[0]], hot[slot][:, k, j, SIDE[1]],
                                            start=False, stop=True, skip_group_check=True)
                    ins.then_inc(counted, 1)

                skewed(pe, NB, [(0, count)])
                pe.wait_ge(summed, 1)
                pe.matmul(counts[:, 1, 0:2], K.before[0:RADIX, 0:RADIX], runs[:, :, RADIX - 1], start=True, stop=True).then_inc(offset_ready, 1)

        hot_ready, turned, turned_copied = S.sem("hot2"), S.sem("turned"), S.sem("tcopied")
        hist_done, base_ready, found, looked = S.sem("hist"), S.sem("base"), S.sem("found"), S.sem("looked")
        placed = S.sem("placed")
        attr_loaded = [S.sem(f"attr{i}") for i in range(2)]
        scattered = [S.indirect(f"scat{i}") for i in range(2)]
        with nc.Block() as block:

            @block.sync
            def _(sp):
                def load(b, slot, turn):
                    await_(sp, scattered[slot], 32 * B * turn)
                    sp.dma_start(rec[1][slot][:, :, 4:68], attr[:, bass.ds(b * B, B), :]).then_inc(attr_loaded[slot], 16)

                skewed(sp, NB, [(0, load)])

            @block.gpsimd
            def _(pool):
                def scatter(b, slot, turn):
                    hold(K, pool, placed, b + 1)
                    hold(K, pool, attr_loaded[slot], 16 * turn + 16)
                    for j in range(B):
                        for k in range(2):
                            pool.indirect_dma_start(
                                K.rec[k], bass.IndirectOffsetOnAxis(ap=place[slot][:, k, j:j + 1], axis=0),
                                rec[k][slot][:, j, :], None).then_inc(scattered[slot], 16)

                skewed(pool, NB, [(0, scatter)])
                for u in range(2):
                    pool.wait_ge(scattered[u], 32 * B * (NB // 2))

            @block.vector
            def _(dve):
                link = S.link(dve, "l2")

                def hots(b, slot, turn):
                    hold(K, dve, hist_done, B * (b - 1))
                    one_hots(dve, b, slot).then_inc(hot_ready, 1)

                def places(b, slot, turn):
                    link.restart()
                    for j in range(B):
                        t = b * B + j
                        c = j % 2
                        await_(dve, hist_done, t + 1)
                        await_(dve, found, t)
                        dve.scalar_tensor_tensor(base[1 - c][:, :, :].rearrange("p k l -> p (k l)"), counts[:, 0, :], 1.0,
                                                 base0[:, :, :].rearrange("p k l -> p (k l)"),
                                                 ALU.mult, ALU.add).then_inc(base_ready, 1)
                        dve.wait_ge(found, t + 1)
                        for k in range(2):
                            dve.scalar_tensor_tensor(
                                junk[:, c, k, 0:RADIX], before[c][:, k * RADIX:(k + 1) * RADIX], 1.0, hot[slot][:, k, j, SIDE[1]],
                                ALU.mult, ALU.mult, accum_out=acc[slot][:, k, j:j + 1])
                            ins = dve.scalar_tensor_tensor(
                                junk[:, c, 2 + k, 0:P], same[c][:, k, 0:P], 1.5, K.lower[0:P, 0:P],
                                ALU.is_gt, ALU.mult, accum_out=acc[slot][:, 2 + k, j:j + 1])
                        ins.then_inc(looked, 1)
                    dve.wait_ge(looked, b * B + B)
                    hold(K, dve, scattered[slot], 32 * B * turn)
                    dve.tensor_tensor(place[slot][:, :, :], acc[slot][:, 0:2, :], acc[slot][:, 2:4, :], ALU.add)
                    tiles = bass.ds(b * B, B)
                    for k in range(2):
                        for c in range(2):
                            dve.tensor_copy(rec[k][slot][:, :, c], ef[:, c, tiles])
                        dve.tensor_copy(rec[k][slot][:, :, 2], ew[:, k, tiles])
                        ins = dve.tensor_copy(rec[k][slot][:, :, 3], ew[:, k, tiles])
                    ins.then_inc(placed, 1)

                skewed(dve, NB, [(0, hots), (1, places)])

            @block.scalar
            def _(act):
                def copy(b, slot, turn):
                    await_(act, turned, b + 1)
                    hold(K, act, found, B * (b - 1))
                    act.activation(hotT[slot][:, :, :, :], transposed[:, :, :, 0:P], ACT.Copy)
                    act.activation(highf[slot][:, :, :, :], transposed[0:RADIX, :, :, 0:P], ACT.Copy).then_inc(turned_copied, 1)

                skewed(act, NB, [(0, copy)])

            @block.tensor
            def _(pe):
                pe.matmul(counts[:, 0, :], zero[:, 0:RADIX], zero[:, :], start=True, stop=True)

                def turn_(b, slot, turn):
                    await_(pe, hot_ready, b + 1)
                    hold(K, pe, turned_copied, b)
                    for h in range(2):
                        for j in range(B):
                            ins = pe.transpose(transposed[:, h, j, 0:P], hot[slot][:, h, j, :], K.identb[0:P, 0:P])
                    ins.then_inc(turned, 1)

                def look(b, slot, turn):
                    pe.wait_ge(turned_copied, b + 1)
                    for j in range(B):
                        t = b * B + j
                        c = j % 2
                        await_(pe, looked, t - 1)
                        for k in range(2):
                            pe.matmul(same[c][:, k, 0:P], hotT[slot][:, k, j, :], hotT[slot][:, k, j, :], start=True, stop=True)
                        await_(pe, base_ready, t)
                        for k in range(2):
                            ins = pe.matmul(counts[:, 0, SIDE[k]], hot[slot][:, k, j, SIDE[0]], hot[slot][:, k, j, SIDE[1]],
                                            start=False, stop=True, skip_group_check=True)
                        ins.then_inc(hist_done, 1)
                        for k in range(2):
                            ins = pe.matmul(before[c][:, k * RADIX:(k + 1) * RADIX], highf[slot][:, k, j, :], base[c][:, k, :],
                                            start=True, stop=True)
                        ins.then_inc(found, 1)

                skewed(pe, NB, [(0, turn_), (1, look)])


def indices(K):
    nc = K.nc
    S = Stage(K, "ix_")
    with S.ctx:
        R = [S.sb(f"R{k}", [P, ET, 4]) for k in range(2)]
        bn = S.sb("bn", [P, 2, 2, NT])
        w = S.sb("w", [P, 2, 6, NT])
        wi = S.sb("wi", [P, 2, NT], i32)
        lastkey = S.sb("lastkey", [128, 2, ET])
        row = [S.ps(f"row{k}", [128, 512]) for k in range(2)]
        loaded, keys_ready, row_ready = S.sem("ld"), S.sem("keys"), S.sem("row")
        with nc.Block() as block:

            @block.sync
            def _(sp):
                for k in range(2):
                    sp.dma_start(R[k][:, :, :], K.rec[k][0:E, 0:4].rearrange("(t p) c -> p t c", p=P)).then_inc(loaded, 16)
                    for c in range(2):
                        sp.dma_start(bn[:, k, c, :], K.bounds[k, c, 0:N].rearrange("(p t) -> p t", t=NT)).then_inc(loaded, 16)

            @block.tensor
            def _(pe):
                pe.wait_ge(keys_ready, 1)
                for k in range(2):
                    pe.matmul(row[k][:, 0:ET], over(K.ident[0:P, P - 1:P], [P, 128]), K.fk[k][:, :, 0],
                              start=True, stop=True).then_inc(row_ready, 1)

            @block.vector
            def _(dve):
                link = S.link(dve, "l")
                dve.wait_ge(loaded, 96)
                for k in range(2):
                    dve.tensor_copy(K.fk[k][:, :, 0], R[k][:, :, k])
                    dve.tensor_copy(K.fk[k][:, :, 1], R[k][:, :, 2])
                    ins = dve.tensor_copy(K.idx[k][:, :, :], R[k][:, :, 0:2])
                ins.then_inc(keys_ready, 1)
                begin, count = bn[:, :, 0, :], bn[:, :, 1, :]
                last, x, tile, prev, t1, t2 = (w[:, :, i, :] for i in range(6))
                link(dve.scalar_tensor_tensor(last, begin, -1.0, count, ALU.add, ALU.add))
                link(dve.tensor_scalar(x, last, 0.5, 1.0 / P, ALU.add, ALU.mult))
                link(dve.tensor_copy(wi[:, :, :], x))
                link(dve.tensor_copy(tile, wi[:, :, :]))
                link(dve.tensor_tensor(t1, tile, x, ALU.is_gt))
                link(dve.tensor_tensor(tile, tile, t1, ALU.subtract))
                link(dve.tensor_scalar(t2, tile, float(P), None, ALU.mult))
                link(dve.tensor_tensor(t1, begin, t2, ALU.is_ge))
                link(dve.tensor_scalar(t1, t1, float(FAR), -1.0, ALU.mult, ALU.add))
                link(dve.tensor_tensor(prev, tile, t1, ALU.add))
                link(dve.tensor_single_scalar(t2, count, 0.0, ALU.is_equal))
                link(dve.tensor_scalar(t2, t2, float(FAR * 16), None, ALU.mult))
                link(dve.tensor_tensor(last, last, t2, ALU.max))
                link(dve.tensor_tensor(prev, prev, t2, ALU.max))
                for k in range(2):
                    dve.tensor_copy(K.at[k][:, 0, :], last[:, k, :])
                    dve.tensor_copy(K.at[k][:, 1, :], prev[:, k, :])
                    dve.wait_ge(row_ready, k + 1)
                    link(dve.tensor_copy(lastkey[:, k, :], row[k][:, 0:ET]))
                    dve.memset(K.runs_on[k][:, 0:1], 0.0)
                    link(dve.tensor_tensor(K.runs_on[k][:, 1:ET], lastkey[:, k, 1:ET], lastkey[:, k, 0:ET - 1], ALU.is_equal))


def normalise(K, name, src, dst, gamma=None, beta=None):
    nc = K.nc
    S = Stage(K, name)
    with S.ctx:
        sq = S.sb("sq", [P, NT, D])
        st = S.sb("st", [P, 5, NT])
        gb = S.sb("gb", [P, 2, D])
        centred, squared, var_ready, root, loaded = S.sem("c"), S.sem("s"), S.sem("v"), S.sem("r"), S.sem("ld")
        with nc.Block() as block:

            @block.sync
            def _(sp):
                if gamma is not None:
                    sp.dma_start(gb[:, 0, :], gamma.partition_broadcast(P)).then_inc(loaded, 16)
                    sp.dma_start(gb[:, 1, :], beta.partition_broadcast(P)).then_inc(loaded, 16)

            @block.vector
            def _(dve):
                link = S.link(dve, "l")
                wide = [P, NT, D]
                link(dve.reduce_sum(st[:, 0, :], src[:, :, :], AX.X))
                link(dve.tensor_scalar(st[:, 1, :], st[:, 0, :], 1.0 / D, None, ALU.mult))
                dve.tensor_tensor(dst[:, :, :], src[:, :, :], over(st[:, 1, :].unsqueeze(2), wide), ALU.subtract).then_inc(centred, 1)
                dve.wait_ge(squared, 1)
                link(dve.reduce_sum(st[:, 2, :], sq[:, :, :], AX.X))
                dve.tensor_scalar(st[:, 3, :], st[:, 2, :], 1.0 / D, EPS, ALU.mult, ALU.add).then_inc(var_ready, 1)
                dve.wait_ge(root, 1)
                link(dve.reciprocal(st[:, 4, :], st[:, 3, :]))
                link(dve.tensor_tensor(dst[:, :, :], dst[:, :, :], over(st[:, 4, :].unsqueeze(2), wide), ALU.mult))
                if gamma is not None:
                    dve.wait_ge(loaded, 32)
                    link(dve.tensor_tensor(dst[:, :, :], dst[:, :, :], over(gb[:, 0, :].unsqueeze(1), wide), ALU.mult))
                    link(dve.tensor_tensor(dst[:, :, :], dst[:, :, :], over(gb[:, 1, :].unsqueeze(1), wide), ALU.add))

            @block.scalar
            def _(act):
                act.wait_ge(centred, 1)
                act.activation(sq[:, :, :], dst[:, :, :], ACT.Square).then_inc(squared, 1)
                act.wait_ge(var_ready, 1)
                act.activation(st[:, 3, :], st[:, 3, :], ACT.Sqrt).then_inc(root, 1)


def project(K, name, src, weights, biases, tables, score=None, into=None):
    nc = K.nc
    S = Stage(K, name)
    M = len(weights)
    wide = [D] if into is not None else [table.shape[1] for table in tables]
    with S.ctx:
        W = S.sb("W", [128, M, 2, D])
        bias = S.sb("bias", [P, M, D])
        vec = S.sb("vec", [P, 2 * D])
        rows = [S.sb(f"rows{i}", [P, D]) for i in range(2)]
        rowsT = [S.sb(f"rowsT{i}", [128, 2, P]) for i in range(2)]
        res = [[S.sb(f"res{i}{m}", [P, wide[m]]) for m in range(M)] for i in range(2)]
        ss = [S.sb(f"ss{i}", [P, 4]) for i in range(2)]
        junk = [S.sb(f"junk{i}", [P, 2, D]) for i in range(2)]
        T = [S.ps(f"T{i}", [128, 2, 256]) for i in range(2)]
        Y = [[S.ps(f"Y{i}{m}", [P, 512]) for m in range(M)] for i in range(2)]
        loaded, staged, turned, copied, done, ready = (S.sem(x) for x in ("ld", "stg", "trn", "cpy", "done", "rdy"))
        stored = [S.sem(f"st{i}") for i in range(2)]
        ones_set = S.sem("ones")
        per_tile = 16 * (M + (score is not None))
        loads = 16 * (M + sum(b is not None for b in biases) + (score is not None))
        with nc.Block() as block:

            @block.sync
            def _(sp):
                for m in range(M):
                    sp.dma_start(W[:, m, :, :], weights[m].rearrange("(k p) n -> p k n", p=128)).then_inc(loaded, 16)
                    if biases[m] is not None:
                        sp.dma_start(bias[:, m, :], biases[m].partition_broadcast(P)).then_inc(loaded, 16)
                if score is not None:
                    sp.dma_start(vec[:, :], score.partition_broadcast(P)).then_inc(loaded, 16)

                def store(t, slot, turn):
                    await_(sp, ready, t + 1)
                    for m in range(M):
                        sp.dma_start(nodes(tables[m])[:, bass.ds(t, 1), :].rearrange("p o w -> p (o w)"), res[slot][m][:, :]).then_inc(stored[slot], 16)
                    if score is not None:
                        sp.dma_start(nodes(K.ss)[:, bass.ds(t, 1), :].rearrange("p o w -> p (o w)"), ss[slot][:, :]).then_inc(stored[slot], 16)

                if into is None:
                    skewed(sp, NT, [(0, store)])
                    sp.wait_ge(stored[0], per_tile * (NT - NT // 2))
                    sp.wait_ge(stored[1], per_tile * (NT // 2))

            @block.gpsimd
            def _(pool):
                for i in range(2):
                    pool.memset(ss[i][:, :], 0.0)
                    for m in range(M):
                        if wide[m] > D:
                            pool.memset(res[i][m][:, D:wide[m]], 1.0)
                pool.memset(junk[0][:, 0, 0:1], 0.0).then_inc(ones_set, 1)

                def stage(t, slot, turn):
                    hold(K, pool, turned, t - 1)
                    pool.tensor_copy(rows[slot][:, :], src[:, bass.ds(t, 1), 0:D].rearrange("p o w -> p (o w)")).then_inc(staged, 1)

                skewed(pool, NT, [(0, stage)])

            @block.tensor
            def _(pe):
                pe.wait_ge(loaded, loads)

                def turn_(t, slot, turn):
                    hold(K, pe, staged, t + 1)
                    hold(K, pe, copied, t - 1)
                    for k in range(2):
                        ins = pe.transpose(T[slot][:, k, 0:P], rows[slot][:, k * 128:(k + 1) * 128], K.ident[0:P, 0:P])
                    ins.then_inc(turned, 1)

                def multiply(t, slot, turn):
                    hold(K, pe, copied, t + 1)
                    hold(K, pe, ready, t - 1)
                    for m in range(M):
                        for k in range(2):
                            ins = pe.matmul(Y[slot][m][:, 0:D], rowsT[slot][:, k, :], W[:, m, k, :], start=(k == 0), stop=(k == 1))
                    ins.then_inc(done, 1)

                skewed(pe, NT, [(0, turn_), (1, multiply)])

            @block.scalar
            def _(act):
                def copy(t, slot, turn):
                    hold(K, act, done, t - 1)
                    await_(act, turned, t + 1)
                    act.activation(rowsT[slot][:, :, :], T[slot][:, :, 0:P], ACT.Copy).then_inc(copied, 1)

                skewed(act, NT, [(0, copy)])

            @block.vector
            def _(dve):
                dve.wait_ge(loaded, loads)
                dve.wait_ge(ones_set, 1)

                def finish(t, slot, turn):
                    hold(K, dve, done, t + 1)
                    if into is not None:
                        dve.tensor_tensor(into[:, bass.ds(t, 1), :].rearrange("p o w -> p (o w)"), Y[slot][0][:, 0:D],
                                          bias[:, 0, :], ALU.add).then_inc(ready, 1)
                        return
                    hold(K, dve, stored[slot], per_tile * turn)
                    for m in range(M):
                        y = Y[slot][m][:, 0:D]
                        if biases[m] is None:
                            ins = dve.tensor_copy(res[slot][m][:, 0:D], y)
                        else:
                            ins = dve.tensor_tensor(res[slot][m][:, 0:D], y, bias[:, m, :], ALU.add)
                    if score is not None:
                        dve.scalar_tensor_tensor(junk[slot][:, 0, :], y, 1.0, vec[:, D:2 * D], ALU.mult, ALU.mult,
                                                 accum_out=res[slot][0][:, D:D + 1])
                        ins = dve.scalar_tensor_tensor(junk[slot][:, 1, :], y, 1.0, vec[:, 0:D], ALU.mult, ALU.mult,
                                                       accum_out=ss[slot][:, 0:1])
                    ins.then_inc(ready, 1)

                skewed(dve, NT, [(0, finish)])


def kernel(**inputs):
    raise NotImplementedError

MESSAGE, ATTEND, GAT, COPY = range(4)
LAGS = {MESSAGE: (1, 2, 3, 4, 3, 5), ATTEND: (1, 0, 0, 0, 2, 3), GAT: (1, 2, 0, 0, 2, 3), COPY: (1, 0, 0, 0, 2, 3)}


def edge_sums(K, name, kind, side, tables, columns, width, a=None):
    nc = K.nc
    S = Stage(K, name)
    take_lag, stats_lag, norm_lag, mul_lag, mask_lag, sum_lag = LAGS[kind]
    last = sum_lag
    T = len(tables)
    tw = [t.shape[1] for t in tables]
    with S.ctx:
        at = [S.sb(f"at{i}", [P, GT, 2], i32) for i in range(2)]
        key = [S.sb(f"key{i}", [P, GT, 2]) for i in range(2)]
        got = [[S.sb(f"got{i}{m}", [P, GT, tw[m]]) for m in range(T)] for i in range(2)]
        V = [S.sb(f"V{i}", [P, GT, width]) for i in range(2)]
        same = [S.sb(f"same{i}", [P, GT, P]) for i in range(2)]
        out = [S.sb(f"out{i}", [P, GT, width]) for i in range(2)]
        keys_row = S.ps("keys", [P, GT, 128])
        bank = 512 if width > D else D
        total = S.ps("total", [P, GT, bank])
        at_ready, key_ready, row_ready, mask_ready = S.sem("at"), S.sem("key"), S.sem("row"), S.sem("mask")
        taken, v_ready, summed, out_ready = S.sem("taken"), S.sem("v"), S.sem("sum"), S.sem("out")
        gathered = [S.indirect(f"gat{i}") for i in range(2)]
        stored = [S.sem(f"st{i}") for i in range(2)]
        per_group = 16 * GT * T
        phases = {e: [] for e in ("pool", "dve", "act", "pe", "sp")}
        loads = 0
        if kind == MESSAGE:
            pre = [S.sb(f"pre{i}", [P, GT, D]) for i in range(2)]
            act1 = [S.sb(f"act{i}", [P, GT, D]) for i in range(2)]
            xn = [S.sb(f"xn{i}", [P, GT, D]) for i in range(2)]
            bn = [S.sb(f"bn{i}", [P, GT, 6]) for i in range(2)]
            mv = [S.sb(f"mv{i}", [P, GT, 2]) for i in range(2)]
            var = [S.sb(f"var{i}", [P, GT]) for i in range(2)]
            rstd = [S.sb(f"rstd{i}", [P, GT]) for i in range(2)]
            minus_half = S.sb("mh", [P, GT])
            wrow = S.sb("wrow", [P, D])
            W2 = S.sb("W2", [128, 2, D])
            gcol = S.sb("gcol", [128, 2, 2])
            b2 = S.sb("b2", [1, 2 * D])
            xT = S.sb("xT", [128, 2, GT, P])
            turnedp = S.ps("tp", [128, 2, GT, 128])
            prod = S.ps("prod", [P, GT, D])
            loaded, weights_ready, pre_ready, silu_ready = S.sem("ld"), S.sem("w"), S.sem("pre"), S.sem("silu")
            stats_ready, rstd_ready, norm_ready = S.sem("stats"), S.sem("rstd"), S.sem("norm")
            turned, copied, multiplied, half_set, bias_ready = S.sem("trn"), S.sem("cpy"), S.sem("mul"), S.sem("mh"), S.sem("bias")
        if kind == GAT:
            score = [S.sb(f"score{i}", [P, GT, 2]) for i in range(2)]
            e = [S.sb(f"e{i}", [P, GT]) for i in range(2)]
            score_ready, e_ready = S.sem("score"), S.sem("e")
        with nc.Block() as block:

            @block.gpsimd
            def _(pool):
                if kind == MESSAGE:
                    pool.memset(minus_half[:, :], -0.5).then_inc(half_set, 1)
                    pool.wait_ge(half_set, 1)

                def gather(g, slot, turn):
                    hold(K, pool, at_ready, g + 1)
                    hold(K, pool, taken if kind == MESSAGE else v_ready, g - 1)
                    for j in range(GT):
                        for m in range(T):
                            c = columns[m]
                            pool.indirect_dma_start(
                                got[slot][m][:, j, :], None, tables[m],
                                bass.IndirectOffsetOnAxis(ap=at[slot][:, j, c:c + 1], axis=0)).then_inc(gathered[slot], 16)

                def power(g, slot, turn):
                    hold(K, pool, stats_ready, g + 1)
                    hold(K, pool, norm_ready, g - 1)
                    pool.tensor_tensor(rstd[slot][:, :], var[slot][:, :], minus_half[:, :], ALU.pow).then_inc(rstd_ready, 1)

                skewed(pool, G, [(0, gather)] + [(stats_lag, power)] * (kind == MESSAGE))

            @block.sync
            def _(sp):
                if kind == MESSAGE:
                    sp.dma_start(wrow[:, :], a["L0_gnn_mW1"][2 * D:2 * D + 1, :].rearrange("o n -> (o n)").partition_broadcast(P)).then_inc(loaded, 16)
                    sp.dma_start(W2[:, :, :], a["L0_gnn_mW2"].rearrange("(k p) n -> p k n", p=128)).then_inc(loaded, 16)
                    sp.dma_start(gcol[:, 0, :], a["L0_gnn_ln_g"].rearrange("(k p) -> p k", p=128), allow_slow_non_contiguous=True).then_inc(loaded, 16)
                    sp.dma_start(gcol[:, 1, :], a["L0_gnn_ln_b"].rearrange("(k p) -> p k", p=128), allow_slow_non_contiguous=True).then_inc(loaded, 16)
                    for h in range(2):
                        sp.dma_start(b2[:, h * D:(h + 1) * D], a["L0_gnn_mb2"].rearrange("(o n) -> o n", o=1)).then_inc(loaded, 16)

                def store(g, slot, turn):
                    sp.wait_ge(out_ready, g + 1)
                    sp.dma_start(K.sums[width].rearrange("(t p) w -> p t w", p=P)[:, bass.ds(g * GT, GT), :], out[slot][:, :, :]).then_inc(stored[slot], 16)

                skewed(sp, G, [(last, store)])
                for u in range(2):
                    sp.wait_ge(stored[u], 16 * (G // 2))

            @block.vector
            def _(dve):
                link = S.link(dve, "l")
                if kind == MESSAGE:
                    dve.wait_ge(loaded, 96)
                    dve.tensor_copy(xT[:, :, 0, 0:1], gcol[:, 1, :].unsqueeze(2)).then_inc(weights_ready, 1)
                    dve.wait_ge(bias_ready, 1)
                    for k in range(2):
                        dve.tensor_scalar(W2[:, k, :], W2[:, k, :], gcol[:, 0, k:k + 1], None, ALU.mult)
                    for h in range(2):
                        ins = dve.tensor_tensor(b2[:, h * D:(h + 1) * D], b2[:, h * D:(h + 1) * D], prod[0:1, 0, :], ALU.add)
                    ins.then_inc(weights_ready, 1)

                def indices_(g, slot, turn):
                    hold(K, dve, gathered[slot], per_group * turn)
                    dve.tensor_copy(at[slot][:, :, :], K.idx[side][:, bass.ds(g * GT, GT), :]).then_inc(at_ready, 1)

                def take(g, slot, turn):
                    hold(K, dve, mask_ready, g - 1)
                    dve.tensor_copy(key[slot][:, :, :], K.fk[side][:, bass.ds(g * GT, GT), :]).then_inc(key_ready, 1)
                    dve.wait_ge(gathered[slot], per_group * (turn + 1))
                    x = got[slot][0]
                    if kind == MESSAGE:
                        dve.wait_ge(key_ready, g + 1)
                        await_(dve, silu_ready, g - 1)
                        dve.tensor_tensor(pre[slot][:, :, :], x[:, :, :], got[slot][1][:, :, :], ALU.add).then_inc(taken, 1)
                        dve.wait_ge(taken, g + 1)
                        for j in range(GT):
                            ins = dve.scalar_tensor_tensor(pre[slot][:, j, :], wrow[:, :], key[slot][:, j, 1:2],
                                                           pre[slot][:, j, :], ALU.mult, ALU.add)
                        ins.then_inc(pre_ready, 1)
                    if kind == ATTEND:
                        await_(dve, summed, g - 1)
                        for j in range(GT):
                            w = K.scores[:, bass.ds(g * GT + j, 1), :].rearrange("p o h -> p (o h)")
                            dve.tensor_tensor(V[slot][:, j, 0:D].rearrange("p (h d) -> p h d", d=DH),
                                              x[:, j, :].rearrange("p (h d) -> p h d", d=DH),
                                              over(w.unsqueeze(2), [P, HEADS, DH]), ALU.mult)
                        dve.tensor_copy(V[slot][:, :, D:D + HEADS], K.scores[:, bass.ds(g * GT, GT), :]).then_inc(v_ready, 1)
                    if kind == GAT:
                        hold(K, dve, e_ready, g - 1)
                        link.restart()
                        link(dve.tensor_tensor(score[slot][:, :, 0], x[:, :, D], got[slot][1][:, :, 0], ALU.add))
                        dve.scalar_tensor_tensor(score[slot][:, :, 1], score[slot][:, :, 0], 0.2, score[slot][:, :, 0],
                                                 ALU.mult, ALU.max).then_inc(score_ready, 1)
                    if kind == COPY:
                        await_(dve, summed, g - 1)
                        dve.tensor_copy(V[slot][:, :, :], x[:, :, :]).then_inc(v_ready, 1)

                def weigh(g, slot, turn):
                    await_(dve, e_ready, g + 1)
                    hold(K, dve, summed, g - 1)
                    for j in range(GT):
                        dve.tensor_scalar(V[slot][:, j, 0:D], got[slot][0][:, j, 0:D], e[slot][:, j:j + 1], None, ALU.mult)
                    dve.tensor_copy(V[slot][:, :, D], e[slot][:, :]).then_inc(v_ready, 1)

                def stats(g, slot, turn):
                    hold(K, dve, silu_ready, g + 1)
                    hold(K, dve, rstd_ready, g - 1)
                    hold(K, dve, norm_ready, g - 1)
                    link.restart()
                    for j in range(GT):
                        ins = dve.bn_stats(bn[slot][:, j, :], act1[slot][:, j, :])
                    link(ins)
                    for j in range(GT):
                        ins = dve.bn_aggr(mv[slot][:, j, :], bn[slot][:, j, :])
                    link(ins)
                    dve.tensor_scalar(var[slot][:, :], mv[slot][:, :, 1], EPS, None, ALU.add).then_inc(stats_ready, 1)

                def norm(g, slot, turn):
                    hold(K, dve, rstd_ready, g + 1)
                    hold(K, dve, turned, g - 1)
                    for j in range(GT):
                        ins = dve.tensor_scalar(xn[slot][:, j, :], act1[slot][:, j, :], mv[slot][:, j, 0:1],
                                                rstd[slot][:, j:j + 1], ALU.subtract, ALU.mult)
                    ins.then_inc(norm_ready, 1)

                def mask(g, slot, turn):
                    hold(K, dve, row_ready, g + 1)
                    hold(K, dve, summed, g - 1)
                    dve.tensor_tensor(same[slot][:, :, :], keys_row[:, :, 0:P], over(key[slot][:, :, 0:1], [P, GT, P]),
                                      ALU.is_equal).then_inc(mask_ready, 1)

                ph = [(0, indices_)]
                if kind == MESSAGE:
                    ph += [(norm_lag, norm), (mask_lag, mask), (stats_lag, stats)]
                elif kind == GAT:
                    ph += [(stats_lag, weigh), (mask_lag, mask)]
                else:
                    ph += [(mask_lag, mask)]
                skewed(dve, G, ph + [(take_lag, take)])

            @block.scalar
            def _(act):
                def silu(g, slot, turn):
                    hold(K, act, norm_ready, g - 1)
                    act.wait_ge(pre_ready, g + 1)
                    act.activation(act1[slot][:, :, :], pre[slot][:, :, :], ACT.Silu).then_inc(silu_ready, 1)

                def copy(g, slot, turn):
                    hold(K, act, multiplied, g)
                    act.wait_ge(turned, g + 1)
                    act.activation(xT[:, :, :, :], turnedp[:, :, :, 0:P], ACT.Copy).then_inc(copied, 1)

                def message(g, slot, turn):
                    hold(K, act, summed, g - 1)
                    act.wait_ge(multiplied, g + 1)
                    act.activation(V[slot][:, :, :], prod[:, :, :], ACT.Silu).then_inc(v_ready, 1)

                def exp(g, slot, turn):
                    hold(K, act, v_ready, g - 1)
                    act.wait_ge(score_ready, g + 1)
                    act.activation(e[slot][:, :], score[slot][:, :, 1], ACT.Exp, scale=-1.0).then_inc(e_ready, 1)

                def evacuate(g, slot, turn):
                    hold(K, act, stored[slot], 16 * turn)
                    act.wait_ge(summed, g + 1)
                    act.activation(out[slot][:, :, :], total[:, :, 0:width], ACT.Copy).then_inc(out_ready, 1)

                ph = [(sum_lag, evacuate)]
                if kind == MESSAGE:
                    ph += [(mul_lag, message), (norm_lag, copy), (take_lag, silu)]
                if kind == GAT:
                    ph += [(take_lag, exp)]
                skewed(act, G, ph)

            @block.tensor
            def _(pe):
                if kind == MESSAGE:
                    pe.wait_ge(weights_ready, 1)
                    for k in range(2):
                        ins = pe.matmul(prod[0:1, 0, :], xT[:, k, 0, 0:1], W2[:, k, :], start=(k == 0), stop=(k == 1))
                    ins.then_inc(bias_ready, 1)
                    pe.wait_ge(weights_ready, 2)

                def turn_(g, slot, turn):
                    hold(K, pe, norm_ready, g + 1)
                    hold(K, pe, copied, g)
                    for j in range(GT):
                        for k in range(2):
                            ins = pe.transpose(turnedp[:, k, j, 0:P], xn[slot][:, j, k * 128:(k + 1) * 128], K.ident[0:P, 0:P])
                    ins.then_inc(turned, 1)

                def multiply(g, slot, turn):
                    hold(K, pe, copied, g + 1)
                    hold(K, pe, v_ready, g)
                    for j in range(GT):
                        if j % 2 == 0:
                            pe.matmul(prod[:, j:j + 2, :].rearrange("p j n -> p (j n)"), K.ones[0:1, 0:P], b2[0:1, :], start=True, stop=True)
                        for k in range(2):
                            ins = pe.matmul(prod[:, j, :], xT[:, k, j, :], W2[:, k, :], start=False, stop=True, skip_group_check=True)
                    ins.then_inc(multiplied, 1)

                def row(g, slot, turn):
                    hold(K, pe, key_ready, g + 1)
                    hold(K, pe, mask_ready, g)
                    for j in range(GT):
                        ins = pe.matmul(keys_row[:, j, 0:P], over(key[slot][:, j, 0:1], [P, P]), K.ident[0:P, 0:P], start=True, stop=True)
                    ins.then_inc(row_ready, 1)

                def add_up(g, slot, turn):
                    hold(K, pe, v_ready, g + 1)
                    hold(K, pe, mask_ready, g + 1)
                    hold(K, pe, out_ready, g)
                    for j in range(GT):
                        ins = pe.matmul(total[:, j, 0:width], same[slot][:, j, :], V[slot][:, j, :], start=True, stop=True)
                    ins.then_inc(summed, 1)

                ph = [(sum_lag, add_up)]
                if kind == MESSAGE:
                    ph += [(mul_lag, multiply), (norm_lag, turn_)]
                skewed(pe, G, ph + [(mask_lag - 1, row)])


def collect(K, name, side, width, dst):
    nc = K.nc
    S = Stage(K, name)
    parts = [(c, min(128, width - c)) for c in range(0, width, 128)]
    R, Q = 100, ET // 100
    with S.ctx:
        carry = S.sb("carry", [P, NT, width])
        ends = S.sb("ends", [R, Q, width])
        endsT = S.sb("endsT", [128, len(parts), ET])
        runs = S.sb("runs", [128, len(parts), ET])
        back = S.sb("back", [R, Q, width])
        T = S.ps("T", [128, len(parts), 512])
        B = S.ps("B", [R, Q, 512])
        loaded, zeroed, turned, copied, scanned = (S.sem(x) for x in ("ld", "z", "t", "c", "s"))
        returned, back_ready, stored, done = (S.sem(x) for x in ("r", "b", "st", "d"))
        gathered = S.indirect("g")
        with nc.Block() as block:

            @block.sync
            def _(sp):
                rows = K.sums[width].rearrange("(t p) w -> p t w", p=P)[P - 1, :, :]
                sp.dma_start(ends[:, :, :], rows.rearrange("(q r) w -> r q w", r=R)).then_inc(loaded, 16)
                sp.wait_ge(back_ready, 1)
                sp.dma_start(K.running[width].rearrange("(q r) w -> r q w", r=R), back[:, :, :]).then_inc(stored, 16)
                sp.wait_ge(stored, 16)

            @block.gpsimd
            def _(pool):
                pool.memset(dst[:, :, 0:width], 0.0).then_inc(zeroed, 1)
                pool.memset(carry[:, :, :], 0.0).then_inc(zeroed, 1)
                pool.wait_ge(zeroed, 2)
                for table, i, to in ((K.sums[width], 0, dst), (K.running[width], 1, carry)):
                    if i == 1:
                        pool.wait_ge(stored, 16)
                    for t in range(NT):
                        pool.indirect_dma_start(to[:, t, 0:width], None, table,
                                                bass.IndirectOffsetOnAxis(ap=K.at[side][:, i, t:t + 1], axis=0),
                                                bounds_check=(E - 1, ET - 1)[i], oob_is_err=False).then_inc(gathered, 16)

            @block.tensor
            def _(pe):
                pe.wait_ge(loaded, 16)
                for i, (c, n) in enumerate(parts):
                    for q in range(Q):
                        ins = pe.transpose(T[0:n, i, q * R:(q + 1) * R], ends[:, q, c:c + n], K.ident[0:R, 0:R])
                ins.then_inc(turned, 1)
                pe.wait_ge(scanned, 1)
                for i, (c, n) in enumerate(parts):
                    for q in range(Q):
                        ins = pe.transpose(B[:, q, c:c + n], runs[0:n, i, q * R:(q + 1) * R], K.ident[0:n, 0:n])
                ins.then_inc(returned, 1)

            @block.scalar
            def _(act):
                act.wait_ge(turned, 1)
                for i, (c, n) in enumerate(parts):
                    ins = act.activation(endsT[0:n, i, :], T[0:n, i, 0:ET], ACT.Copy)
                ins.then_inc(copied, 1)
                act.wait_ge(returned, 1)
                act.activation(back[:, :, :], B[:, :, 0:width], ACT.Copy).then_inc(back_ready, 1)

            @block.vector
            def _(dve):
                dve.wait_ge(copied, 1)
                for i, (c, n) in enumerate(parts):
                    ins = dve.tensor_tensor_scan(runs[0:n, i, :], K.runs_on[side][0:n, :], endsT[0:n, i, :], 0.0, ALU.mult, ALU.add)
                ins.then_inc(scanned, 1)
                dve.wait_ge(gathered, 32 * NT)
                dve.tensor_tensor(dst[:, :, 0:width], dst[:, :, 0:width], carry[:, :, :], ALU.add).then_inc(done, 1)
                dve.wait_ge(done, 1)



def turn(K, name, src, T, gate=None):
    nc = K.nc
    S = Stage(K, name)
    W_, b_, n, gout = gate if gate is not None else (None, None, 1, None)
    with S.ctx:
        W = S.sb("W", [128, 2, n])
        bias = S.sb("bias", [P, n])
        rows = [S.sb(f"rows{i}", [P, D]) for i in range(2)]
        rowsT = [S.sb(f"rowsT{i}", [128, 2, P]) for i in range(2)]
        ps = [S.ps(f"ps{i}", [128, 2, 256]) for i in range(2)]
        Y = [S.ps(f"Y{i}", [P, 512]) for i in range(2)]
        loaded, staged, turned, copied, kept, done, ready, padded = (S.sem(x) for x in ("ld", "stg", "trn", "cpy", "kept", "done", "rdy", "pad"))
        with nc.Block() as block:

            @block.sync
            def _(sp):
                if gate is not None:
                    sp.dma_start(W[:, :, :], W_.rearrange("(k p) n -> p k n", p=128), allow_slow_non_contiguous=True).then_inc(loaded, 16)
                    sp.dma_start(bias[:, :], b_.partition_broadcast(P)).then_inc(loaded, 16)

            @block.gpsimd
            def _(pool):
                for k in range(2):
                    ins = pool.memset(T[:, k, :].rearrange("q (t p) -> q t p", p=128)[:, :, P:128], 0.0)
                ins.then_inc(padded, 1)

                def stage(t, slot, turn):
                    hold(K, pool, turned, t - 1)
                    pool.tensor_copy(rows[slot][:, :], src[:, bass.ds(t, 1), 0:D].rearrange("p o w -> p (o w)")).then_inc(staged, 1)

                skewed(pool, NT, [(0, stage)])

            @block.tensor
            def _(pe):
                def turn_(t, slot, turn):
                    hold(K, pe, staged, t + 1)
                    hold(K, pe, copied, t - 1)
                    for k in range(2):
                        ins = pe.transpose(ps[slot][:, k, 0:P], rows[slot][:, k * 128:(k + 1) * 128], K.ident[0:P, 0:P])
                    ins.then_inc(turned, 1)

                def multiply(t, slot, turn):
                    hold(K, pe, copied, t + 1)
                    hold(K, pe, ready, t - 1)
                    for k in range(2):
                        ins = pe.matmul(Y[slot][:, 0:n], rowsT[slot][:, k, :], W[:, k, :], start=(k == 0), stop=(k == 1))
                    ins.then_inc(done, 1)

                if gate is not None:
                    pe.wait_ge(loaded, 32)
                skewed(pe, NT, [(0, turn_)] + [(1, multiply)] * (gate is not None))

            @block.scalar
            def _(act):
                def copy(t, slot, turn):
                    hold(K, act, kept, t - 1)
                    if gate is not None:
                        hold(K, act, done, t - 1)
                    await_(act, turned, t + 1)
                    act.activation(rowsT[slot][:, :, :], ps[slot][:, :, 0:P], ACT.Copy).then_inc(copied, 1)

                skewed(act, NT, [(0, copy)])

            @block.vector
            def _(dve):
                def keep(t, slot, turn):
                    hold(K, dve, copied, t + 1)
                    dve.tensor_copy(T[:, :, bass.ds(t * 128, P)], rowsT[slot][:, :, :]).then_inc(kept, 1)

                def finish(t, slot, turn):
                    hold(K, dve, done, t + 1)
                    dve.tensor_tensor(gout[:, bass.ds(t, 1), :].rearrange("p o w -> p (o w)"), Y[slot][:, 0:n], bias[:, :], ALU.add).then_inc(ready, 1)

                if gate is not None:
                    dve.wait_ge(loaded, 32)
                skewed(dve, NT, [(0, keep)] + [(1, finish)] * (gate is not None))


def feed_forward(K, name, ins, F, W1, b1, W2, b2, func, dst, experts=1, by_tile=None, factor=None,
                 chosen=None):
    nc = K.nc
    S = Stage(K, name)
    KC = 2 * len(ins)
    ES = 2 if experts > 1 else 1
    H = F * 128
    CH = NT // CHUNK
    with S.ctx:
        w1 = [S.sb(f"w1{i}", [128, KC, H]) for i in range(ES)]
        c1 = [S.sb(f"c1{i}", [128, F]) for i in range(ES)]
        w2 = [S.sb(f"w2{i}", [128, F, D]) for i in range(ES)]
        c2 = [S.sb(f"c2{i}", [1, 2 * D]) for i in range(ES)]
        hid = [S.sb(f"hid{i}", [128, CW]) for i in range(2)]
        wt = [S.sb(f"wt{i}", [P, CHUNK]) for i in range(2)]
        hp = [S.ps(f"hp{i}", [128, 2, 512]) for i in range(2)]
        y = S.ps("y", [P, 6, D])
        loaded = [S.sem(f"ld{i}") for i in range(ES)]
        h_done, h_used, y_done, added, w_ready = (S.sem(x) for x in ("hd", "hu", "yd", "add", "wt"))

        def units(eng, body):
            if experts == 1:
                with eng.Fori(0, CH) as c:
                    body(0, 0, 0, c, c)
            else:
                with eng.Fori(0, experts // 2) as e2:
                    for u in range(2):
                        with eng.Fori(0, CH) as c:
                            body(2 * e2 + u, u, e2, c, (2 * e2 + u) * CH + c)

        def pick(ap, e):
            return ap if experts == 1 and chosen is None else ap[bass.ds(e, 1)].rearrange("o a b -> (o a) b") if len(ap.shape) == 3 else ap[bass.ds(e, 1), :].rearrange("o b -> (o b)")

        with nc.Block() as block:

            @block.sync
            def _(sp):
                def load(e, slot):
                    sp.dma_start(w1[slot][:, :, :], pick(W1, e).rearrange("(k p) f -> p k f", p=128)).then_inc(loaded[slot], 16)
                    sp.dma_start(c1[slot][:, :], pick(b1, e).rearrange("(f p) -> p f", p=128), allow_slow_non_contiguous=True).then_inc(loaded[slot], 16)
                    sp.dma_start(w2[slot][:, :, :], pick(W2, e).rearrange("(f p) n -> p f n", p=128)).then_inc(loaded[slot], 16)
                    for h in range(2):
                        sp.dma_start(c2[slot][:, h * D:(h + 1) * D], pick(b2, e).rearrange("(o n) -> o n", o=1)).then_inc(loaded[slot], 16)

                if chosen is not None:
                    load(sp.value_load(chosen, min_val=0, max_val=7), 0)
                elif experts == 1:
                    load(0, 0)
                else:
                    load(0, 0)
                    load(1, 1)
                    with sp.Fori(1, experts // 2) as e2:
                        for u in range(2):
                            sp.wait_ge(y_done, (2 * e2 + (u - 1)) * (CH * F) + 2)
                            load(2 * e2 + u, u)

            @block.tensor
            def _(pe):
                pe.sem_inc(y_done, 2)

                def body(e, slot, turn, c, n):
                    hold(K, pe, loaded[slot], 80 * (turn + 1))
                    cols = c * CW

                    def hidden(f):
                        hold(K, pe, h_used, n * F + (f + 1))
                        for half in range(2):
                            for k in range(KC):
                                ins_ = pe.matmul(hp[f % 2][:, half, 0:HW], w1[slot][:, k, f * 128:(f + 1) * 128],
                                                 ins[k // 2][:, k % 2, bass.ds(cols + half * HW, HW)],
                                                 start=(k == 0), stop=(k == KC - 1))
                        ins_.then_inc(h_done, 1)

                    def outward(f):
                        pe.wait_ge(h_used, n * F + (f + 3))
                        if f == 0:
                            hold(K, pe, added, n + 1)
                            for b in range(3):
                                w = min(2, CHUNK - 2 * b)
                                pe.matmul(y[:, 2 * b:2 * b + w, :].rearrange("p j n -> p (j n)"), K.ones[0:1, 0:P],
                                          c2[slot][0:1, 0:w * D], start=True, stop=True)
                        for t in range(CHUNK):
                            ins_ = pe.matmul(y[:, t, :], hid[f % 2][:, t * 128:t * 128 + P], w2[slot][:, f, :],
                                             start=False, stop=True, skip_group_check=True)
                        ins_.then_inc(y_done, 1)

                    hidden(0)
                    for f in range(1, F):
                        hidden(f)
                        outward(f - 1)
                    outward(F - 1)

                units(pe, body)

            @block.scalar
            def _(act):
                act.sem_inc(h_used, 2)

                def body(e, slot, turn, c, n):
                    hold(K, act, loaded[slot], 80 * (turn + 1))
                    for f in range(F):
                        hold(K, act, y_done, n * F + (f + 1))
                        act.wait_ge(h_done, n * F + (f + 1))
                        act.activation(hid[f % 2][:, :].rearrange("p (h w) -> p h w", h=2), hp[f % 2][:, :, 0:HW], func,
                                       bias=c1[slot][:, f:f + 1]).then_inc(h_used, 1)

                units(act, body)

            @block.vector
            def _(dve):
                dve.sem_inc(added, 1)
                link = S.link(dve, "l")

                def body(e, slot, turn, c, n):
                    link.restart()
                    hold(K, dve, added, n + 1)
                    if by_tile is not None:
                        link(dve.tensor_copy(wt[0][:, :], by_tile[:, bass.ds(c * CHUNK, CHUNK), bass.ds(e, 1)].rearrange("p t o -> p (t o)")))
                    hold(K, dve, y_done, (n + 1) * F + 2)
                    for t in range(CHUNK):
                        to = dst[:, bass.ds(c * CHUNK + t, 1), :].rearrange("p o w -> p (o w)")
                        if by_tile is None and factor is None:
                            ins_ = dve.tensor_tensor(to, y[:, t, :], to, ALU.add)
                        else:
                            w = factor[:, 0:1] if factor is not None else wt[0][:, t:t + 1]
                            ins_ = dve.scalar_tensor_tensor(to, y[:, t, :], w, to, ALU.mult, ALU.add)
                    ins_.then_inc(added, 1)

                units(dve, body)


def add_into(K, name, dst, src):
    S = Stage(K, name)
    with S.ctx:
        done = S.sem("done")
        with K.nc.Block() as block:

            @block.vector
            def _(dve):
                dve.tensor_tensor(dst[:, :, :], dst[:, :, :], src[:, :, 0:D], ALU.add).then_inc(done, 1)
                dve.wait_ge(done, 1)


def message_layer(K, a):
    nc = K.nc
    A, B = K.dram("mA", (N, D)), K.dram("mB", (N, D))
    normalise(K, "m0_", K.X, K.H)
    W = a["L0_gnn_mW1"]
    project(K, "m1_", K.H, [W[0:D, :], W[D:2 * D, :]], [None, a["L0_gnn_mb1"]], [A, B])
    edge_sums(K, "m2_", MESSAGE, 0, [A, B], [0, 1], D, a)
    S = Stage(K, "m3_")
    with S.ctx:
        agg = S.sb("agg", [P, NT, D])
        T = [S.sb(f"T{i}", [128, 2, NT * 128]) for i in range(2)]
        collect(K, "m4_", 0, D, agg)
        turn(K, "m5_", K.H, T[0])
        turn(K, "m6_", agg, T[1])
        add_into(K, "m7_", K.X, K.H)
        feed_forward(K, "m8_", T, 2, a["L0_gnn_uW1"], a["L0_gnn_ub1"], a["L0_gnn_uW2"], a["L0_gnn_ub2"], ACT.Silu, K.X)


def top2_layer(K, a):
    nc = K.nc
    normalise(K, "t0_", K.X, K.H)
    normalise(K, "t1_", K.H, K.H, a["L0_ffn_gamma"], a["L0_ffn_beta"])
    S = Stage(K, "t_")
    with S.ctx:
        T = S.sb("T", [128, 2, NT * 128])
        logit = S.sb("logit", [P, NT, 8])
        top = S.sb("top", [P, NT, 8])
        which = S.sb("which", [P, NT, 8], u32)
        whichf = S.sb("whichf", [P, NT, 2])
        w = S.sb("w", [P, 4, NT])
        a2 = S.sb("a2", [P, NT, 8])
        wts = S.sb("wts", [P, NT, 8])
        turn(K, "t2_", K.H, T, gate=(a["L0_ffn_Wr"], a["L0_ffn_br"], 8, logit))
        diff, exped = S.sem("diff"), S.sem("exp")
        with nc.Block() as block:

            @block.vector
            def _(dve):
                link = S.link(dve, "l")
                for t in range(NT):
                    link.mark(dve.max(top[:, t, :], logit[:, t, :]))
                dve.wait_ge(link.sem, link.n)
                for t in range(NT):
                    ins = dve.max_index(which[:, t, :], top[:, t, :], logit[:, t, :])
                link(ins)
                link(dve.tensor_copy(whichf[:, :, :], which[:, :, 0:2]))
                dve.tensor_tensor(w[:, 0, :], top[:, :, 1], top[:, :, 0], ALU.subtract).then_inc(diff, 1)
                dve.wait_ge(exped, 1)
                link(dve.tensor_scalar(w[:, 2, :], w[:, 1, :], 1.0, None, ALU.add))
                link(dve.reciprocal(w[:, 2, :], w[:, 2, :]))
                link(dve.tensor_tensor(w[:, 3, :], w[:, 1, :], w[:, 2, :], ALU.mult))
                wide = [P, NT, 8]
                link(dve.tensor_tensor(wts[:, :, :], over(K.iota64[0:P, 0:8].unsqueeze(1), wide), over(whichf[:, :, 0:1], wide), ALU.is_equal))
                link(dve.tensor_tensor(wts[:, :, :], wts[:, :, :], over(w[:, 2, :].unsqueeze(2), wide), ALU.mult))
                link(dve.tensor_tensor(a2[:, :, :], over(K.iota64[0:P, 0:8].unsqueeze(1), wide), over(whichf[:, :, 1:2], wide), ALU.is_equal))
                link(dve.tensor_tensor(a2[:, :, :], a2[:, :, :], over(w[:, 3, :].unsqueeze(2), wide), ALU.mult))
                link(dve.tensor_tensor(wts[:, :, :], wts[:, :, :], a2[:, :, :], ALU.add))

            @block.scalar
            def _(act):
                act.wait_ge(diff, 1)
                act.activation(w[:, 1, :], w[:, 0, :], ACT.Exp).then_inc(exped, 1)

        feed_forward(K, "t3_", [T], 4, a["L0_ffn_W1"], a["L0_ffn_b1"], a["L0_ffn_W2"], a["L0_ffn_b2"], ACT.Gelu, K.X,
                     experts=8, by_tile=wts)


def edge_scores(K, name, a, q, k):
    nc = K.nc
    S = Stage(K, name)
    AW = REC_W[1] - 4
    with S.ctx:
        at = [S.sb(f"at{i}", [P, GT, 2], i32) for i in range(2)]
        got = [[S.sb(f"got{i}{m}", [P, GT, D]) for m in range(2)] for i in range(2)]
        attr = [S.sb(f"attr{i}", [P, GT, AW]) for i in range(2)]
        attrT = [S.sb(f"attrT{i}", [AW, GT, P]) for i in range(2)]
        keyed = [S.sb(f"keyed{i}", [P, GT, D]) for i in range(2)]
        prod = [S.sb(f"prod{i}", [P, GT, D]) for i in range(2)]
        dots = [S.sb(f"dots{i}", [P, GT, HEADS]) for i in range(2)]
        We = S.sb("We", [AW, DH])
        be = S.sb("be", [1, DH])
        T = S.ps("T", [AW, GT, 128])
        ep = [S.ps(f"ep{i}", [P, GT, 128]) for i in range(2)]
        at_ready, taken, turned, copied, ep_ready, scored, loaded = (S.sem(x) for x in ("at", "tk", "tr", "cp", "ep", "sc", "ld"))
        gathered = [S.indirect(f"gat{i}") for i in range(2)]
        attr_in = [S.sem(f"attr{i}") for i in range(2)]
        with nc.Block() as block:

            @block.gpsimd
            def _(pool):
                def gather(g, slot, turn):
                    hold(K, pool, at_ready, g + 1)
                    hold(K, pool, taken, g - 1)
                    for j in range(GT):
                        for m, (table, c) in enumerate(((q, 1), (k, 0))):
                            pool.indirect_dma_start(
                                got[slot][m][:, j, :], None, table,
                                bass.IndirectOffsetOnAxis(ap=at[slot][:, j, c:c + 1], axis=0)).then_inc(gathered[slot], 16)

                skewed(pool, G, [(0, gather)])

            @block.sync
            def _(sp):
                sp.dma_start(We[:, :], a["L1_gnn_We"]).then_inc(loaded, 16)
                sp.dma_start(be[:, :], a["L1_gnn_be"].rearrange("(o n) -> o n", o=1)).then_inc(loaded, 16)

                def load(g, slot, turn):
                    await_(sp, turned, g - 1)
                    sp.dma_start(attr[slot][:, :, :], K.rec[1][0:E, :].rearrange("(t p) c -> p t c", p=P)[:, bass.ds(g * GT, GT), 4:4 + AW]).then_inc(attr_in[slot], 16)

                skewed(sp, G, [(0, load)])

            @block.tensor
            def _(pe):
                pe.wait_ge(loaded, 32)

                def turn_(g, slot, turn):
                    pe.wait_ge(attr_in[slot], 16 * turn + 16)
                    hold(K, pe, copied, g)
                    for j in range(GT):
                        ins = pe.transpose(T[:, j, 0:P], attr[slot][:, j, :], K.ident[0:P, 0:P])
                    ins.then_inc(turned, 1)

                def multiply(g, slot, turn):
                    hold(K, pe, copied, g + 1)
                    hold(K, pe, taken, g - 1)
                    for j in range(GT):
                        pe.matmul(ep[slot][:, j, 0:DH], K.ones[0:1, 0:P], be[0:1, :], start=True, stop=False)
                        ins = pe.matmul(ep[slot][:, j, 0:DH], attrT[slot][:, j, :], We[:, :], start=False, stop=True)
                    ins.then_inc(ep_ready, 1)

                skewed(pe, G, [(1, multiply), (0, turn_)])

            @block.scalar
            def _(act):
                def copy(g, slot, turn):
                    hold(K, act, ep_ready, g - 1)
                    act.wait_ge(turned, g + 1)
                    act.activation(attrT[slot][:, :, :], T[:, :, 0:P], ACT.Copy).then_inc(copied, 1)

                skewed(act, G, [(0, copy)])

            @block.vector
            def _(dve):
                link = S.link(dve, "l")

                def indices_(g, slot, turn):
                    hold(K, dve, gathered[slot], 128 * turn)
                    dve.tensor_copy(at[slot][:, :, :], K.idx[1][:, bass.ds(g * GT, GT), :]).then_inc(at_ready, 1)

                def score(g, slot, turn):
                    link.restart()
                    dve.wait_ge(gathered[slot], 128 * turn + 128)
                    dve.wait_ge(ep_ready, g + 1)
                    for j in range(GT):
                        ins = dve.tensor_tensor(keyed[slot][:, j, :].rearrange("p (h d) -> p h d", d=DH),
                                                got[slot][1][:, j, :].rearrange("p (h d) -> p h d", d=DH),
                                                over(ep[slot][:, j, 0:DH].unsqueeze(1), [P, HEADS, DH]), ALU.add)
                    link(ins)
                    dve.tensor_tensor(prod[slot][:, :, :], keyed[slot][:, :, :], got[slot][0][:, :, :], ALU.mult).then_inc(taken, 1)
                    dve.wait_ge(taken, g + 1)
                    link(dve.reduce_sum(dots[slot][:, :, :], prod[slot][:, :, :].rearrange("p j (h d) -> p j h d", d=DH), AX.X))
                    groups = bass.ds(g * GT, GT)
                    link(dve.scalar_tensor_tensor(K.scores[:, groups, :], dots[slot][:, :, :], DH ** -0.5,
                                                  over(K.fk[1][:, groups, 1:2], [P, GT, HEADS]), ALU.mult, ALU.mult))

                skewed(dve, G, [(0, indices_), (1, score)])


def softmax_numerators(K, name):
    nc = K.nc
    S = Stage(K, name)
    PT = ET // SCAN
    L = PT * P
    C = SCAN * HEADS
    with S.ctx:
        s = S.sb("s", [C, L])
        key = S.sb("key", [C, L])
        pen = S.sb("pen", [C, L + 1])
        fwd = S.sb("fwd", [C, L])
        bwd = S.sb("bwd", [C, L])
        parted = S.sb("parted", [P, 2, PT, SCAN, HEADS])
        col = S.sb("col", [C, 4])
        rows = S.sb("rows", [1, 4, C])
        small = S.sb("small", [1, 8, C])
        back = S.sb("back", [C, 2])
        big = S.sb("big", [C, 1])
        zero = S.sb("zero", [C, L], u32)
        ps = [S.ps(f"ps{i}", [C, GT, 128]) for i in range(7)]
        bank = S.ps("bank", [C, 512])
        turned, copied, keys_turned, keys_copied = S.sem("t"), S.sem("c"), S.sem("kt"), S.sem("kc")
        cols_ready, rows_ready, edges_ready, edges_back, max_ready, exped = (S.sem(x) for x in ("co", "ro", "er", "eb", "mr", "ex"))
        out_turned, out_copied, parted_ready = S.sem("ot"), S.sem("oc"), S.sem("pr")
        where = [(j // GT, j % GT) for j in range(PT)]
        with nc.Block() as block:

            @block.tensor
            def _(pe):
                pe.wait_ge(parted_ready, 1)
                for x, (done, before) in enumerate(((turned, None), (keys_turned, copied))):
                    for j, (b, i) in enumerate(where):
                        if before is not None and i == 0:
                            pe.wait_ge(before, b + 1)
                        ins = pe.transpose(ps[b][:, i, 0:P], parted[:, x, j, :, :].rearrange("p c h -> p (c h)"), K.ident[0:P, 0:P])
                        if i == GT - 1 or j == PT - 1:
                            ins.then_inc(done, 1)
                pe.wait_ge(cols_ready, 1)
                for i in range(4):
                    ins = pe.matmul(bank[0:1, i * C:(i + 1) * C], col[:, i:i + 1], K.ident[:, :], start=True, stop=True)
                ins.then_inc(rows_ready, 1)
                pe.wait_ge(edges_ready, 1)
                for i in range(2):
                    ins = pe.matmul(bank[:, i:i + 1], small[0:1, 6 + i, :], K.ones[0:1, 0:1], start=True, stop=True)
                ins.then_inc(edges_back, 1)
                pe.wait_ge(exped, 1)
                for j, (b, i) in enumerate(where):
                    ins = pe.transpose(ps[b][0:P, i, :], fwd[:, j * P:(j + 1) * P], K.ident[:, :])
                    if i == GT - 1 or j == PT - 1:
                        ins.then_inc(out_turned, 1)

            @block.scalar
            def _(act):
                for dst, done, told in ((s, turned, copied), (key, keys_turned, keys_copied)):
                    for b in range(7):
                        n = min(GT, PT - b * GT)
                        act.wait_ge(done, b + 1)
                        act.activation(dst[:, b * GT * P:(b * GT + n) * P].rearrange("c (j e) -> c j e", e=P), ps[b][:, 0:n, 0:P], ACT.Copy).then_inc(told, 1)
                act.wait_ge(max_ready, 1)
                act.activation(fwd[:, :], s[:, :], ACT.Exp).then_inc(exped, 1)
                for j, (b, i) in enumerate(where):
                    if i == 0:
                        act.wait_ge(out_turned, b + 1)
                    act.activation(K.scores[:, j:ET:PT, :], ps[b][0:P, i, :].rearrange("p (c h) -> p c h", h=HEADS), ACT.Copy).then_inc(out_copied, 1)
                act.wait_ge(out_copied, PT)

            @block.vector
            def _(dve):
                link = S.link(dve, "l")
                dve.tensor_copy(parted[:, 0, :, :, :], K.scores[:, :, :].rearrange("p (c j) h -> p j c h", j=PT))
                dve.tensor_copy(parted[:, 1, :, :, :], over(K.fk[1][:, :, 0].rearrange("p (c j) -> p j c", j=PT).unsqueeze(3), [P, PT, SCAN, HEADS])).then_inc(parted_ready, 1)
                link(dve.memset(pen[:, :], -1e30))
                link(dve.memset(zero[:, :], 0))
                dve.wait_ge(keys_copied, 7)
                link(dve.tensor_tensor(pen[:, 1:L], key[:, 1:L], key[:, 0:L - 1], ALU.is_equal))
                link(dve.tensor_scalar(pen[:, 1:L], pen[:, 1:L], -1.0, 1e30, ALU.add, ALU.mult))
                link(dve.tensor_tensor_scan(fwd[:, :], pen[:, 0:L], s[:, :], -1e30, ALU.add, ALU.max))
                link(dve.tensor_tensor_scan(bwd[:, ::-1], pen[:, L:0:-1], s[:, ::-1], -1e30, ALU.add, ALU.max))
                dve.tensor_copy(col[:, 0:1], key[:, 0:1])
                dve.tensor_copy(col[:, 1:2], key[:, L - 1:L])
                dve.tensor_copy(col[:, 2:3], fwd[:, L - 1:L])
                dve.tensor_copy(col[:, 3:4], bwd[:, 0:1]).then_inc(cols_ready, 1)
                dve.wait_ge(rows_ready, 1)
                link(dve.tensor_copy(rows[:, :, :].rearrange("o i (h c) -> o i h c", h=HEADS),
                                     bank[0:1, :].rearrange("o (i c h) -> o i h c", i=4, h=HEADS)))
                first, last_, fend, bbeg = (rows[:, i, :].rearrange("o (h c) -> o h c", h=HEADS) for i in range(4))
                v = [small[:, i, :].rearrange("o (h c) -> o h c", h=HEADS) for i in range(8)]
                link(dve.memset(small[:, :, :], 0.0))
                link(dve.tensor_tensor(v[0][:, :, 1:SCAN], first[:, :, 1:SCAN], last_[:, :, 0:SCAN - 1], ALU.is_equal))
                link(dve.tensor_tensor(v[1][:, :, :], first, last_, ALU.is_equal))
                link(dve.tensor_tensor(v[2][:, :, :], v[1], v[0], ALU.mult))
                link(dve.tensor_tensor(v[3][:, :, 0:SCAN - 1], v[1][:, :, 0:SCAN - 1], v[0][:, :, 1:SCAN], ALU.mult))
                for i in (2, 3):
                    link(dve.tensor_scalar(small[:, i, :], small[:, i, :], -1.0, 1e30, ALU.add, ALU.mult))
                link(dve.tensor_tensor_scan(small[:, 4, :], small[:, 2, :], rows[:, 2, :], -1e30, ALU.add, ALU.max))
                link(dve.tensor_tensor_scan(small[:, 5, ::-1], small[:, 3, ::-1], rows[:, 3, ::-1], -1e30, ALU.add, ALU.max))
                link(dve.memset(small[:, 6:8, :], -1e30))
                into = [small[:, i, :].rearrange("o (c h) -> o h c", h=HEADS) for i in (6, 7)]
                link(dve.tensor_scalar(v[1][:, :, :], v[0], -1.0, 1e30, ALU.add, ALU.mult))
                link(dve.tensor_tensor(into[0][:, :, 1:SCAN], v[4][:, :, 0:SCAN - 1], v[0][:, :, 1:SCAN], ALU.mult))
                link(dve.tensor_tensor(into[0][:, :, 1:SCAN], into[0][:, :, 1:SCAN], v[1][:, :, 1:SCAN], ALU.add))
                link(dve.tensor_tensor(into[1][:, :, 0:SCAN - 1], v[5][:, :, 1:SCAN], v[0][:, :, 1:SCAN], ALU.mult))
                dve.tensor_tensor(into[1][:, :, 0:SCAN - 1], into[1][:, :, 0:SCAN - 1], v[1][:, :, 1:SCAN], ALU.add).then_inc(edges_ready, 1)
                link(dve.tensor_tensor(fwd[:, :], fwd[:, :], bwd[:, :], ALU.max))
                dve.wait_ge(edges_back, 1)
                link(dve.tensor_copy(back[:, :], bank[:, 0:2]))
                for i in range(2):
                    link(dve.tensor_scalar(bwd[:, :], key[:, :], col[:, i:i + 1], None, ALU.is_equal))
                    link(dve.tensor_scalar(pen[:, 0:L], bwd[:, :], -1.0, 1e30, ALU.add, ALU.mult))
                    link(dve.scalar_tensor_tensor(bwd[:, :], bwd[:, :], back[:, i:i + 1], pen[:, 0:L], ALU.mult, ALU.add))
                    link(dve.tensor_tensor(fwd[:, :], fwd[:, :], bwd[:, :], ALU.max))
                link(dve.tensor_scalar(bwd[:, :].bitcast(u32), fwd[:, :], FLT_MAX, None, ALU.is_gt))
                link(dve.copy_predicated(fwd[:, :], bwd[:, :].bitcast(u32), zero[:, :].bitcast(fp32)))
                link(dve.tensor_scalar(bwd[:, :].bitcast(u32), fwd[:, :], -FLT_MAX, None, ALU.is_lt))
                link(dve.copy_predicated(fwd[:, :], bwd[:, :].bitcast(u32), zero[:, :].bitcast(fp32)))
                dve.tensor_tensor(s[:, :], s[:, :], fwd[:, :], ALU.subtract).then_inc(max_ready, 1)


def attention_layer(K, a):
    nc = K.nc
    Q, Kt, V = (K.dram(n, (N, D)) for n in ("aQ", "aK", "aV"))
    normalise(K, "a0_", K.X, K.H)
    S = Stage(K, "a_")
    with S.ctx:
        H2 = S.sb("H2", [P, NT, D])
        normalise(K, "a1_", K.H, H2, a["L1_gnn_ln1_g"], a["L1_gnn_ln1_b"])
        project(K, "a2_", H2, [a["L1_gnn_W" + c] for c in "qkv"], [a["L1_gnn_b" + c] for c in "qkv"], [Q, Kt, V])
    edge_scores(K, "a3_", a, Q, Kt)
    softmax_numerators(K, "a4_")
    edge_sums(K, "a5_", ATTEND, 1, [V], [0], D + HEADS)
    S = Stage(K, "ab_")
    with S.ctx:
        agg = S.sb("agg", [P, NT, D + HEADS])
        rec = S.sb("rec", [P, NT, HEADS])
        H2 = S.sb("H2", [P, NT, D])
        ab = S.sb("ab", [P, 2])
        done, loaded = S.sem("done"), S.sem("ld")
        collect(K, "a6_", 1, D + HEADS, agg)
        with nc.Block() as block:

            @block.sync
            def _(sp):
                for i, n in enumerate(("alpha", "beta")):
                    sp.dma_start(ab[:, i:i + 1], a["L1_gnn_" + n].partition_broadcast(P)).then_inc(loaded, 16)
                sp.wait_ge(loaded, 32)

            @block.vector
            def _(dve):
                link = S.link(dve, "l")
                link(dve.tensor_scalar(rec[:, :, :], agg[:, :, D:D + HEADS], 1e-30, None, ALU.max))
                link(dve.reciprocal(rec[:, :, :], rec[:, :, :]))
                for t in range(NT):
                    ins = dve.tensor_tensor(agg[:, t, 0:D].rearrange("p (h d) -> p h d", d=DH), agg[:, t, 0:D].rearrange("p (h d) -> p h d", d=DH),
                                            over(rec[:, t, :].unsqueeze(2), [P, HEADS, DH]), ALU.mult)
                link(ins)

        project(K, "a7_", agg, [a["L1_gnn_Wo"]], [a["L1_gnn_bo"]], None, into=H2)
        with nc.Block() as block:

            @block.vector
            def _(dve):
                link = S.link(dve, "l2")
                link(dve.scalar_tensor_tensor(K.H[:, :, :].rearrange("p t w -> p (t w)"), H2[:, :, :].rearrange("p t w -> p (t w)"), ab[:, 0:1],
                                              K.H[:, :, :].rearrange("p t w -> p (t w)"), ALU.mult, ALU.add))
                link(dve.tensor_tensor(K.X[:, :, :], K.X[:, :, :], K.H[:, :, :], ALU.add))

        normalise(K, "a8_", K.H, H2, a["L1_gnn_ln2_g"], a["L1_gnn_ln2_b"])
        T = S.sb("T", [128, 2, NT * 128])
        turn(K, "a9_", H2, T)
        feed_forward(K, "aa_", [T], 8, a["L1_gnn_W1"], a["L1_gnn_b1"], a["L1_gnn_W2"], a["L1_gnn_b2"], ACT.Gelu, K.X, factor=ab[:, 1:2])


def switch_layer(K, a):
    nc = K.nc
    EX, F = 8, 8
    ROOM = -(-N * 125 // (100 * EX))
    SLOT = 512
    buf, ybuf = K.dram("buf", (EX * SLOT, D)), K.dram("ybuf", (EX * SLOT, D))
    normalise(K, "s0_", K.X, K.H)
    S = Stage(K, "s_")
    with S.ctx:
        logit = S.sb("logit", [P, NT, EX])
        row = S.sb("row", [P, 2, NT], i32)
        wt = S.sb("wt", [P, NT])
        S2 = Stage(K, "sa_")
        with S2.ctx:
            T = S2.sb("T", [128, 2, NT * 128])
            turn(K, "s1_", K.H, T, gate=(a["L1_ffn_gate_w"], a["L1_ffn_gate_b"], EX, logit))
        S2 = Stage(K, "sb_")
        with S2.ctx:
            prob = S2.sb("prob", [P, NT, EX])
            m = S2.sb("m", [P, 6, NT])
            top = S2.sb("top", [P, NT, 8])
            which = S2.sb("which", [P, NT, 8], u32)
            hot = S2.sb("hot", [P, NT, EX])
            incl = S2.sb("incl", [P, NT, EX])
            zeros = S2.sb("zeros", [128, 8, D])
            earlier = S2.ps("earlier", [P, 512])
            shifted, exped, counted, summed, zero_set = (S2.sem(x) for x in ("sh", "ex", "cn", "sm", "z"))
            row_ready, cleared, scattered = S2.sem("row"), S2.sem("clr"), S2.indirect("ind")
            wide = [P, NT, EX]
            with nc.Block() as block:

                @block.vector
                def _(dve):
                    link = S2.link(dve, "l")
                    dve.memset(zeros[:, :, :], 0.0).then_inc(zero_set, 1)
                    link(dve.reduce_max(m[:, 0, :], logit[:, :, :], AX.X))
                    dve.tensor_tensor(logit[:, :, :], logit[:, :, :], over(m[:, 0, :].unsqueeze(2), wide), ALU.subtract).then_inc(shifted, 1)
                    dve.wait_ge(exped, 1)
                    link(dve.reduce_sum(m[:, 1, :], prob[:, :, :], AX.X))
                    link(dve.reciprocal(m[:, 2, :], m[:, 1, :]))
                    link(dve.tensor_tensor(prob[:, :, :], prob[:, :, :], over(m[:, 2, :].unsqueeze(2), wide), ALU.mult))
                    for t in range(NT):
                        ins = dve.max(top[:, t, :], prob[:, t, :])
                    link(ins)
                    for t in range(NT):
                        ins = dve.max_index(which[:, t, :], top[:, t, :], prob[:, t, :])
                    link(ins)
                    link(dve.tensor_copy(m[:, 3, :], which[:, :, 0]))
                    link(dve.tensor_tensor(hot[:, :, :], over(K.iota64[0:P, 0:EX].unsqueeze(1), wide), over(m[:, 3, :].unsqueeze(2), wide), ALU.is_equal))
                    for e in range(EX):
                        ins = dve.tensor_tensor_scan(incl[:, :, e], hot[:, :, e], hot[:, :, e], 0.0, ALU.add, ALU.bypass)
                    ins.then_inc(counted, 1)
                    dve.wait_ge(summed, 1)
                    link(dve.tensor_tensor(prob[:, :, :], incl[:, :, :], over(earlier[:, 0:EX].unsqueeze(1), wide), ALU.add))
                    link(dve.tensor_tensor(prob[:, :, :], prob[:, :, :], hot[:, :, :], ALU.mult))
                    link(dve.reduce_sum(m[:, 4, :], prob[:, :, :], AX.X))
                    link(dve.tensor_scalar(m[:, 5, :], m[:, 4, :], float(ROOM), None, ALU.is_le))
                    link(dve.tensor_tensor(wt[:, :], m[:, 5, :], top[:, :, 0], ALU.mult))
                    link(dve.tensor_scalar(m[:, 4, :], m[:, 4, :], float(ROOM), -1.0, ALU.min, ALU.add))
                    link(dve.scalar_tensor_tensor(m[:, 4, :], m[:, 3, :], float(SLOT), m[:, 4, :], ALU.mult, ALU.add))
                    link(dve.tensor_copy(row[:, 0, :], m[:, 4, :]))
                    link(dve.tensor_scalar(m[:, 5, :], m[:, 5, :], -2.0 * EX * SLOT, 2.0 * EX * SLOT, ALU.mult, ALU.add))
                    dve.tensor_tensor(row[:, 1, :], m[:, 4, :], m[:, 5, :], ALU.add).then_inc(row_ready, 1)

                @block.scalar
                def _(act):
                    act.wait_ge(shifted, 1)
                    act.activation(prob[:, :, :], logit[:, :, :], ACT.Exp).then_inc(exped, 1)

                @block.tensor
                def _(pe):
                    pe.wait_ge(counted, 1)
                    pe.matmul(earlier[:, 0:EX], K.before[0:P, 0:P], incl[:, NT - 1, :], start=True, stop=True).then_inc(summed, 1)

                @block.sync
                def _(sp):
                    sp.wait_ge(zero_set, 1)
                    for i in range(EX * SLOT // 1024):
                        sp.dma_start(buf[i * 1024:(i + 1) * 1024, :].rearrange("(p j) n -> p j n", p=128), zeros[:, :, :]).then_inc(cleared, 16)

                @block.gpsimd
                def _(pool):
                    pool.wait_ge(cleared, 16 * (EX * SLOT // 1024))
                    pool.wait_ge(row_ready, 1)
                    for t in range(NT):
                        pool.indirect_dma_start(buf, bass.IndirectOffsetOnAxis(ap=row[:, 1, t:t + 1], axis=0), K.H[:, t, :], None,
                                                bounds_check=EX * SLOT - 1, oob_is_err=False).then_inc(scattered, 16)
                    pool.wait_ge(scattered, 16 * NT)

        switch_experts(K, "s3_", a, buf, ybuf, SLOT, EX, F)
        S2 = Stage(K, "sc_")
        with S2.ctx:
            y = S2.sb("y", [P, NT, D])
            odd = S2.sb("odd", [P, NT, D], u32)
            value = S2.sb("value", [P, 4])
            gathered = S2.indirect("ind")
            with nc.Block() as block:

                @block.gpsimd
                def _(pool):
                    for t in range(NT):
                        pool.indirect_dma_start(y[:, t, :], None, ybuf, bass.IndirectOffsetOnAxis(ap=row[:, 0, t:t + 1], axis=0)).then_inc(gathered, 16)

                @block.vector
                def _(dve):
                    link = S2.link(dve, "l")
                    for i, v in enumerate((0.0, 1e4, -1e4)):
                        link(dve.memset(value[:, i:i + 1], v))
                    dve.wait_ge(gathered, 16 * NT)
                    link(dve.tensor_tensor(y[:, :, :], y[:, :, :], over(wt[:, :].unsqueeze(2), [P, NT, D]), ALU.mult))
                    flat, mask = y[:, :, :].rearrange("p t w -> p (t w)"), odd[:, :, :].rearrange("p t w -> p (t w)")
                    for i in range(3):
                        if i == 0:
                            link(dve.tensor_tensor(mask, flat, flat, ALU.not_equal))
                        else:
                            link(dve.tensor_scalar(mask, flat, (FLT_MAX, -FLT_MAX)[i - 1], None, (ALU.is_gt, ALU.is_lt)[i - 1]))
                        link(dve.copy_predicated(flat, mask, over(value[:, i:i + 1], [P, NT * D])))
                    link(dve.tensor_tensor(K.X[:, :, :], K.X[:, :, :], y[:, :, :], ALU.add))


def switch_experts(K, name, a, buf, ybuf, SLOT, EX, F):
    nc = K.nc
    S = Stage(K, name)
    R = SLOT // 128
    H = F * 128
    with S.ctx:
        w1 = [S.sb(f"w1{i}", [128, 2, H]) for i in range(2)]
        c1 = [S.sb(f"c1{i}", [128, F]) for i in range(2)]
        w2 = [S.sb(f"w2{i}", [128, F, D]) for i in range(2)]
        c2 = [S.sb(f"c2{i}", [1, 2 * D]) for i in range(2)]
        rows = [S.sb(f"rows{i}", [128, R, D]) for i in range(2)]
        rowsT = [S.sb(f"rowsT{i}", [128, 2, SLOT]) for i in range(2)]
        hid = [S.sb(f"hid{i}", [128, SLOT]) for i in range(2)]
        res = [S.sb(f"res{i}", [128, R, D]) for i in range(2)]
        T = S.ps("T", [128, 2, SLOT])
        hp = [S.ps(f"hp{i}", [128, SLOT]) for i in range(2)]
        y = S.ps("y", [128, R, D])
        loaded = [S.sem(f"ld{i}") for i in range(2)]
        stored = [S.sem(f"st{i}") for i in range(2)]
        turned, copied, h_done, h_used, y_done, ready = (S.sem(x) for x in ("tr", "cp", "hd", "hu", "yd", "rd"))
        with nc.Block() as block:

            @block.sync
            def _(sp):
                def load(e, slot, turn):
                    await_(sp, y_done, (e - 1) * F)
                    one = bass.ds(e, 1)
                    sp.dma_start(w1[slot][:, :, :], a["L1_ffn_w1"][one].rearrange("o (k p) f -> p (o k) f", p=128)).then_inc(loaded[slot], 16)
                    sp.dma_start(c1[slot][:, :], a["L1_ffn_b1"][one, :].rearrange("o (f p) -> p (o f)", p=128), allow_slow_non_contiguous=True).then_inc(loaded[slot], 16)
                    sp.dma_start(w2[slot][:, :, :], a["L1_ffn_w2"][one].rearrange("o (f p) n -> p (o f) n", p=128)).then_inc(loaded[slot], 16)
                    for h in range(2):
                        sp.dma_start(c2[slot][:, h * D:(h + 1) * D], a["L1_ffn_b2"][one, :]).then_inc(loaded[slot], 16)
                    sp.dma_start(rows[slot][:, :, :], buf[bass.ds(e * SLOT, SLOT), :].rearrange("(r p) n -> p r n", p=128)).then_inc(loaded[slot], 16)

                def store(e, slot, turn):
                    sp.wait_ge(ready, e + 1)
                    sp.dma_start(ybuf[bass.ds(e * SLOT, SLOT), :].rearrange("(r p) n -> p r n", p=128), res[slot][:, :, :]).then_inc(stored[slot], 16)

                skewed(sp, EX, [(2, store), (0, load)])
                for u in range(2):
                    sp.wait_ge(stored[u], 16 * (EX // 2))

            @block.tensor
            def _(pe):
                def turn_(e, slot, turn):
                    pe.wait_ge(loaded[slot], 96 * (turn + 1))
                    hold(K, pe, copied, e)
                    for k in range(2):
                        for r in range(R):
                            ins = pe.transpose(T[:, k, r * 128:(r + 1) * 128], rows[slot][:, r, k * 128:(k + 1) * 128], K.ident[:, :])
                    ins.then_inc(turned, 1)

                def expert(e, slot, turn):
                    hold(K, pe, copied, e + 1)

                    def hidden(f):
                        await_(pe, h_used, e * F + (f - 1))
                        for k in range(2):
                            ins = pe.matmul(hp[f % 2][:, :], w1[slot][:, k, f * 128:(f + 1) * 128], rowsT[slot][:, k, :], start=(k == 0), stop=(k == 1))
                        ins.then_inc(h_done, 1)

                    def outward(f):
                        pe.wait_ge(h_used, e * F + (f + 1))
                        if f == 0:
                            await_(pe, ready, e)
                            for b in range(2):
                                pe.matmul(y[:, 2 * b:2 * b + 2, :].rearrange("p j n -> p (j n)"), K.ones[0:1, 0:128], c2[slot][0:1, :], start=True, stop=True)
                        for r in range(R):
                            ins = pe.matmul(y[:, r, :], hid[f % 2][:, r * 128:(r + 1) * 128], w2[slot][:, f, :], start=False, stop=True, skip_group_check=True)
                        ins.then_inc(y_done, 1)

                    hidden(0)
                    for f in range(1, F):
                        hidden(f)
                        outward(f - 1)
                    outward(F - 1)

                skewed(pe, EX, [(0, turn_), (1, expert)])

            @block.scalar
            def _(act):
                def copy(e, slot, turn):
                    hold(K, act, y_done, (e - 1) * F)
                    act.wait_ge(turned, e + 1)
                    act.activation(rowsT[slot][:, :, :], T[:, :, :], ACT.Copy).then_inc(copied, 1)

                def expert(e, slot, turn):
                    for f in range(F):
                        if f == 0:
                            hold(K, act, loaded[slot], 96 * (turn + 1))
                        hold(K, act, y_done, e * F + (f - 1))
                        act.wait_ge(h_done, e * F + (f + 1))
                        act.activation(hid[f % 2][:, :], hp[f % 2][:, :], ACT.Relu, bias=c1[slot][:, f:f + 1]).then_inc(h_used, 1)

                skewed(act, EX, [(0, copy), (1, expert)])

            @block.vector
            def _(dve):
                def finish(e, slot, turn):
                    hold(K, dve, stored[slot], 16 * turn)
                    dve.wait_ge(y_done, (e + 1) * F)
                    dve.tensor_copy(res[slot][:, :, :], y[:, :, :]).then_inc(ready, 1)

                skewed(dve, EX, [(0, finish)])


def gat_layer(K, a):
    nc = K.nc
    normalise(K, "g0_", K.X, K.H)
    for layer in (1, 2):
        pre = f"g{layer}"
        table = K.dram(pre + "t", (N, D + 1))
        project(K, pre + "a_", K.H, [a[f"L2_gnn_W{layer}"]], [None], [table], score=a[f"L2_gnn_a{layer}"])
        edge_sums(K, pre + "b_", GAT, 0, [table, K.ss], [1, 0], D + 1)
        S = Stage(K, pre + "_")
        with S.ctx:
            agg = S.sb("agg", [P, NT, D + 1])
            rec = S.sb("rec", [P, NT])
            neg = S.sb("neg", [P, NT, D])
            negative, exped = S.sem("neg"), S.sem("ex")
            collect(K, pre + "c_", 0, D + 1, agg)
            with nc.Block() as block:

                @block.vector
                def _(dve):
                    link = S.link(dve, "l")
                    link(dve.reciprocal(rec[:, :], agg[:, :, D]))
                    link(dve.tensor_tensor(K.H[:, :, :], agg[:, :, 0:D], over(rec[:, :].unsqueeze(2), [P, NT, D]), ALU.mult))
                    flat = K.H[:, :, :].rearrange("p t w -> p (t w)")
                    nflat = neg[:, :, :].rearrange("p t w -> p (t w)")
                    dve.tensor_scalar(nflat, flat, 0.0, None, ALU.min).then_inc(negative, 1)
                    dve.wait_ge(exped, 1)
                    link(dve.tensor_scalar(nflat, nflat, -1.0, None, ALU.add))
                    link(dve.scalar_tensor_tensor(flat, flat, 0.0, nflat, ALU.max, ALU.add))
                    if layer == 2:
                        link(dve.tensor_tensor(K.X[:, :, :], K.X[:, :, :], K.H[:, :, :], ALU.add))

                @block.scalar
                def _(act):
                    act.wait_ge(negative, 1)
                    act.activation(neg[:, :, :], neg[:, :, :], ACT.Exp).then_inc(exped, 1)


def depth_layer(K, a):
    nc = K.nc
    SELECTED = N // 2 - 1
    wrow = K.dram("wrow", (N,))
    normalise(K, "d0_", K.X, K.H)
    S = Stage(K, "d_")
    with S.ctx:
        T = S.sb("T", [128, 2, NT * 128])
        w = S.sb("w", [P, NT, 1])
        wts = S.sb("wts", [P, NT, 1])
        turn(K, "d1_", K.H, T, gate=(a["L2_ffn_wr"], a["L2_ffn_br"], 1, w))
        S2 = Stage(K, "da_")
        with S2.ctx:
            row = S2.sb("row", [P, N])
            sooner = S2.sb("sooner", [P, N + NT])
            later = S2.sb("later", [P, N + NT])
            junk = S2.sb("junk", [P, 2, N])
            rank = S2.sb("rank", [P, 2, NT])
            stored, loaded, masks = S2.sem("st"), S2.sem("ld"), S2.sem("m")
            with nc.Block() as block:

                @block.sync
                def _(sp):
                    sp.dma_start(wrow.rearrange("(p t) -> p t", t=NT), w[:, :, 0]).then_inc(stored, 16)
                    sp.wait_ge(stored, 16)
                    sp.dma_start(row[:, :], wrow.partition_broadcast(P)).then_inc(loaded, 16)

                @block.gpsimd
                def _(pool):
                    pool.memset(sooner[:, :], 1.0).then_inc(masks, 1)
                    pool.memset(later[:, :], 0.0).then_inc(masks, 1)
                    pool.wait_ge(masks, 2)
                    for m, fill in ((sooner, 0.0), (later, 1.0)):
                        pool.affine_select(out=m[:, :], in_=m[:, :], compare_op=ALU.is_gt, fill=fill, base=NT - 1,
                                           pattern=[[-1, N + NT]], channel_multiplier=NT).then_inc(masks, 1)

                @block.vector
                def _(dve):
                    link = S2.link(dve, "l")
                    dve.wait_ge(loaded, 16)
                    dve.wait_ge(masks, 4)
                    for t in range(NT):
                        at = slice(NT - 1 - t, NT - 1 - t + N)
                        dve.scalar_tensor_tensor(junk[:, 0, :], row[:, :], w[:, t, 0:1], sooner[:, at], ALU.is_ge, ALU.mult, accum_out=rank[:, 0, t:t + 1])
                        link(dve.scalar_tensor_tensor(junk[:, 1, :], row[:, :], w[:, t, 0:1], later[:, at], ALU.is_gt, ALU.mult, accum_out=rank[:, 1, t:t + 1]))
                    link(dve.tensor_tensor(rank[:, 0, :], rank[:, 0, :], rank[:, 1, :], ALU.add))
                    link(dve.scalar_tensor_tensor(wts[:, :, 0], rank[:, 0, :], float(SELECTED), w[:, :, 0], ALU.is_lt, ALU.mult))

        add_into(K, "d2_", K.X, K.H)
        feed_forward(K, "d3_", [T], 8, a["L2_ffn_w1"], a["L2_ffn_b1"], a["L2_ffn_w2"], a["L2_ffn_b2"], ACT.Gelu_apprx_tanh, K.X, by_tile=wts)


def conv_layer(K, a):
    nc = K.nc
    WT, table = K.dram("WT", (D, D)), K.dram("cT", (N, D + 1))
    normalise(K, "v0_", K.X, K.H)
    S = Stage(K, "va_")
    with S.ctx:
        w = S.sb("w", [128, 2, D])
        wt = S.sb("wt", [128, 2, D])
        ps = S.ps("ps", [128, 2, D])
        loaded, turned, copied, stored = (S.sem(x) for x in ("ld", "tr", "cp", "st"))
        with nc.Block() as block:

            @block.sync
            def _(sp):
                sp.dma_start(w[:, :, :], a["L3_gnn_W"].rearrange("(k p) i -> p k i", p=128)).then_inc(loaded, 16)
                sp.wait_ge(copied, 1)
                sp.dma_start(WT.rearrange("(k p) o -> p k o", p=128), wt[:, :, :]).then_inc(stored, 16)
                sp.wait_ge(stored, 16)

            @block.tensor
            def _(pe):
                pe.wait_ge(loaded, 16)
                for k in range(2):
                    for o in range(2):
                        ins = pe.transpose(ps[:, k, o * 128:(o + 1) * 128], w[:, o, k * 128:(k + 1) * 128], K.ident[:, :])
                ins.then_inc(turned, 1)

            @block.scalar
            def _(act):
                act.wait_ge(turned, 1)
                act.activation(wt[:, :, :], ps[:, :, :], ACT.Copy).then_inc(copied, 1)

    project(K, "v1_", K.H, [WT], [a["L3_gnn_b"]], [table])
    edge_sums(K, "v2_", COPY, 1, [table], [0], D + 1)
    S = Stage(K, "vb_")
    with S.ctx:
        agg = S.sb("agg", [P, NT, D + 1])
        rec = S.sb("rec", [P, NT])
        collect(K, "v3_", 1, D + 1, agg)
        with nc.Block() as block:

            @block.vector
            def _(dve):
                link = S.link(dve, "l")
                link(dve.tensor_scalar(rec[:, :], agg[:, :, D], 1.0, None, ALU.add))
                link(dve.reciprocal(rec[:, :], rec[:, :]))
                link(dve.tensor_tensor(K.H[:, :, :], agg[:, :, 0:D], over(rec[:, :].unsqueeze(2), [P, NT, D]), ALU.mult))
                link(dve.tensor_tensor(K.X[:, :, :], K.X[:, :, :], K.H[:, :, :], ALU.add))


def mixture_layer(K, a):
    nc = K.nc
    EX = 8
    CAPACITY = float(-(-N * 125 // (100 * EX)))
    normalise(K, "x0_", K.X, K.H)
    S = Stage(K, "x_")
    with S.ctx:
        T = S.sb("T", [128, 2, NT * 128])
        which = S.sb("which", [P, 8], u32)
        w2 = S.sb("w2", [P, 2])
        S2 = Stage(K, "xa_")
        with S2.ctx:
            mean = S2.sb("mean", [128, 2])
            Wr = S2.sb("Wr", [128, 2, EX])
            br = S2.sb("br", [P, EX])
            v = S2.sb("v", [P, 8, EX])
            c = S2.sb("c", [P, 8])
            top = S2.sb("top", [P, 8])
            ps = [S2.ps(f"ps{i}", [128, 512]) for i in range(3)]
            loaded, summed, mean_ready, routed = (S2.sem(x) for x in ("ld", "sm", "mn", "rt"))
            shifted, exped = S2.sem("sh"), S2.sem("ex")
            with nc.Block() as block:

                @block.sync
                def _(sp):
                    sp.dma_start(Wr[:, :, :], a["L3_ffn_Wr"].rearrange("(k p) n -> p k n", p=128)).then_inc(loaded, 16)
                    sp.dma_start(br[:, :], a["L3_ffn_br"].partition_broadcast(P)).then_inc(loaded, 16)

                @block.tensor
                def _(pe):
                    pe.wait_ge(loaded, 32)
                    for k in range(2):
                        for t in range(NT):
                            ins = pe.matmul(ps[k][:, 0:1], K.H[:, t, k * 128:(k + 1) * 128], K.ones[0:P, 0:1], start=(t == 0), stop=(t == NT - 1))
                    ins.then_inc(summed, 1)
                    pe.wait_ge(mean_ready, 1)
                    for k in range(2):
                        ins = pe.matmul(ps[2][0:P, 0:EX], over(mean[:, k:k + 1], [128, P]), Wr[:, k, :], start=(k == 0), stop=(k == 1))
                    ins.then_inc(routed, 1)

                @block.scalar
                def _(act):
                    for i in range(2):
                        act.wait_ge(shifted, i + 1)
                        act.activation(v[:, 2, :], v[:, 1, :], ACT.Exp, accum_out=c[:, 1:2]).then_inc(exped, 1)
                    act.wait_ge(shifted, 3)
                    act.activation(c[:, 4:5], c[:, 3:4], ACT.Exp).then_inc(exped, 1)

                @block.vector
                def _(dve):
                    link = S2.link(dve, "l")
                    dve.wait_ge(summed, 1)
                    dve.tensor_scalar(mean[:, 0:1], ps[0][:, 0:1], 1.0 / N, None, ALU.mult)
                    dve.tensor_scalar(mean[:, 1:2], ps[1][:, 0:1], 1.0 / N, None, ALU.mult).then_inc(mean_ready, 1)
                    dve.wait_ge(routed, 1)
                    link(dve.tensor_tensor(v[:, 0, :], ps[2][0:P, 0:EX], br[:, :], ALU.add))

                    def softmax(i):
                        link(dve.reduce_max(c[:, 0:1], v[:, 0, :], AX.X))
                        dve.tensor_scalar(v[:, 1, :], v[:, 0, :], c[:, 0:1], None, ALU.subtract).then_inc(shifted, 1)
                        dve.wait_ge(exped, i + 1)
                        link(dve.reciprocal(c[:, 2:3], c[:, 1:2]))
                        link(dve.tensor_scalar(v[:, 3, :], v[:, 2, :], c[:, 2:3], None, ALU.mult))

                    softmax(0)
                    link(dve.tensor_scalar(v[:, 4, :], v[:, 3, :], float(N), None, ALU.mult))
                    link(dve.reciprocal(v[:, 5, :], v[:, 4, :]))
                    link(dve.tensor_scalar(v[:, 6, :], v[:, 4, :], CAPACITY, None, ALU.is_gt))
                    link(dve.scalar_tensor_tensor(v[:, 5, :], v[:, 5, :], CAPACITY, v[:, 6, :], ALU.mult, ALU.mult))
                    link(dve.tensor_scalar(v[:, 6, :], v[:, 6, :], -1.0, 1.0, ALU.mult, ALU.add))
                    link(dve.tensor_tensor(v[:, 5, :], v[:, 5, :], v[:, 6, :], ALU.add))
                    link(dve.tensor_tensor(v[:, 0, :], v[:, 3, :], v[:, 5, :], ALU.mult))
                    softmax(1)
                    link(dve.max(top[:, :], v[:, 3, :]))
                    link(dve.max_index(which[:, :], top[:, :], v[:, 3, :]))
                    dve.tensor_tensor(c[:, 3:4], top[:, 1:2], top[:, 0:1], ALU.subtract).then_inc(shifted, 1)
                    dve.wait_ge(exped, 3)
                    link(dve.tensor_scalar(c[:, 5:6], c[:, 4:5], 1.0, None, ALU.add))
                    link(dve.reciprocal(w2[:, 0:1], c[:, 5:6]))
                    link(dve.tensor_tensor(w2[:, 1:2], c[:, 4:5], w2[:, 0:1], ALU.mult))

        turn(K, "x1_", K.H, T)
        for i in range(2):
            feed_forward(K, f"x2{i}_", [T], 4, a["L3_ffn_W1"], a["L3_ffn_b1"], a["L3_ffn_W2"], a["L3_ffn_b2"], ACT.Gelu, K.H,
                         factor=w2[:, i:i + 1], chosen=which[0:1, i:i + 1])
    normalise(K, "x3_", K.H, K.H, a["L3_ffn_gamma"], a["L3_ffn_beta"])
    add_into(K, "x4_", K.X, K.H)


def store_result(K, out):
    stored = K.nc.alloc_semaphore("result")
    with K.nc.Block() as block:

        @block.sync
        def _(sp):
            sp.dma_start(nodes(out), K.X[:, :, :]).then_inc(stored, 16)
            sp.wait_ge(stored, 16)


def build(nc, a, out):
    K = Kernel()
    K.nc = nc
    shared(K, lambda name, shape, dt=fp32: nc.dram_tensor(name, shape, dt, kind="Internal").ap())
    constants(K, a)
    sort_edges(K, a)
    indices(K)
    message_layer(K, a)
    top2_layer(K, a)
    attention_layer(K, a)
    switch_layer(K, a)
    gat_layer(K, a)
    depth_layer(K, a)
    conv_layer(K, a)
    mixture_layer(K, a)
    store_result(K, out)


def kernel(**inputs):
    import concourse.bacc as bacc
    from concourse.bass_utils import run_bass_kernel_spmd as run

    nc = bacc.Bacc("TRN2", target_bir_lowering=False, num_devices=1)
    arrays, a = {}, {}
    for name, value in inputs.items():
        if name == "L2_ffn_attention_mask":
            continue
        v = np.ascontiguousarray(value)
        arrays["in_" + name] = v
        a[name] = nc.dram_tensor("in_" + name, v.shape, mybir.dt.from_np(v.dtype), kind="ExternalInput").ap()
    out = nc.dram_tensor("out", (N, D), fp32, kind="ExternalOutput").ap()
    build(nc, a, out)
    return run(nc, [arrays], core_ids=[0]).results[0]["out"]
```

```python
import numpy as np
import concourse.bass as bass
from concourse import mybir
from contextlib import ExitStack

fp32 = mybir.dt.float32
fp32r = mybir.dt.float32r
bf16 = mybir.dt.bfloat16
i32 = mybir.dt.int32
u32 = mybir.dt.uint32
ALU = mybir.AluOpType
ACT = mybir.ActivationFunctionType
AX = mybir.AxisListType

N, D, E = 3125, 256, 50000
NT = 25
P = N // NT
ET = E // P
GT = 4
G = ET // GT
HEADS, DH = 8, 32
RADIX = 64
SORT_TILES = 8
SCAN = 16
FAR = 4096
CHUNK = 5
CW = CHUNK * 128
HW = CW // 2
EPS = 1e-5
FIELD = 32
REC_W = (4, 68)
FLT_MAX = 3.4028234663852886e38


class Link:

    def __init__(self, eng, sem):
        self.eng, self.sem, self.n = eng, sem, 0

    def restart(self):
        self.eng.sem_clear(self.sem)
        self.n = 0

    def __call__(self, ins):
        self.mark(ins)
        self.eng.wait_ge(self.sem, self.n)

    def mark(self, ins):
        self.n += 1
        ins.then_inc(self.sem, 1)


class Stage:

    def __init__(self, K, name):
        self.K, self.name, self.ctx, self.sems, self.held = K, name, ExitStack(), ExitStack(), []
        self.ctx.push(self.give_back)

    def sb(self, name, shape, dt=fp32):
        return self.ctx.enter_context(self.K.nc.sbuf_tensor(self.name + name, shape, dt))

    def ps(self, name, shape, dt=fp32):
        return self.ctx.enter_context(self.K.nc.psum_tensor(self.name + name, shape, dt))

    def sem(self, name):
        self.held.append(self.sems.enter_context(self.K.nc.semaphore(self.name + name)))
        return self.held[-1]

    def indirect(self, name):
        return self.K.nc.alloc_semaphore(self.name + name)

    def link(self, eng, name):
        return Link(eng, self.sem(name))

    def give_back(self, failure, *_):
        if failure:
            return
        with self.K.nc.Block() as block:

            @block.sync
            def _(sp):
                for sem in self.held:
                    sp.sem_clear(sem)

        self.sems.close()


class Kernel:
    pass


def over(ap, shape):
    return ap.to_broadcast(shape)


def await_(eng, sem, value):
    if isinstance(value, int) and value <= 0:
        return
    eng.wait_ge(sem, value)


def hold(K, eng, sem, value):
    if isinstance(value, int) and value <= 0:
        return
    eng.wait_ge(sem, value)
    eng.sem_inc(K.tick)


def skewed(eng, total, phases, peel=0):
    lag_max = max(lag for lag, _ in phases)
    start = 2 * ((lag_max + 3) // 2)
    end = total - total % 2 - 2 * peel
    for t in range(start):
        for lag, fn in phases:
            if t - lag >= 0:
                fn(t - lag, (t - lag) % 2, (t - lag) // 2)
    with eng.Fori(start // 2, end // 2) as i:
        for u in range(2):
            for lag, fn in phases:
                fn(2 * i + (u - lag), (u - lag) % 2, i + (u - lag) // 2)
    for t in range(end, total + lag_max):
        for lag, fn in phases:
            if t - lag < total:
                fn(t - lag, (t - lag) % 2, (t - lag) // 2)


def nodes(ap):
    return ap.rearrange("(p t) w -> p t w", t=NT)


def shared(K, dram):
    nc = K.nc

    def sb(name, shape, dt=fp32):
        return nc.alloc_sbuf_tensor(name, shape, dt)

    K.dram = dram
    K.tick = nc.alloc_semaphore("tick")
    K.X = sb("X", [P, NT, D])
    K.H = sb("H", [P, NT, D])
    K.ident = sb("ident", [128, 128])
    K.identb = sb("identb", [128, 128], bf16)
    K.before = sb("before", [128, 128])
    K.lower = sb("lower", [128, 128])
    K.ones = sb("ones", [128, 128])
    K.ones_r = sb("ones_r", [2, 128], fp32r)
    K.iota64 = sb("iota64", [128, RADIX], bf16)
    K.bounds = dram("bounds", (2, 2, RADIX * RADIX))
    K.idx = [sb(f"idx{k}", [P, ET, 2], i32) for k in range(2)]
    K.fk = [sb(f"fk{k}", [P, ET, 2]) for k in range(2)]
    K.runs_on = [sb(f"runs_on{k}", [128, ET]) for k in range(2)]
    K.starts = [dram(f"starts{k}", (E, 2)) for k in range(2)]
    K.first = [sb(f"first{k}", [P, NT], i32) for k in range(2)]
    K.place_t = sb("place_t", [P, ET], i32)
    K.fields = sb("fields", [P, ET, 4])
    K.at = [sb(f"at{k}", [P, 2, NT], i32) for k in range(2)]
    K.sums = {w: dram(f"sums{w}", (E, w)) for w in (D, D + 1, D + HEADS)}
    K.running = {w: dram(f"running{w}", (ET, w)) for w in (D, D + 1, D + HEADS)}
    K.rec = [dram(f"rec{k}", (E + 1, w)) for k, w in enumerate(REC_W)]


def constants(K, a):
    nc = K.nc
    zeros_done, made, loaded = (nc.alloc_semaphore(x) for x in ("c_zeros", "c_made", "c_x"))
    with nc.Block() as block:

        @block.sync
        def _(sp):
            sp.dma_start(K.X[:, :, :], nodes(a["x"])).then_inc(loaded, 16)
            sp.wait_ge(loaded, 16)

        @block.gpsimd
        def _(pool):
            pool.memset(K.ident[:, :], 0.0).then_inc(zeros_done, 1)
            pool.memset(K.identb[:, :], 0.0).then_inc(zeros_done, 1)
            pool.memset(K.ones[:, :], 1.0).then_inc(zeros_done, 1)
            pool.memset(K.before[:, :], 1.0).then_inc(zeros_done, 1)
            pool.memset(K.lower[:, :], 1.0).then_inc(zeros_done, 1)
            pool.wait_ge(zeros_done, 5)
            for m in (K.ident, K.identb):
                pool.affine_select(out=m[:, :], in_=m[:, :], compare_op=ALU.not_equal, fill=1.0, base=0,
                                   pattern=[[-1, 128]], channel_multiplier=1).then_inc(made, 1)
            pool.affine_select(out=K.before[:, :], in_=K.before[:, :], compare_op=ALU.is_gt, fill=0.0, base=0,
                               pattern=[[1, 128]], channel_multiplier=-1).then_inc(made, 1)
            pool.affine_select(out=K.lower[:, :], in_=K.lower[:, :], compare_op=ALU.is_gt, fill=0.0, base=0,
                               pattern=[[-1, 128]], channel_multiplier=1).then_inc(made, 1)
            pool.iota(K.iota64[:, :], pattern=[[1, RADIX]], base=0, channel_multiplier=0,
                      allow_small_or_imprecise_dtypes=True).then_inc(made, 1)
            pool.tensor_copy(K.ones_r[:, :], K.ones[0:2, :]).then_inc(made, 1)
            pool.wait_ge(made, 6)


def sort_edges(K, a):
    nc = K.nc
    S = Stage(K, "so_")
    B, NB = SORT_TILES, ET // SORT_TILES
    SIDE = [slice(0, RADIX), slice(RADIX, 2 * RADIX)]
    with S.ctx:
        ei = S.sb("ei", [P, 2, ET], i32)
        hl = S.sb("hl", [P, 2, 2, ET], i32)
        digit = S.sb("digit", [P, 2, 2, ET], bf16)
        ef = S.sb("ef", [P, 2, ET])
        ew = S.sb("ew", [P, 2, ET])
        hot = [S.sb(f"hot{i}", [P, 2, B, 2 * RADIX], bf16) for i in range(2)]
        hotT = [S.sb(f"hotT{i}", [128, 2, B, P], bf16) for i in range(2)]
        highf = [S.sb(f"highf{i}", [RADIX, 2, B, P]) for i in range(2)]
        base0 = S.sb("first", [RADIX, 2, RADIX])
        runs = S.sb("runs", [RADIX, 2, RADIX])
        tot = S.sb("tot", [RADIX, 2, RADIX])
        base = [S.sb(f"base{i}", [RADIX, 2, RADIX]) for i in range(2)]
        acc = [S.sb(f"acc{i}", [P, 4, B]) for i in range(2)]
        junk = S.sb("junk", [P, 2, 4, 128])
        zero = S.sb("zero", [P, 128], bf16)
        place = [S.sb(f"place{i}", [P, 1, B], i32) for i in range(2)]
        rec = [S.sb(f"rec{i}", [P, B, REC_W[0]]) for i in range(2)]
        tail = S.sb("tail", [1, 4])
        no_starts = S.sb("no_starts", [P, ET, 2])
        starts_zero = S.sem("sz")
        counts = S.ps("counts", [RADIX, 4, 2 * RADIX])
        transposed = S.ps("tr", [128, 2, B, 128], bf16)
        same = [S.ps(f"same{i}", [P, 2, 256]) for i in range(2)]
        before = [S.ps(f"below{i}", [P, 512]) for i in range(2)]
        loaded, hot_ready, counted, summed = S.sem("ld"), S.sem("hot"), S.sem("cnt"), S.sem("sum")
        tables_ready = S.sem("tables")
        offset_ready, tail_ready, stored = S.sem("offs"), S.sem("tail"), S.sem("st")

        def one_hot(dve, b, slot, k, h):
            return dve.tensor_tensor(
                hot[slot][:, k, :, SIDE[h]],
                over(digit[:, h, k, bass.ds(b * B, B)].unsqueeze(2), [P, B, RADIX]),
                over(K.iota64[0:P, :].unsqueeze(1), [P, B, RADIX]), ALU.is_equal)

        def one_hots(dve, b, slot):
            for h in range(2):
                for k in range(2):
                    ins = one_hot(dve, b, slot, k, h)
            return ins

        with nc.Block() as block:

            @block.sync
            def _(sp):
                for k, n in enumerate(("src", "dst")):
                    sp.dma_start(ei[:, k, :], a[n].rearrange("(p t) -> p t", t=ET)).then_inc(loaded, 16)
                sp.dma_start(ew[:, 0, :], a["edge_weight1"].rearrange("(p t) o -> p (t o)", t=ET)).then_inc(loaded, 16)
                sp.dma_start(ew[:, 1, :], a["edge_weight"].rearrange("(p t) -> p t", t=ET)).then_inc(loaded, 16)
                sp.wait_ge(tail_ready, 1)
                for k in range(2):
                    sp.dma_start(K.rec[k][E:E + 1, 0:4], tail[:, :]).then_inc(stored, 16)
                sp.wait_ge(tables_ready, 1)
                for k in range(2):
                    for c, table in enumerate((base0, tot)):
                        sp.dma_start(K.bounds[k, c, :].rearrange("(h l) -> h l", l=RADIX), table[:, k, :]).then_inc(stored, 16)
                sp.wait_ge(starts_zero, 1)
                for k in range(2):
                    sp.dma_start(K.starts[k].rearrange("(p t) c -> p t c", t=ET), no_starts[:, :, :]).then_inc(stored, 16)
                sp.wait_ge(stored, 128)

            @block.gpsimd
            def _(pool):
                pool.memset(no_starts[:, :, :], 0.0).then_inc(starts_zero, 1)

            @block.vector
            def _(dve):
                link = S.link(dve, "l1")
                dve.memset(tail[:, :], -1.0).then_inc(tail_ready, 1)
                link(dve.memset(zero[:, :], 0.0))
                dve.wait_ge(loaded, 64)
                link(dve.tensor_single_scalar(hl[:, 0, :, :], ei[:, :, :], 6, ALU.logical_shift_right))
                link(dve.tensor_single_scalar(hl[:, 1, :, :], ei[:, :, :], RADIX - 1, ALU.bitwise_and))
                link(dve.tensor_copy(digit[:, :, :, :], hl[:, :, :, :]))
                link(dve.tensor_copy(ef[:, :, :], ei[:, :, :]))
                for c in range(4):
                    ins = dve.tensor_copy(K.fields[:, :, c], ef[:, c, :] if c < 2 else ew[:, 1, :])
                link(ins)

                def hots(b, slot, turn):
                    await_(dve, counted, b - 1)
                    one_hots(dve, b, slot).then_inc(hot_ready, 1)

                skewed(dve, NB, [(0, hots)])
                dve.wait_ge(counted, NB)
                link(dve.tensor_copy(tot[:, :, :], counts[:, 0, :].rearrange("p (k l) -> p k l", k=2)))
                for k in range(2):
                    ins = dve.tensor_tensor_scan(runs[:, k, :], tot[:, k, :], tot[:, k, :], 0.0, ALU.add, ALU.bypass)
                ins.then_inc(summed, 1)
                dve.wait_ge(summed, 1)
                link(dve.tensor_tensor(base0[:, :, :], runs[:, :, :], tot[:, :, :], ALU.subtract))
                dve.wait_ge(offset_ready, 1)
                link(dve.tensor_tensor(base0[:, :, :], base0[:, :, :],
                                       over(counts[:, 1, 0:2].unsqueeze(2), [RADIX, 2, RADIX]), ALU.add))
                dve.tensor_copy(base[0][:, :, :], base0[:, :, :]).then_inc(tables_ready, 1)

            @block.tensor
            def _(pe):
                pe.wait_ge(hot_ready, 1)
                pe.matmul(counts[:, 0, :], zero[:, 0:RADIX], zero[:, :], start=True, stop=True)

                def count(b, slot, turn):
                    pe.wait_ge(hot_ready, b + 1)
                    for j in range(B):
                        for k in range(2):
                            ins = pe.matmul(counts[:, 0, SIDE[k]], hot[slot][:, k, j, SIDE[0]], hot[slot][:, k, j, SIDE[1]],
                                            start=False, stop=True, skip_group_check=True)
                    ins.then_inc(counted, 1)

                skewed(pe, NB, [(0, count)])
                pe.wait_ge(summed, 1)
                pe.matmul(counts[:, 1, 0:2], K.before[0:RADIX, 0:RADIX], runs[:, :, RADIX - 1], start=True, stop=True).then_inc(offset_ready, 1)

        hot_ready, turned, turned_copied = S.sem("hot2"), S.sem("turned"), S.sem("tcopied")
        hist_done, base_ready, found, looked = S.sem("hist"), S.sem("base"), S.sem("found"), S.sem("looked")
        placed = S.sem("placed")
        scattered = [S.indirect(f"scat{i}") for i in range(2)]
        with nc.Block() as block:

            @block.gpsimd
            def _(pool):
                def scatter(b, slot, turn):
                    hold(K, pool, placed, b + 1)
                    for j in range(B):
                        pool.indirect_dma_start(K.rec[0], bass.IndirectOffsetOnAxis(ap=place[slot][:, 0, j:j + 1], axis=0),
                                                rec[slot][:, j, :], None).then_inc(scattered[slot], 16)

                skewed(pool, NB, [(0, scatter)])
                for u in range(2):
                    pool.wait_ge(scattered[u], 16 * B * (NB // 2))

            @block.vector
            def _(dve):
                link = S.link(dve, "l2")

                def next_hots(b, slot, k, h):
                    ins = one_hot(dve, b, slot, k, h)
                    if h == 1:
                        ins.then_inc(hot_ready, 1)

                def places(b, slot, turn):
                    link.restart()
                    for j in range(B):
                        t = b * B + j
                        c = j % 2
                        await_(dve, hist_done, t + 1)
                        await_(dve, found, t)
                        dve.scalar_tensor_tensor(base[1 - c][:, :, :].rearrange("p k l -> p (k l)"), counts[:, 0, :], 1.0,
                                                 base0[:, :, :].rearrange("p k l -> p (k l)"),
                                                 ALU.mult, ALU.add).then_inc(base_ready, 1)
                        dve.wait_ge(found, t + 1)
                        for k in range(2):
                            dve.scalar_tensor_tensor(
                                junk[:, c, k, 0:RADIX], before[c][:, k * RADIX:(k + 1) * RADIX], 1.0, hot[slot][:, k, j, SIDE[1]],
                                ALU.mult, ALU.mult, accum_out=acc[slot][:, k, j:j + 1])
                            ins = dve.scalar_tensor_tensor(
                                junk[:, c, 2 + k, 0:P], same[c][:, k, 0:P], 1.5, K.lower[0:P, 0:P],
                                ALU.is_gt, ALU.mult, accum_out=acc[slot][:, 2 + k, j:j + 1])
                        ins.then_inc(looked, 1)
                        if j < 4 and not (isinstance(b, int) and b == NB - 1):
                            next_hots(b + 1, 1 - slot, j // 2, j % 2)
                    dve.wait_ge(looked, b * B + B)
                    hold(K, dve, scattered[slot], 16 * B * turn)
                    tiles = bass.ds(b * B, B)
                    dve.tensor_tensor(place[slot][:, :, :], acc[slot][:, 0:1, :], acc[slot][:, 2:3, :], ALU.add)
                    dve.tensor_tensor(K.place_t[:, tiles], acc[slot][:, 1, :], acc[slot][:, 3, :], ALU.add)
                    for c in range(2):
                        dve.tensor_copy(rec[slot][:, :, c], ef[:, c, tiles])
                    dve.tensor_copy(rec[slot][:, :, 2], ew[:, 0, tiles])
                    dve.tensor_copy(rec[slot][:, :, 3], ew[:, 0, tiles]).then_inc(placed, 1)

                for k in range(2):
                    for h in range(2):
                        next_hots(0, 0, k, h)
                skewed(dve, NB, [(0, places)], peel=1)

            @block.scalar
            def _(act):
                def copy(b, slot, turn):
                    hold(K, act, found, B * (b - 1))
                    for k in range(2):
                        act.wait_ge(turned, 2 * b + (k + 1))
                        act.activation(hotT[slot][:, k, :, :], transposed[:, k, :, 0:P], ACT.Copy)
                        ins = act.activation(highf[slot][:, k, :, :], transposed[0:RADIX, k, :, 0:P], ACT.Copy)
                    ins.then_inc(turned_copied, 1)

                skewed(act, NB, [(0, copy)])

            @block.tensor
            def _(pe):
                pe.matmul(counts[:, 0, :], zero[:, 0:RADIX], zero[:, :], start=True, stop=True)

                def turn_(b, slot, k):
                    pe.wait_ge(hot_ready, 2 * b + (k + 1))
                    for j in range(B):
                        ins = pe.transpose(transposed[:, k, j, 0:P], hot[slot][:, k, j, :], K.identb[0:P, 0:P])
                    ins.then_inc(turned, 1)

                def look(b, slot, turn):
                    pe.wait_ge(turned_copied, b + 1)
                    for j in range(B):
                        t = b * B + j
                        c = j % 2
                        await_(pe, looked, t - 1)
                        for k in range(2):
                            pe.matmul(same[c][:, k, 0:P], hotT[slot][:, k, j, :], hotT[slot][:, k, j, :], start=True, stop=True)
                        await_(pe, base_ready, t)
                        for k in range(2):
                            ins = pe.matmul(counts[:, 0, SIDE[k]], hot[slot][:, k, j, SIDE[0]], hot[slot][:, k, j, SIDE[1]],
                                            start=False, stop=True, skip_group_check=True)
                        ins.then_inc(hist_done, 1)
                        for k in range(2):
                            ins = pe.matmul(before[c][:, k * RADIX:(k + 1) * RADIX], highf[slot][:, k, j, :], base[c][:, k, :],
                                            start=True, stop=True)
                        ins.then_inc(found, 1)
                        if j in (4, 5) and not (isinstance(b, int) and b == NB - 1):
                            turn_(b + 1, 1 - slot, j - 4)

                for k in range(2):
                    turn_(0, 0, k)
                skewed(pe, NB, [(0, look)], peel=1)


class TargetRecords:

    def __init__(self, K, a, S):
        self.K = K
        self.B, self.NB = SORT_TILES, ET // SORT_TILES
        self.attr = a["edge_attr_64"].rearrange("(p t) w -> p t w", t=ET)
        self.rec = [S.sb(f"trec{i}", [P, self.B, REC_W[1]]) for i in range(2)]
        self.place = [S.sb(f"tplace{i}", [P, self.B], i32) for i in range(2)]
        self.scattered = [S.indirect(f"tscat{i}") for i in range(2)]
        self.attr_in = [S.indirect(f"tattr{i}") for i in range(2)]
        self.begun = S.sem("tbegun")

    def load(self, pool, b, slot, turn):
        hold(self.K, pool, self.scattered[slot], 16 * self.B * turn)
        pool.dma_start(self.rec[slot][:, :, 4:], self.attr[:, bass.ds(b * self.B, self.B), :]).then_inc(self.attr_in[slot], 16)

    def batch(self, pool, b, slot, turn, more=True):
        tiles = bass.ds(b * self.B, self.B)
        pool.tensor_copy(self.rec[slot][:, :, 0:4], self.K.fields[:, tiles, :])
        pool.tensor_copy(self.place[slot][:, :], self.K.place_t[:, tiles]).then_inc(self.begun, 1)
        hold(self.K, pool, self.begun, b + 1)
        hold(self.K, pool, self.attr_in[slot], 16 * turn + 16)
        for j in range(self.B):
            pool.indirect_dma_start(self.K.rec[1], bass.IndirectOffsetOnAxis(ap=self.place[slot][:, j:j + 1], axis=0),
                                    self.rec[slot][:, j, :], None).then_inc(self.scattered[slot], 16)
            if more and j == self.B // 2:
                self.load(pool, b + 1, 1 - slot, turn + slot)

    def first(self, pool, n):
        self.load(pool, 0, 0, 0)
        for b in range(n):
            self.batch(pool, b, b % 2, b // 2)

    def middle(self, pool, half, pairs):
        with pool.Fori(0, pairs) as i:
            for u in range(2):
                self.batch(pool, 2 * (half + i) + u, u, half + i)

    def last(self, pool, n):
        for b in range(self.NB - n, self.NB):
            self.batch(pool, b, b % 2, b // 2, more=b + 1 < self.NB)
        for u in range(2):
            pool.wait_ge(self.scattered[u], 16 * self.B * (self.NB // 2))


def indices(K, side):
    nc = K.nc
    S = Stage(K, f"ix{side}_")
    with S.ctx:
        R = S.sb("R", [P, ET, 4])
        bn = S.sb("bn", [P, 2, NT])
        w = S.sb("w", [P, 6, NT])
        wi = S.sb("wi", [P, NT], i32)
        lastkey = S.sb("lastkey", [128, ET])
        row = S.ps("row", [128, 512])
        loaded, keys_ready, row_ready = S.sem("ld"), S.sem("keys"), S.sem("row")
        with nc.Block() as block:

            @block.sync
            def _(sp):
                sp.dma_start(R[:, :, :], K.rec[side][0:E, 0:4].rearrange("(t p) c -> p t c", p=P)).then_inc(loaded, 16)
                for c in range(2):
                    sp.dma_start(bn[:, c, :], K.bounds[side, c, 0:N].rearrange("(p t) -> p t", t=NT)).then_inc(loaded, 16)

            @block.tensor
            def _(pe):
                pe.wait_ge(keys_ready, 1)
                pe.matmul(row[:, 0:ET], over(K.ident[0:P, P - 1:P], [P, 128]), K.fk[side][:, :, 0], start=True, stop=True).then_inc(row_ready, 1)

            @block.vector
            def _(dve):
                link = S.link(dve, "l")
                dve.wait_ge(loaded, 48)
                dve.tensor_copy(K.fk[side][:, :, 0], R[:, :, side]).then_inc(keys_ready, 1)
                dve.tensor_copy(K.fk[side][:, :, 1], R[:, :, 2])
                dve.tensor_copy(K.idx[side][:, :, :], R[:, :, 0:2])
                begin, count = bn[:, 0, :], bn[:, 1, :]
                last, x, tile, prev, t1, t2 = (w[:, i, :] for i in range(6))
                link(dve.scalar_tensor_tensor(last, begin, -1.0, count, ALU.add, ALU.add))
                link(dve.tensor_scalar(x, last, 0.5, 1.0 / P, ALU.add, ALU.mult))
                link(dve.tensor_copy(wi[:, :], x))
                link(dve.tensor_copy(tile, wi[:, :]))
                link(dve.tensor_tensor(t1, tile, x, ALU.is_gt))
                link(dve.tensor_tensor(tile, tile, t1, ALU.subtract))
                link(dve.tensor_scalar(t2, tile, float(P), None, ALU.mult))
                link(dve.tensor_tensor(t1, begin, t2, ALU.is_ge))
                link(dve.tensor_scalar(t1, t1, float(FAR), -1.0, ALU.mult, ALU.add))
                link(dve.tensor_tensor(prev, tile, t1, ALU.add))
                link(dve.tensor_single_scalar(t2, count, 0.0, ALU.is_equal))
                link(dve.tensor_scalar(t2, t2, float(FAR * 16), None, ALU.mult))
                link(dve.tensor_tensor(last, last, t2, ALU.max))
                link(dve.tensor_tensor(prev, prev, t2, ALU.max))
                dve.tensor_copy(K.at[side][:, 0, :], last)
                dve.tensor_copy(K.at[side][:, 1, :], prev)
                link(dve.tensor_tensor(begin, begin, t2, ALU.max))
                dve.tensor_copy(K.first[side][:, :], begin)
                dve.wait_ge(row_ready, 1)
                link(dve.tensor_copy(lastkey[:, :], row[:, 0:ET]))
                dve.memset(K.runs_on[side][:, 0:1], 0.0)
                link(dve.tensor_tensor(K.runs_on[side][:, 1:ET], lastkey[:, 1:ET], lastkey[:, 0:ET - 1], ALU.is_equal))


def normalise(K, name, src, dst, gamma=None, beta=None):
    nc = K.nc
    S = Stage(K, name)
    with S.ctx:
        bn = S.sb("bn", [P, NT, 6])
        mv = S.sb("mv", [P, NT, 2])
        st = S.sb("st", [P, 2, NT])
        gb = S.sb("gb", [P, 2, D])
        var_ready, root, loaded = S.sem("v"), S.sem("r"), S.sem("ld")
        with nc.Block() as block:

            @block.sync
            def _(sp):
                if gamma is not None:
                    sp.dma_start(gb[:, 0, :], gamma.partition_broadcast(P)).then_inc(loaded, 16)
                    sp.dma_start(gb[:, 1, :], beta.partition_broadcast(P)).then_inc(loaded, 16)

            @block.vector
            def _(dve):
                link = S.link(dve, "l")
                for t in range(NT):
                    ins = dve.bn_stats(bn[:, t, :], src[:, t, :])
                link(ins)
                for t in range(NT):
                    ins = dve.bn_aggr(mv[:, t, :], bn[:, t, :])
                link(ins)
                dve.tensor_scalar(st[:, 0, :], mv[:, :, 1], EPS, None, ALU.add).then_inc(var_ready, 1)
                dve.wait_ge(root, 1)
                link(dve.reciprocal(st[:, 1, :], st[:, 0, :]))
                if gamma is not None:
                    dve.wait_ge(loaded, 32)
                    for t in range(NT):
                        ins = dve.scalar_tensor_tensor(dst[:, t, :], src[:, t, :], mv[:, t, 0:1], gb[:, 0, :], ALU.subtract, ALU.mult)
                    link(ins)
                    for t in range(NT):
                        ins = dve.scalar_tensor_tensor(dst[:, t, :], dst[:, t, :], st[:, 1, t:t + 1], gb[:, 1, :], ALU.mult, ALU.add)
                else:
                    for t in range(NT):
                        ins = dve.tensor_scalar(dst[:, t, :], src[:, t, :], mv[:, t, 0:1], st[:, 1, t:t + 1], ALU.subtract, ALU.mult)
                link(ins)

            @block.scalar
            def _(act):
                act.wait_ge(var_ready, 1)
                act.activation(st[:, 0, :], st[:, 0, :], ACT.Sqrt).then_inc(root, 1)


def transpose_chunk(pe, K, ps, src, c):
    for k in range(2):
        for j in range(CHUNK):
            ins = pe.transpose(ps[:, k * CHUNK + j, 0:P], src[:, c * CHUNK + j, k * 128:(k + 1) * 128], K.ident[0:P, 0:P])
    return ins


def project(K, name, src, weights, biases, tables, score=None, own=None, into=None, head_bias=None):
    nc = K.nc
    S = Stage(K, name)
    M = len(weights)
    BANKS = 5
    CH = NT // CHUNK
    wide = [D] if into is not None else [table.shape[1] for table in tables]
    with S.ctx:
        W = S.sb("W", [128, M, 2, D])
        bias = S.sb("bias", [P, M, D])
        hb = S.sb("hb", [P, DH])
        if score is not None:
            vec = S.sb("vec", [P, 2 * D])
            junk = S.sb("junk", [P, BANKS, 2, D])
        rowsT = [S.sb(f"rowsT{i}", [128, 2 * CHUNK, P]) for i in range(2)]
        res = [] if into is not None else [[S.sb(f"res{i}{m}", [P, CHUNK, wide[m]]) for m in range(M)] for i in range(2)]
        ps = S.ps("ps", [128, 12, 128])
        Y = [S.ps(f"Y{i}", [P, 512]) for i in range(BANKS)]
        loaded, turned, copied, done, ready, ones_set = (S.sem(x) for x in ("ld", "trn", "cpy", "done", "rdy", "ones"))
        stored = [S.sem(f"st{i}") for i in range(2)]
        bias_ready = S.sem("br")
        per_chunk = 16 * M
        loads = 16 * (M + sum(b is not None for b in biases) + (score is not None) + (head_bias is not None))
        with nc.Block() as block:

            @block.sync
            def _(sp):
                for m in range(M):
                    sp.dma_start(W[:, m, :, :], weights[m].rearrange("(k p) n -> p k n", p=128)).then_inc(loaded, 16)
                    if biases[m] is not None:
                        sp.dma_start(bias[:, m, :], biases[m].partition_broadcast(P)).then_inc(loaded, 16)
                if score is not None:
                    sp.dma_start(vec[:, :], score.partition_broadcast(P)).then_inc(loaded, 16)
                if head_bias is not None:
                    sp.dma_start(hb[:, :], head_bias.partition_broadcast(P)).then_inc(loaded, 16)
                for c in range(CH if into is None else 0):
                    tiles = slice(c * CHUNK, (c + 1) * CHUNK)
                    sp.wait_ge(ready, (c + 1) * CHUNK * M)
                    for m in range(M):
                        sp.dma_start(nodes(tables[m])[:, tiles, :], res[c % 2][m][:, :, :]).then_inc(stored[c % 2], 16)
                if into is None:
                    sp.wait_ge(stored[0], per_chunk * (CH - CH // 2))
                    sp.wait_ge(stored[1], per_chunk * (CH // 2))

            @block.gpsimd
            def _(pool):
                for i in range(2 if wide[0] > D else 0):
                    pool.memset(res[i][0][:, :, D:], 1.0).then_inc(ones_set, 1)

            @block.tensor
            def _(pe):
                transpose_chunk(pe, K, ps, src, 0).then_inc(turned, 1)
                pe.wait_ge(loaded, loads)
                for c in range(CH):
                    pe.wait_ge(copied, c + 1)
                    if c + 1 < CH:
                        transpose_chunk(pe, K, ps, src, c + 1).then_inc(turned, 1)
                    for u in range(c * CHUNK * M, (c + 1) * CHUNK * M):
                        j, m = u // M - c * CHUNK, u % M
                        await_(pe, ready, u - BANKS + 1)
                        for k in range(2):
                            ins = pe.matmul(Y[u % BANKS][:, 0:D], rowsT[c % 2][:, k * CHUNK + j, :], W[:, m, k, :], start=(k == 0), stop=(k == 1))
                        ins.then_inc(done, 1)

            @block.scalar
            def _(act):
                for c in range(CH):
                    await_(act, done, (c - 1) * CHUNK * M)
                    act.wait_ge(turned, c + 1)
                    act.activation(rowsT[c % 2][:, :, :], ps[:, 0:2 * CHUNK, 0:P], ACT.Copy).then_inc(copied, 1)

            @block.vector
            def _(dve):
                dve.wait_ge(loaded, loads)
                if wide[0] > D:
                    dve.wait_ge(ones_set, 2)
                if head_bias is not None:
                    by_head = bias[:, 0, :].rearrange("p (h d) -> p h d", d=DH)
                    dve.tensor_tensor(by_head, by_head, over(hb[:, :].unsqueeze(1), [P, HEADS, DH]), ALU.add).then_inc(bias_ready, 1)
                    dve.wait_ge(bias_ready, 1)
                for u in range(NT * M):
                    t, m = u // M, u % M
                    c, j = t // CHUNK, t % CHUNK
                    if into is None and j == 0 and m == 0:
                        await_(dve, stored[c % 2], per_chunk * (c // 2))
                    dve.wait_ge(done, u + 1)
                    y = Y[u % BANKS][:, 0:D]
                    to = into[:, t, :] if into is not None else res[c % 2][m][:, j, 0:D]
                    if biases[m] is None:
                        ins = dve.tensor_copy(to, y)
                    else:
                        ins = dve.tensor_tensor(to, y, bias[:, m, :], ALU.add)
                    if score is not None:
                        dve.scalar_tensor_tensor(junk[:, u % BANKS, 0, :], y, 1.0, vec[:, D:2 * D], ALU.mult, ALU.mult,
                                                 accum_out=res[c % 2][0][:, j, D:D + 1])
                        ins = dve.scalar_tensor_tensor(junk[:, u % BANKS, 1, :], y, 1.0, vec[:, 0:D], ALU.mult, ALU.mult,
                                                       accum_out=own[:, t, 0:1])
                    ins.then_inc(ready, 1)
                dve.wait_ge(ready, NT * M)


MESSAGE, ATTEND, GAT, COPY = range(4)
LAGS = {MESSAGE: (1, 2, 3, 4, 3, 5), ATTEND: (1, 0, 0, 0, 2, 3), GAT: (1, 2, 0, 0, 2, 3), COPY: (1, 0, 0, 0, 2, 3)}


def edge_sums(K, name, kind, side, tables, columns, width, a=None, own=None):
    nc = K.nc
    S = Stage(K, name)
    take_lag, stats_lag, norm_lag, mul_lag, mask_lag, sum_lag = LAGS[kind]
    last = sum_lag
    T = len(tables)
    tw = [t.shape[1] for t in tables]
    with S.ctx:
        at = [S.sb(f"at{i}", [P, GT, 2], i32) for i in range(2)]
        key = [S.sb(f"key{i}", [P, GT, 2]) for i in range(2)]
        got = [[S.sb(f"got{i}{m}", [P, GT, tw[m]]) for m in range(T)] for i in range(2)]
        V = [S.sb(f"V{i}", [P, GT, width]) for i in range(2)]
        same = [S.sb(f"same{i}", [P, GT, P]) for i in range(2)]
        out = [S.sb(f"out{i}", [P, GT, width]) for i in range(2)]
        keys_row = S.ps("keys", [P, GT, 128])
        bank = 512 if width > D else D
        total = S.ps("total", [P, GT, bank])
        at_ready, key_ready, row_ready, mask_ready = S.sem("at"), S.sem("key"), S.sem("row"), S.sem("mask")
        taken, v_ready, summed, out_ready = S.sem("taken"), S.sem("v"), S.sem("sum"), S.sem("out")
        gathered = [S.indirect(f"gat{i}") for i in range(2)]
        stored = [S.sem(f"st{i}") for i in range(2)]
        per_group = 16 * GT * T
        if kind == MESSAGE:
            pre = [S.sb(f"pre{i}", [P, GT, D]) for i in range(2)]
            act1 = [S.sb(f"act{i}", [P, GT, D]) for i in range(2)]
            xn = [S.sb(f"xn{i}", [P, GT, D]) for i in range(2)]
            bn = [S.sb(f"bn{i}", [P, GT, 6]) for i in range(2)]
            mv = [S.sb(f"mv{i}", [P, GT, 2]) for i in range(2)]
            var = [S.sb(f"var{i}", [P, GT]) for i in range(2)]
            rstd = [S.sb(f"rstd{i}", [P, GT]) for i in range(2)]
            minus_half = S.sb("mh", [P, GT])
            wrow = S.sb("wrow", [P, D])
            W2 = S.sb("W2", [128, 2, D])
            gcol = S.sb("gcol", [128, 2, 2])
            b2 = S.sb("b2", [2, 2 * D])
            b2_parts = [S.sb(f"b2{x}", [2, 2 * D], fp32r) for x in "lr"]
            b2_both = S.sb("b2b", [2, 2 * D], fp32r)
            xT = S.sb("xT", [128, 2, GT, P])
            turnedp = S.ps("tp", [128, 2, GT, 128])
            prod = S.ps("prod", [P, GT, D])
            loaded, weights_ready, pre_ready, silu_ready = S.sem("ld"), S.sem("w"), S.sem("pre"), S.sem("silu")
            stats_ready, rstd_ready, norm_ready = S.sem("stats"), S.sem("rstd"), S.sem("norm")
            turned, copied, multiplied, half_set, bias_ready = S.sem("trn"), S.sem("cpy"), S.sem("mul"), S.sem("mh"), S.sem("bias")
        if kind == GAT:
            score = [S.sb(f"score{i}", [P, GT, 2]) for i in range(2)]
            e = [S.sb(f"e{i}", [P, GT]) for i in range(2)]
            score_ready, e_ready, rows_free = S.sem("score"), S.sem("e"), S.sem("free")
        with nc.Block() as block:

            @block.gpsimd
            def _(pool):
                if kind == MESSAGE:
                    pool.memset(minus_half[:, :], -0.5).then_inc(half_set, 1)
                    pool.wait_ge(half_set, 1)

                def gather(g, slot, turn):
                    hold(K, pool, at_ready, g + 1)
                    if kind != GAT:
                        hold(K, pool, taken if kind == MESSAGE else v_ready, g - 1)
                    for j in range(GT):
                        if kind == GAT and j % 2 == 0:
                            hold(K, pool, rows_free, 2 * g + (j // 2 - 3))
                        for m in range(T):
                            c = columns[m]
                            pool.indirect_dma_start(
                                got[slot][m][:, j, :], None, tables[m],
                                bass.IndirectOffsetOnAxis(ap=at[slot][:, j, c:c + 1], axis=0)).then_inc(gathered[slot], 16)

                def power(g, slot, turn):
                    hold(K, pool, stats_ready, g + 1)
                    hold(K, pool, norm_ready, g - 1)
                    pool.tensor_tensor(rstd[slot][:, :], var[slot][:, :], minus_half[:, :], ALU.pow).then_inc(rstd_ready, 1)

                skewed(pool, G, [(0, gather)] + [(stats_lag, power)] * (kind == MESSAGE))

            @block.sync
            def _(sp):
                if kind == MESSAGE:
                    sp.dma_start(wrow[:, :], a["L0_gnn_mW1"][2 * D:2 * D + 1, :].rearrange("o n -> (o n)").partition_broadcast(P)).then_inc(loaded, 16)
                    sp.dma_start(W2[:, :, :], a["L0_gnn_mW2"].rearrange("(k p) n -> p k n", p=128)).then_inc(loaded, 16)
                    sp.dma_start(gcol[:, 0, :], a["L0_gnn_ln_g"].rearrange("(k p) -> p k", p=128), allow_slow_non_contiguous=True).then_inc(loaded, 16)
                    sp.dma_start(gcol[:, 1, :], a["L0_gnn_ln_b"].rearrange("(k p) -> p k", p=128), allow_slow_non_contiguous=True).then_inc(loaded, 16)
                    for h in range(2):
                        sp.dma_start(b2[:, h * D:(h + 1) * D], a["L0_gnn_mb2"].partition_broadcast(2)).then_inc(loaded, 16)

                def store(g, slot, turn):
                    sp.wait_ge(out_ready, g + 1)
                    sp.dma_start(K.sums[width].rearrange("(t p) w -> p t w", p=P)[:, bass.ds(g * GT, GT), :], out[slot][:, :, :]).then_inc(stored[slot], 16)

                skewed(sp, G, [(last, store)])
                for u in range(2):
                    sp.wait_ge(stored[u], 16 * (G // 2))

            @block.vector
            def _(dve):
                link = S.link(dve, "l")
                if kind == MESSAGE:
                    dve.wait_ge(loaded, 96)
                    dve.tensor_copy(xT[:, :, 0, 0:2], over(gcol[:, 1, :].unsqueeze(2), [128, 2, 2])).then_inc(weights_ready, 1)
                    dve.wait_ge(bias_ready, 1)
                    for k in range(2):
                        dve.tensor_scalar(W2[:, k, :], W2[:, k, :], gcol[:, 0, k:k + 1], None, ALU.mult)
                    for h in range(2):
                        ins = dve.tensor_tensor(b2[:, h * D:(h + 1) * D], b2[:, h * D:(h + 1) * D], prod[0:2, 0, :], ALU.add)
                    link(ins)
                    link(dve.tensor_copy(b2_parts[0][:, :], b2[:, :]))
                    link(dve.tensor_tensor(b2_parts[1][:, :], b2[:, :], b2_parts[0][:, :].bitcast(fp32), ALU.subtract))
                    for i in range(2):
                        ins = dve.tensor_scalar(b2_parts[i][:, :], b2_parts[i][:, :].bitcast(fp32), K.ident[0:2, i:i + 1], None, ALU.mult)
                    link(ins)
                    dve.tensor_tensor(b2_both[:, :], b2_parts[0][:, :].bitcast(fp32), b2_parts[1][:, :].bitcast(fp32), ALU.add).then_inc(weights_ready, 1)

                def indices_(g, slot, turn):
                    hold(K, dve, gathered[slot], per_group * turn)
                    dve.tensor_copy(at[slot][:, :, :], K.idx[side][:, bass.ds(g * GT, GT), :]).then_inc(at_ready, 1)

                def take(g, slot, turn):
                    hold(K, dve, mask_ready, g - 1)
                    dve.tensor_copy(key[slot][:, :, :], K.fk[side][:, bass.ds(g * GT, GT), :]).then_inc(key_ready, 1)
                    dve.wait_ge(gathered[slot], per_group * (turn + 1))
                    x = got[slot][0]
                    if kind == MESSAGE:
                        dve.wait_ge(key_ready, g + 1)
                        await_(dve, silu_ready, g - 1)
                        dve.tensor_tensor(pre[slot][:, :, :], x[:, :, :], got[slot][1][:, :, :], ALU.add).then_inc(taken, 1)
                        dve.wait_ge(taken, g + 1)
                        for j in range(GT):
                            ins = dve.scalar_tensor_tensor(pre[slot][:, j, :], wrow[:, :], key[slot][:, j, 1:2],
                                                           pre[slot][:, j, :], ALU.mult, ALU.add)
                        ins.then_inc(pre_ready, 1)
                    if kind == ATTEND:
                        await_(dve, summed, g - 1)
                        for j in range(GT):
                            w = K.scores[:, bass.ds(g * GT + j, 1), :].rearrange("p o h -> p (o h)")
                            dve.tensor_tensor(V[slot][:, j, 0:D].rearrange("p (h d) -> p h d", d=DH),
                                              x[:, j, :].rearrange("p (h d) -> p h d", d=DH),
                                              over(w.unsqueeze(2), [P, HEADS, DH]), ALU.mult)
                        dve.tensor_copy(V[slot][:, :, D:D + HEADS], K.scores[:, bass.ds(g * GT, GT), :]).then_inc(v_ready, 1)
                    if kind == GAT:
                        hold(K, dve, e_ready, g - 1)
                        link.restart()
                        link(dve.tensor_tensor(score[slot][:, :, 0], x[:, :, D], own[:, bass.ds(g * GT, GT)], ALU.add))
                        dve.scalar_tensor_tensor(score[slot][:, :, 1], score[slot][:, :, 0], 0.2, score[slot][:, :, 0],
                                                 ALU.mult, ALU.max).then_inc(score_ready, 1)
                    if kind == COPY:
                        await_(dve, summed, g - 1)
                        dve.tensor_copy(V[slot][:, :, :], x[:, :, :]).then_inc(v_ready, 1)

                def weigh(g, slot, turn):
                    await_(dve, e_ready, g + 1)
                    hold(K, dve, summed, g - 1)
                    for j in range(GT):
                        ins = dve.tensor_scalar(V[slot][:, j, 0:D], got[slot][0][:, j, 0:D], e[slot][:, j:j + 1], None, ALU.mult)
                        if j % 2 == 1:
                            ins.then_inc(rows_free, 1)
                    dve.tensor_copy(V[slot][:, :, D], e[slot][:, :]).then_inc(v_ready, 1)

                def stats(g, slot, turn):
                    hold(K, dve, silu_ready, g + 1)
                    hold(K, dve, rstd_ready, g - 1)
                    hold(K, dve, norm_ready, g - 1)
                    link.restart()
                    for j in range(GT):
                        ins = dve.bn_stats(bn[slot][:, j, :], act1[slot][:, j, :])
                    link(ins)
                    for j in range(GT):
                        ins = dve.bn_aggr(mv[slot][:, j, :], bn[slot][:, j, :])
                    link(ins)
                    dve.tensor_scalar(var[slot][:, :], mv[slot][:, :, 1], EPS, None, ALU.add).then_inc(stats_ready, 1)

                def norm(g, slot, turn):
                    hold(K, dve, rstd_ready, g + 1)
                    hold(K, dve, turned, g - 1)
                    for j in range(GT):
                        ins = dve.tensor_scalar(xn[slot][:, j, :], act1[slot][:, j, :], mv[slot][:, j, 0:1],
                                                rstd[slot][:, j:j + 1], ALU.subtract, ALU.mult)
                    ins.then_inc(norm_ready, 1)

                def mask(g, slot, turn):
                    hold(K, dve, row_ready, g + 1)
                    hold(K, dve, summed, g - 1)
                    dve.tensor_tensor(same[slot][:, :, :], keys_row[:, :, 0:P], over(key[slot][:, :, 0:1], [P, GT, P]),
                                      ALU.is_equal).then_inc(mask_ready, 1)

                ph = [(0, indices_)]
                if kind == MESSAGE:
                    ph += [(norm_lag, norm), (mask_lag, mask), (stats_lag, stats)]
                elif kind == GAT:
                    ph += [(stats_lag, weigh), (mask_lag, mask)]
                else:
                    ph += [(mask_lag, mask)]
                skewed(dve, G, ph + [(take_lag, take)])

            @block.scalar
            def _(act):
                def silu(g, slot, turn):
                    hold(K, act, norm_ready, g - 1)
                    act.wait_ge(pre_ready, g + 1)
                    act.activation(act1[slot][:, :, :], pre[slot][:, :, :], ACT.Silu).then_inc(silu_ready, 1)

                def copy(g, slot, turn):
                    hold(K, act, multiplied, g)
                    act.wait_ge(turned, g + 1)
                    act.activation(xT[:, :, :, :], turnedp[:, :, :, 0:P], ACT.Copy).then_inc(copied, 1)

                def message(g, slot, turn):
                    hold(K, act, summed, g - 1)
                    act.wait_ge(multiplied, g + 1)
                    act.activation(V[slot][:, :, :], prod[:, :, :], ACT.Silu).then_inc(v_ready, 1)

                def exp(g, slot, turn):
                    hold(K, act, v_ready, g - 1)
                    act.wait_ge(score_ready, g + 1)
                    act.activation(e[slot][:, :], score[slot][:, :, 1], ACT.Exp, scale=-1.0).then_inc(e_ready, 1)

                def evacuate(g, slot, turn):
                    hold(K, act, stored[slot], 16 * turn)
                    act.wait_ge(summed, g + 1)
                    act.activation(out[slot][:, :, :], total[:, :, 0:width], ACT.Copy).then_inc(out_ready, 1)

                ph = [(sum_lag, evacuate)]
                if kind == MESSAGE:
                    ph += [(mul_lag, message), (norm_lag, copy), (take_lag, silu)]
                if kind == GAT:
                    ph += [(take_lag, exp)]
                skewed(act, G, ph)

            @block.tensor
            def _(pe):
                if kind == MESSAGE:
                    pe.wait_ge(weights_ready, 1)
                    for k in range(2):
                        ins = pe.matmul(prod[0:2, 0, :], xT[:, k, 0, 0:2], W2[:, k, :], start=(k == 0), stop=(k == 1))
                    ins.then_inc(bias_ready, 1)
                    pe.wait_ge(weights_ready, 2)

                def turn_(g, slot, turn):
                    hold(K, pe, norm_ready, g + 1)
                    hold(K, pe, copied, g)
                    for j in range(GT):
                        for k in range(2):
                            ins = pe.transpose(turnedp[:, k, j, 0:P], xn[slot][:, j, k * 128:(k + 1) * 128], K.ident[0:P, 0:P])
                    ins.then_inc(turned, 1)

                def multiply(g, slot, turn):
                    hold(K, pe, copied, g + 1)
                    hold(K, pe, v_ready, g)
                    for j in range(GT):
                        if j % 2 == 0:
                            pe.matmul(prod[:, j:j + 2, :].rearrange("p j n -> p (j n)"), K.ones_r[:, 0:P], b2_both[:, :], start=True, stop=True)
                        for k in range(2):
                            ins = pe.matmul(prod[:, j, :], xT[:, k, j, :], W2[:, k, :], start=False, stop=True, skip_group_check=True)
                    ins.then_inc(multiplied, 1)

                def row(g, slot, turn):
                    hold(K, pe, key_ready, g + 1)
                    hold(K, pe, mask_ready, g)
                    for j in range(GT):
                        ins = pe.matmul(keys_row[:, j, 0:P], over(key[slot][:, j, 0:1], [P, P]), K.ident[0:P, 0:P], start=True, stop=True)
                    ins.then_inc(row_ready, 1)

                def add_up(g, slot, turn):
                    hold(K, pe, v_ready, g + 1)
                    hold(K, pe, mask_ready, g + 1)
                    hold(K, pe, out_ready, g)
                    for j in range(GT):
                        ins = pe.matmul(total[:, j, 0:width], same[slot][:, j, :], V[slot][:, j, :], start=True, stop=True)
                    ins.then_inc(summed, 1)

                ph = [(sum_lag, add_up)]
                if kind == MESSAGE:
                    ph += [(mul_lag, multiply), (norm_lag, turn_)]
                skewed(pe, G, ph + [(mask_lag - 1, row)])


def spread(K, name, side, by_node, by_edge):
    nc = K.nc
    S = Stage(K, name)
    R, Q = 100, ET // 100
    edges = K.dram(name + "edges", (E,))
    with S.ctx:
        at_start = S.sb("at_start", [P, ET, 2])
        on = S.sb("on", [P, ET])
        zero = S.sb("zero", [P, ET])
        value = S.sb("value", [P, ET])
        whole = S.sb("whole", [P, ET])
        ends = S.sb("ends", [1, 2, P])
        into = S.sb("into", [1, P])
        back = S.sb("back", [P, 1])
        tiles = S.sb("tiles", [R, Q, P])
        rows = S.ps("rows", [128, 512])
        T = S.ps("T", [P, 512])
        one_set, numbers_in, values_ready, rows_ready = (S.sem(x) for x in ("o", "n", "v", "r"))
        into_ready, back_ready, spread_out, stored = (S.sem(x) for x in ("i", "b", "so", "st"))
        tiles_in, turned = S.sem("ti"), S.sem("t")
        scattered = S.indirect("sc")
        with nc.Block() as block:

            @block.vector
            def _(dve):
                link = S.link(dve, "l")
                dve.memset(by_node[:, :, 1:2], 1.0).then_inc(one_set, 1)
                dve.memset(zero[:, :], 0.0)
                link(dve.memset(into[:, :], 0.0))
                dve.wait_ge(numbers_in, 16)
                link(dve.tensor_scalar(on[:, :], at_start[:, :, 1], -1.0, 1.0, ALU.mult, ALU.add))
                dve.tensor_tensor_scan(value[:, :], on[:, :], at_start[:, :, 0], 0.0, ALU.mult, ALU.add)
                dve.tensor_tensor_scan(whole[:, :], on[:, :], zero[:, :], 1.0, ALU.mult, ALU.add).then_inc(values_ready, 1)
                dve.wait_ge(rows_ready, 1)
                link(dve.tensor_copy(ends[:, :, :], rows[0:1, 0:2 * P].rearrange("o (i p) -> o i p", i=2)))
                dve.tensor_tensor_scan(into[:, 1:P], ends[:, 1, 0:P - 1], ends[:, 0, 0:P - 1], 0.0, ALU.mult, ALU.add).then_inc(into_ready, 1)
                dve.wait_ge(back_ready, 1)
                link(dve.tensor_copy(back[:, :], rows[0:P, 256:257]))
                dve.scalar_tensor_tensor(value[:, :], whole[:, :], back[:, 0:1], value[:, :], ALU.mult, ALU.add).then_inc(spread_out, 1)
                dve.wait_ge(turned, 1)
                link(dve.tensor_copy(by_edge[:, :], T[:, 0:ET]))

            @block.gpsimd
            def _(pool):
                pool.wait_ge(one_set, 1)
                for t in range(NT):
                    pool.indirect_dma_start(K.starts[side], bass.IndirectOffsetOnAxis(ap=K.first[side][:, t:t + 1], axis=0), by_node[:, t, :], None,
                                            bounds_check=E - 1, oob_is_err=False).then_inc(scattered, 16)

            @block.sync
            def _(sp):
                sp.wait_ge(scattered, 16 * NT)
                sp.dma_start(at_start[:, :, :], K.starts[side].rearrange("(p t) c -> p t c", t=ET)).then_inc(numbers_in, 16)
                sp.wait_ge(spread_out, 1)
                sp.dma_start(edges.rearrange("(p t) -> p t", t=ET), value[:, :]).then_inc(stored, 16)
                sp.wait_ge(stored, 16)
                sp.dma_start(tiles[:, :, :], edges.rearrange("(q r p) -> r q p", r=R, p=P)).then_inc(tiles_in, 16)

            @block.tensor
            def _(pe):
                pe.wait_ge(values_ready, 1)
                for i, x in enumerate((value, whole)):
                    ins = pe.matmul(rows[0:1, i * P:(i + 1) * P], x[:, ET - 1:ET], K.ident[0:P, 0:P], start=True, stop=True)
                ins.then_inc(rows_ready, 1)
                pe.wait_ge(into_ready, 1)
                pe.matmul(rows[0:P, 256:257], into[0:1, :], K.ones[0:1, 0:1], start=True, stop=True).then_inc(back_ready, 1)
                pe.wait_ge(tiles_in, 16)
                for q in range(Q):
                    ins = pe.transpose(T[:, q * R:(q + 1) * R], tiles[:, q, :], K.ident[0:R, 0:R])
                ins.then_inc(turned, 1)


def collect(K, name, side, width, dst):
    nc = K.nc
    S = Stage(K, name)
    parts = [(c, min(128, width - c)) for c in range(0, width, 128)]
    R, Q = 100, ET // 100
    with S.ctx:
        carry = S.sb("carry", [P, NT, width])
        ends = S.sb("ends", [R, Q, width])
        endsT = S.sb("endsT", [128, len(parts), ET])
        runs = S.sb("runs", [128, len(parts), ET])
        back = S.sb("back", [R, Q, width])
        T = S.ps("T", [128, len(parts), 512])
        B = S.ps("B", [R, Q, 512])
        loaded, zeroed, turned, copied, scanned = (S.sem(x) for x in ("ld", "z", "t", "c", "s"))
        returned, back_ready, stored, done = (S.sem(x) for x in ("r", "b", "st", "d"))
        gathered = S.indirect("g")
        with nc.Block() as block:

            @block.sync
            def _(sp):
                rows = K.sums[width].rearrange("(t p) w -> p t w", p=P)[P - 1, :, :]
                sp.dma_start(ends[:, :, :], rows.rearrange("(q r) w -> r q w", r=R)).then_inc(loaded, 16)
                sp.wait_ge(back_ready, 1)
                sp.dma_start(K.running[width].rearrange("(q r) w -> r q w", r=R), back[:, :, :]).then_inc(stored, 16)
                sp.wait_ge(stored, 16)

            @block.gpsimd
            def _(pool):
                for table, i, to in ((K.sums[width], 0, dst), (K.running[width], 1, carry)):
                    if i == 1:
                        pool.wait_ge(zeroed, 3)
                        pool.wait_ge(stored, 16)
                    for t in range(NT):
                        if i == 0 and t in (0, CHUNK):
                            pool.wait_ge(zeroed, 1 + t // CHUNK)
                        pool.indirect_dma_start(to[:, t, 0:width], None, table,
                                                bass.IndirectOffsetOnAxis(ap=K.at[side][:, i, t:t + 1], axis=0),
                                                bounds_check=(E - 1, ET - 1)[i], oob_is_err=False).then_inc(gathered, 16)

            @block.tensor
            def _(pe):
                pe.wait_ge(loaded, 16)
                for i, (c, n) in enumerate(parts):
                    for q in range(Q):
                        ins = pe.transpose(T[0:n, i, q * R:(q + 1) * R], ends[:, q, c:c + n], K.ident[0:R, 0:R])
                ins.then_inc(turned, 1)
                pe.wait_ge(scanned, 1)
                for i, (c, n) in enumerate(parts):
                    for q in range(Q):
                        ins = pe.transpose(B[:, q, c:c + n], runs[0:n, i, q * R:(q + 1) * R], K.ident[0:n, 0:n])
                ins.then_inc(returned, 1)

            @block.scalar
            def _(act):
                act.wait_ge(turned, 1)
                for i, (c, n) in enumerate(parts):
                    ins = act.activation(endsT[0:n, i, :], T[0:n, i, 0:ET], ACT.Copy)
                ins.then_inc(copied, 1)
                act.wait_ge(returned, 1)
                act.activation(back[:, :, :], B[:, :, 0:width], ACT.Copy).then_inc(back_ready, 1)

            @block.vector
            def _(dve):
                dve.memset(dst[:, 0:CHUNK, 0:width], 0.0).then_inc(zeroed, 1)
                dve.memset(dst[:, CHUNK:NT, 0:width], 0.0).then_inc(zeroed, 1)
                dve.memset(carry[:, :, :], 0.0).then_inc(zeroed, 1)
                dve.wait_ge(copied, 1)
                for i, (c, n) in enumerate(parts):
                    ins = dve.tensor_tensor_scan(runs[0:n, i, :], K.runs_on[side][0:n, :], endsT[0:n, i, :], 0.0, ALU.mult, ALU.add)
                ins.then_inc(scanned, 1)
                dve.wait_ge(gathered, 32 * NT)
                dve.tensor_tensor(dst[:, :, 0:width], dst[:, :, 0:width], carry[:, :, :], ALU.add).then_inc(done, 1)
                dve.wait_ge(done, 1)



def turn(K, name, src, T, gate=None):
    nc = K.nc
    S = Stage(K, name)
    W_, b_, n, gout = gate if gate is not None else (None, None, 1, None)
    CH = NT // CHUNK
    with S.ctx:
        W = S.sb("W", [128, 2, n])
        bias = S.sb("bias", [P, n])
        rowsT = [S.sb(f"rowsT{i}", [128, 2 * CHUNK, P]) for i in range(2)]
        ps = [S.ps(f"ps{i}", [128, 12, 128]) for i in range(2)]
        Y = [S.ps(f"Y{i}", [P, 512]) for i in range(2)]
        zeros = S.sb("zeros", [128, 128])
        loaded, turned, copied, kept, done, ready, zeroed = (S.sem(x) for x in ("ld", "trn", "cpy", "kept", "done", "rdy", "z"))

        def columns(part, c):
            return part[:, :, c * CW:(c + 1) * CW].rearrange("q k (j p) -> q k j p", p=128)[:, :, :, 0:P]

        with nc.Block() as block:

            @block.sync
            def _(sp):
                if gate is not None:
                    sp.dma_start(W[:, :, :], W_.rearrange("(k p) n -> p k n", p=128), allow_slow_non_contiguous=True).then_inc(loaded, 16)
                    sp.dma_start(bias[:, :], b_.partition_broadcast(P)).then_inc(loaded, 16)

            @block.gpsimd
            def _(pool):
                pool.memset(zeros[:, :], 0.0).then_inc(zeroed, 1)
                pool.wait_ge(zeroed, 1)
                for part in () if T is None else T if isinstance(T, tuple) else (T,):
                    for k in range(2):
                        pool.tensor_copy(part[:, k, :].rearrange("q (t p) -> q t p", p=128)[:, :, P:128],
                                         over(zeros[:, 0:128 - P].unsqueeze(1), [128, NT, 128 - P]))

            @block.tensor
            def _(pe):
                def multiply(c):
                    pe.wait_ge(copied, c + 1)
                    await_(pe, ready, c - 1)
                    for j in range(CHUNK):
                        for k in range(2):
                            ins = pe.matmul(Y[c % 2][:, j * n:(j + 1) * n], rowsT[c % 2][:, k * CHUNK + j, :], W[:, k, :], start=(k == 0), stop=(k == 1))
                    ins.then_inc(done, 1)

                for c in range(CH):
                    await_(pe, kept, c - 1)
                    transpose_chunk(pe, K, ps[c % 2], src, c).then_inc(turned, 1)
                    if gate is not None:
                        if c == 0:
                            pe.wait_ge(loaded, 32)
                        else:
                            multiply(c - 1)
                if gate is not None:
                    multiply(CH - 1)

            @block.scalar
            def _(act):
                for c in range(CH):
                    got = ps[c % 2][:, 0:2 * CHUNK, 0:P]
                    act.wait_ge(turned, c + 1)
                    if T is not None:
                        part = T[0] if isinstance(T, tuple) else T
                        ins = act.activation(columns(part, c), got.rearrange("q (k j) p -> q k j p", k=2), ACT.Copy)
                    if gate is not None:
                        await_(act, done, c - 1)
                        ins = act.activation(rowsT[c % 2][:, :, :], got, ACT.Copy)
                    ins.then_inc(copied, 1)

            @block.vector
            def _(dve):
                def finish(c):
                    dve.wait_ge(done, c + 1)
                    dve.tensor_tensor(gout[:, c * CHUNK:(c + 1) * CHUNK, 0:n], Y[c % 2][:, 0:CHUNK * n].rearrange("p (j n) -> p j n", n=n),
                                      over(bias[:, :].unsqueeze(1), [P, CHUNK, n]), ALU.add).then_inc(ready, 1)

                if gate is not None:
                    dve.wait_ge(loaded, 32)
                for c in range(CH):
                    dve.wait_ge(copied, c + 1)
                    if isinstance(T, tuple):
                        got = ps[c % 2][:, 0:2 * CHUNK, 0:P].rearrange("q (k j) p -> q k j p", k=2)
                        dve.tensor_tensor(columns(T[1], c), got, columns(T[0], c).bitcast(fp32), ALU.subtract).then_inc(kept, 1)
                    else:
                        dve.sem_inc(kept, 1)
                    if gate is not None and c > 0:
                        finish(c - 1)
                if gate is not None:
                    finish(CH - 1)
                    dve.wait_ge(ready, CH)


def feed_forward(K, name, ins, F, W1, b1, W2, b2, func, dst, experts=1, by_tile=None, factor=None,
                 chosen=None, records=None):
    nc = K.nc
    S = Stage(K, name)
    KC = 2 * len(ins)
    ES = 2 if experts > 1 else 1
    H = F * 128
    CH = NT // CHUNK
    split = isinstance(ins[0], tuple)
    LOAD = 80
    with S.ctx:
        raw = 1 if split else ES
        w1 = [S.sb(f"w1{i}", [128, KC, H]) for i in range(raw)] * (ES // raw)
        c1 = [S.sb(f"c1{i}", [128, F]) for i in range(ES)]
        w2 = [S.sb(f"w2{i}", [128, F, D]) for i in range(raw)] * (ES // raw)
        c2 = [S.sb(f"c2{i}", [2, 2 * D]) for i in range(raw)] * (ES // raw)
        hid = [S.sb(f"hid{i}", [128, CW]) for i in range(2)]
        if split:
            w1_parts = [[S.sb(f"w1{x}{i}", [128, KC, H], fp32r) for x in "lr"] for i in range(ES)]
            w2_parts = [[S.sb(f"w2{x}{i}", [128, F, D], fp32r) for x in "lr"] for i in range(ES)]
            hid_parts = [[S.sb(f"hid{x}{i}", [128, CW], fp32r) for x in "lr"] for i in range(2)]
            c2_parts = [S.sb(f"c2{x}", [2, 2 * D], fp32r) for x in "lr"]
            c2_both = [S.sb(f"c2b{i}", [2, 2 * D], fp32r) for i in range(ES)]
        side_work = TargetRecords(K, records, S) if records is not None else None
        wt = [S.sb(f"wt{i}", [P, CHUNK]) for i in range(2)]
        hp = [S.ps(f"hp{i}", [128, 2, 512]) for i in range(2)]
        y = S.ps("y", [P, 6, D])
        loaded = [S.sem(f"ld{i}") for i in range(ES)]
        h_done, h_used, y_done, added, h_split, first_split, w_split = (S.sem(x) for x in ("hd", "hu", "yd", "add", "hs", "fs", "ws"))

        def units(eng, step, rest):
            def expert(e, slot, turn, before):
                step((e, slot, turn, 0, e * CH), before)
                with eng.Fori(1, CH) as c:
                    step((e, slot, turn, c, e * CH + c), (e, slot, turn, c - 1, e * CH + (c - 1)))
                return e, slot, turn, CH - 1, e * CH + (CH - 1)

            last = expert(0, 0, 0, None)
            if experts > 1:
                expert(1, 1, 0, last)
                with eng.Fori(1, experts // 2) as e2:
                    last = expert(2 * e2, 0, e2, (2 * e2 - 1, 1, e2 - 1, CH - 1, 2 * e2 * CH - 1))
                    expert(2 * e2 + 1, 1, e2, last)
                last = (experts - 1, 1, experts // 2 - 1, CH - 1, experts * CH - 1)
            rest(last)

        def split_(eng, link, whole, parts):
            lead, rest = parts
            link(eng.tensor_copy(lead[:], whole[:]))
            return eng.tensor_tensor(rest[:], whole[:], lead[:].bitcast(fp32), ALU.subtract)

        def split_weights(eng, link, e, slot, turn, told):
            link.restart()
            hold(K, eng, loaded[slot], LOAD * (turn + 1))
            split_(eng, link, w1[slot], w1_parts[slot])
            split_(eng, link, w2[slot], w2_parts[slot])
            link(split_(eng, link, c2[slot], c2_parts))
            for i in range(2):
                ins = eng.tensor_scalar(c2_parts[i][:, :], c2_parts[i][:, :].bitcast(fp32), K.ident[0:2, i:i + 1], None, ALU.mult)
            link(ins)
            eng.tensor_tensor(c2_both[slot][:, :], c2_parts[0][:, :].bitcast(fp32), c2_parts[1][:, :].bitcast(fp32), ALU.add).then_inc(told, 1)

        def pick(ap, e):
            return ap if experts == 1 and chosen is None else ap[bass.ds(e, 1)].rearrange("o a b -> (o a) b") if len(ap.shape) == 3 else ap[bass.ds(e, 1), :].rearrange("o b -> (o b)")

        with nc.Block() as block:

            @block.sync
            def _(sp):
                def load(e, slot):
                    sp.dma_start(w1[slot][:, :, :], pick(W1, e).rearrange("(k p) f -> p k f", p=128)).then_inc(loaded[slot], 16)
                    sp.dma_start(c1[slot][:, :], pick(b1, e).rearrange("(f p) -> p f", p=128), allow_slow_non_contiguous=True).then_inc(loaded[slot], 16)
                    sp.dma_start(w2[slot][:, :, :], pick(W2, e).rearrange("(f p) n -> p f n", p=128)).then_inc(loaded[slot], 16)
                    for h in range(2):
                        sp.dma_start(c2[slot][:, h * D:(h + 1) * D], pick(b2, e).partition_broadcast(2)).then_inc(loaded[slot], 16)

                if chosen is not None:
                    load(sp.value_load(chosen, min_val=0, max_val=7), 0)
                elif experts == 1:
                    load(0, 0)
                else:
                    load(0, 0)
                    if split:
                        sp.wait_ge(first_split, 1)
                    load(1, 1)
                    with sp.Fori(1, experts // 2) as e2:
                        for u in range(2):
                            sp.wait_ge(y_done, (2 * e2 + (u - 1)) * (CH * F) + 2)
                            if split:
                                sp.wait_ge(w_split, 2 * e2 + (u - 1))
                            load(2 * e2 + u, u)

            @block.gpsimd
            def _(pool):
                if split and experts > 1:
                    link = S.link(pool, "wl")
                    each = 3 * (experts - 2)
                    if side_work is not None:
                        ends = side_work.NB // 2 - each
                        begin = 2 * ends - 2
                    split_weights(pool, link, 1, 1, 0, w_split)
                    if side_work is not None:
                        side_work.first(pool, begin)
                    with pool.Fori(1, experts // 2) as e2:
                        for u in range(2):
                            split_weights(pool, link, 2 * e2 + u, u, e2, w_split)
                            if side_work is not None:
                                side_work.middle(pool, 6 * e2 + (3 * u - 6 + begin // 2), 3)
                    if side_work is not None:
                        side_work.last(pool, 2 * ends - begin)

            @block.tensor
            def _(pe):
                pe.sem_inc(y_done, 2)

                def hidden(unit, f):
                    e, slot, turn, c, n = unit
                    if f == 0 and split:
                        if isinstance(e, int) and e == 0:
                            hold(K, pe, first_split, 1)
                        else:
                            hold(K, pe, w_split, e)
                    elif f == 0:
                        hold(K, pe, loaded[slot], LOAD * (turn + 1))
                    cols = c * CW
                    hold(K, pe, h_used, n * F + (f + 1))
                    at = slice(f * 128, (f + 1) * 128)
                    for half in range(2):
                        of = bass.ds(cols + half * HW, HW)
                        pairs = []
                        for k in range(KC):
                            if split:
                                lead, rest = (part[:, k % 2, of] for part in ins[k // 2])
                                w_lead, w_rest = (part[:, k, at] for part in w1_parts[slot])
                                pairs += [(w_lead, lead), (w_lead, rest), (w_rest, lead)]
                            else:
                                pairs += [(w1[slot][:, k, at], ins[k // 2][:, k % 2, of])]
                        for i, (w, x) in enumerate(pairs):
                            ins_ = pe.matmul(hp[f % 2][:, half, 0:HW], w, x, start=(i == 0), stop=(i == len(pairs) - 1))
                    ins_.then_inc(h_done, 1)

                def outward(unit, f):
                    e, slot, turn, c, n = unit
                    if split:
                        pe.wait_ge(h_split, n * F + (f + 1))
                    else:
                        pe.wait_ge(h_used, n * F + (f + 3))
                    if f == 0:
                        hold(K, pe, added, n + 1)
                        for b in range(3):
                            w = min(2, CHUNK - 2 * b)
                            one, bias = (K.ones_r[:, 0:P], c2_both[slot]) if split else (K.ones[0:1, 0:P], c2[slot][0:1, :])
                            pe.matmul(y[:, 2 * b:2 * b + w, :].rearrange("p j n -> p (j n)"), one,
                                      bias[:, 0:w * D], start=True, stop=True)
                    for t in range(CHUNK):
                        at = slice(t * 128, t * 128 + P)
                        if split:
                            lead, rest = (part[:, at] for part in hid_parts[f % 2])
                            w_lead, w_rest = (part[:, f, :] for part in w2_parts[slot])
                            pairs = [(lead, w_lead), (lead, w_rest), (rest, w_lead)]
                        else:
                            pairs = [(hid[f % 2][:, at], w2[slot][:, f, :])]
                        for x, w in pairs:
                            ins_ = pe.matmul(y[:, t, :], x, w, start=False, stop=True, skip_group_check=True)
                    ins_.then_inc(y_done, 1)

                def step(unit, before):
                    hidden(unit, 0)
                    if before is not None:
                        outward(before, F - 1)
                    for f in range(1, F):
                        hidden(unit, f)
                        outward(unit, f - 1)

                units(pe, step, lambda last: outward(last, F - 1))

            @block.scalar
            def _(act):
                act.sem_inc(h_used, 2)

                def step(unit, before):
                    e, slot, turn, c, n = unit
                    hold(K, act, loaded[slot], LOAD * (turn + 1))
                    for f in range(F):
                        hold(K, act, y_done, n * F + (f + 1))
                        act.wait_ge(h_done, n * F + (f + 1))
                        act.activation(hid[f % 2][:, :].rearrange("p (h w) -> p h w", h=2), hp[f % 2][:, :, 0:HW], func,
                                       bias=c1[slot][:, f:f + 1]).then_inc(h_used, 1)

                units(act, step, lambda last: None)

            @block.vector
            def _(dve):
                dve.sem_inc(added, 1)
                link = S.link(dve, "l")

                if split:
                    split_weights(dve, link, 0, 0, 0, first_split)

                def prepare(unit):
                    e, slot, turn, c, n = unit
                    hold(K, dve, added, n + 1)
                    if by_tile is not None:
                        link(dve.tensor_copy(wt[0][:, :], by_tile[:, bass.ds(c * CHUNK, CHUNK), bass.ds(e, 1)].rearrange("p t o -> p (t o)")))

                def finish(unit):
                    e, slot, turn, c, n = unit
                    hold(K, dve, y_done, (n + 1) * F + 2)
                    to = dst[:, bass.ds(c * CHUNK, CHUNK), :]
                    if by_tile is not None:
                        for t in range(CHUNK):
                            to = dst[:, bass.ds(c * CHUNK + t, 1), :].rearrange("p o w -> p (o w)")
                            ins_ = dve.scalar_tensor_tensor(to, y[:, t, :], wt[0][:, t:t + 1], to, ALU.mult, ALU.add)
                    elif factor is not None:
                        ins_ = dve.scalar_tensor_tensor(to, y[:, 0:CHUNK, :], factor[:, 0:1], to, ALU.mult, ALU.add)
                    else:
                        ins_ = dve.tensor_tensor(to, y[:, 0:CHUNK, :], to, ALU.add)
                    ins_.then_inc(added, 1)

                def last_unit(unit):
                    prepare(unit)
                    finish(unit)

                def step(unit, before):
                    link.restart()
                    if before is not None:
                        prepare(before)
                    for f in range(F):
                        if split:
                            hold(K, dve, h_used, unit[4] * F + (f + 3))
                            split_(dve, link, hid[f % 2], hid_parts[f % 2]).then_inc(h_split, 1)
                        if f == 0 and before is not None:
                            finish(before)

                units(dve, step, last_unit)


def add_into(K, name, dst, src):
    S = Stage(K, name)
    with S.ctx:
        done = S.sem("done")
        with K.nc.Block() as block:

            @block.vector
            def _(dve):
                dve.tensor_tensor(dst[:, :, :], dst[:, :, :], src[:, :, 0:D], ALU.add).then_inc(done, 1)
                dve.wait_ge(done, 1)


def message_layer(K, a):
    nc = K.nc
    A, B = K.dram("mA", (N, D)), K.dram("mB", (N, D))
    normalise(K, "m0_", K.X, K.H)
    W = a["L0_gnn_mW1"]
    project(K, "m1_", K.H, [W[0:D, :], W[D:2 * D, :]], [None, a["L0_gnn_mb1"]], [A, B])
    edge_sums(K, "m2_", MESSAGE, 0, [A, B], [0, 1], D, a)
    S = Stage(K, "m3_")
    with S.ctx:
        agg = S.sb("agg", [P, NT, D])
        T = [S.sb(f"T{i}", [128, 2, NT * 128]) for i in range(2)]
        collect(K, "m4_", 0, D, agg)
        turn(K, "m5_", K.H, T[0])
        turn(K, "m6_", agg, T[1])
        add_into(K, "m7_", K.X, K.H)
        feed_forward(K, "m8_", T, 2, a["L0_gnn_uW1"], a["L0_gnn_ub1"], a["L0_gnn_uW2"], a["L0_gnn_ub2"], ACT.Silu, K.X)


def top2_layer(K, a):
    nc = K.nc
    normalise(K, "t0_", K.X, K.H)
    normalise(K, "t1_", K.H, K.H, a["L0_ffn_gamma"], a["L0_ffn_beta"])
    S = Stage(K, "t_")
    with S.ctx:
        T = tuple(S.sb(f"T{i}", [128, 2, NT * 128], fp32r) for i in range(2))
        logit = S.sb("logit", [P, NT, 8])
        top = S.sb("top", [P, NT, 8])
        which = S.sb("which", [P, NT, 8], u32)
        whichf = S.sb("whichf", [P, NT, 2])
        w = S.sb("w", [P, 4, NT])
        a2 = S.sb("a2", [P, NT, 8])
        wts = S.sb("wts", [P, NT, 8])
        turn(K, "t2_", K.H, T, gate=(a["L0_ffn_Wr"], a["L0_ffn_br"], 8, logit))
        diff, exped = S.sem("diff"), S.sem("exp")
        with nc.Block() as block:

            @block.vector
            def _(dve):
                link = S.link(dve, "l")
                for t in range(NT):
                    link.mark(dve.max(top[:, t, :], logit[:, t, :]))
                dve.wait_ge(link.sem, link.n)
                for t in range(NT):
                    ins = dve.max_index(which[:, t, :], top[:, t, :], logit[:, t, :])
                link(ins)
                link(dve.tensor_copy(whichf[:, :, :], which[:, :, 0:2]))
                dve.tensor_tensor(w[:, 0, :], top[:, :, 1], top[:, :, 0], ALU.subtract).then_inc(diff, 1)
                dve.wait_ge(exped, 1)
                link(dve.tensor_scalar(w[:, 2, :], w[:, 1, :], 1.0, None, ALU.add))
                link(dve.reciprocal(w[:, 2, :], w[:, 2, :]))
                link(dve.tensor_tensor(w[:, 3, :], w[:, 1, :], w[:, 2, :], ALU.mult))
                wide = [P, NT, 8]
                link(dve.tensor_tensor(wts[:, :, :], over(K.iota64[0:P, 0:8].unsqueeze(1), wide), over(whichf[:, :, 0:1], wide), ALU.is_equal))
                link(dve.tensor_tensor(wts[:, :, :], wts[:, :, :], over(w[:, 2, :].unsqueeze(2), wide), ALU.mult))
                link(dve.tensor_tensor(a2[:, :, :], over(K.iota64[0:P, 0:8].unsqueeze(1), wide), over(whichf[:, :, 1:2], wide), ALU.is_equal))
                link(dve.tensor_tensor(a2[:, :, :], a2[:, :, :], over(w[:, 3, :].unsqueeze(2), wide), ALU.mult))
                link(dve.tensor_tensor(wts[:, :, :], wts[:, :, :], a2[:, :, :], ALU.add))

            @block.scalar
            def _(act):
                act.wait_ge(diff, 1)
                act.activation(w[:, 1, :], w[:, 0, :], ACT.Exp).then_inc(exped, 1)

        feed_forward(K, "t3_", [T], 4, a["L0_ffn_W1"], a["L0_ffn_b1"], a["L0_ffn_W2"], a["L0_ffn_b2"], ACT.Gelu, K.X,
                     experts=8, by_tile=wts, records=a)


def pack(K, name, side, src, by_node, packed):
    nc = K.nc
    S = Stage(K, name)
    rows = K.dram(name + "rows", (N, D))
    with S.ctx:
        count = S.sb("count", [P, NT])
        has = S.sb("has", [P, NT])
        incl = S.sb("incl", [P, NT])
        rank = S.sb("rank", [P, NT])
        far = S.sb("far", [P, NT])
        zeros = S.sb("zeros", [P, CHUNK, D])
        to = S.sb("to", [P, NT], i32)
        earlier = S.ps("earlier", [P, 512])
        loaded, counted, summed, to_ready, zeroed, cleared, in_ = (S.sem(x) for x in ("ld", "c", "s", "to", "z", "cl", "in"))
        scattered = S.indirect("sc")
        with nc.Block() as block:

            @block.sync
            def _(sp):
                sp.dma_start(count[:, :], K.bounds[side, 1, 0:N].rearrange("(p t) -> p t", t=NT)).then_inc(loaded, 16)
                sp.wait_ge(zeroed, 1)
                for b in range(0, NT, CHUNK):
                    sp.dma_start(rows.rearrange("(b r) n -> r b n", r=P)[:, b:b + CHUNK, :], zeros[:, :, :]).then_inc(cleared, 16)
                sp.wait_ge(scattered, 16 * NT)
                for b in range(0, NT, CHUNK):
                    sp.dma_start(src[:, b:b + CHUNK, :], rows.rearrange("(b r) n -> r b n", r=P)[:, b:b + CHUNK, :]).then_inc(in_, 16)

            @block.gpsimd
            def _(pool):
                pool.wait_ge(cleared, 16 * NT // CHUNK)
                pool.wait_ge(to_ready, 1)
                for t in range(NT):
                    pool.indirect_dma_start(rows, bass.IndirectOffsetOnAxis(ap=to[:, t:t + 1], axis=0), src[:, t, :], None,
                                            bounds_check=N - 1, oob_is_err=False).then_inc(scattered, 16)

            @block.tensor
            def _(pe):
                pe.wait_ge(counted, 1)
                pe.matmul(earlier[:, 0:1], K.before[0:P, 0:P], incl[:, NT - 1:NT], start=True, stop=True).then_inc(summed, 1)

            @block.vector
            def _(dve):
                link = S.link(dve, "l")
                dve.memset(zeros[:, :, :], 0.0).then_inc(zeroed, 1)
                dve.wait_ge(zeroed, 1)
                for part in packed:
                    dve.tensor_copy(part[:, NT, :], zeros[:, 0, :])
                dve.wait_ge(loaded, 16)
                link(dve.tensor_single_scalar(has[:, :], count[:, :], 0.0, ALU.is_gt))
                dve.tensor_tensor_scan(incl[:, :], has[:, :], has[:, :], 0.0, ALU.add, ALU.bypass).then_inc(counted, 1)
                dve.wait_ge(summed, 1)
                link(dve.tensor_copy(far[:, 0:1], earlier[:, 0:1]))
                link(dve.tensor_scalar(rank[:, :], incl[:, :], far[:, 0:1], -1.0, ALU.add, ALU.add))
                dve.tensor_copy(by_node[:, :, 0], rank[:, :])
                link(dve.tensor_scalar(far[:, :], has[:, :], -float(FAR), float(FAR), ALU.mult, ALU.add))
                link(dve.tensor_tensor(rank[:, :], rank[:, :], far[:, :], ALU.max))
                dve.tensor_copy(to[:, :], rank[:, :]).then_inc(to_ready, 1)
                dve.wait_ge(in_, 16 * NT // CHUNK)
                link(dve.tensor_copy(packed[0][:, 0:NT, :], src[:, :, :]))
                link(dve.tensor_tensor(packed[1][:, 0:NT, :], src[:, :, :], packed[0][:, 0:NT, :].bitcast(fp32), ALU.subtract))


def blocks(K, name, by_edge, block_of):
    nc = K.nc
    S = Stage(K, name)
    with S.ctx:
        x = S.sb("x", [P, ET])
        b = S.sb("b", [P, ET])
        over_ = S.sb("over", [P, ET])
        whole = S.sb("whole", [P, ET], i32)
        words = S.sb("words", [P, G])
        row = S.ps("row", [P, 512])
        spread_ = S.sem("sp")
        with nc.Block() as block:

            @block.tensor
            def _(pe):
                pe.matmul(row[:, 0:ET], over(K.ident[0:P, 0:1], [P, P]), by_edge[:, :], start=True, stop=True).then_inc(spread_, 1)

            @block.vector
            def _(dve):
                link = S.link(dve, "l")
                dve.wait_ge(spread_, 1)
                link(dve.tensor_scalar(x[:, :], row[:, 0:ET], 0.5, 1.0 / P, ALU.add, ALU.mult))
                link(dve.tensor_copy(whole[:, :], x[:, :]))
                link(dve.tensor_copy(b[:, :], whole[:, :]))
                link(dve.tensor_tensor(over_[:, :], b[:, :], x[:, :], ALU.is_gt))
                link(dve.tensor_tensor(b[:, :], b[:, :], over_[:, :], ALU.subtract))
                of = b[:, :].rearrange("p (g j) -> p j g", j=GT)
                link(dve.tensor_copy(words[:, :], of[:, GT - 1, :]))
                for j in range(GT - 2, -1, -1):
                    link(dve.scalar_tensor_tensor(words[:, :], words[:, :], float(FIELD), of[:, j, :], ALU.mult, ALU.add))
                dve.tensor_copy(block_of[:, :], words[:, :])
                link(dve.scalar_tensor_tensor(by_edge[:, :], b[:, :], -float(P), by_edge[:, :], ALU.mult, ALU.add))


def edge_scores(K, name, a, packed, place, block_of, k):
    nc = K.nc
    S = Stage(K, name)
    AW = REC_W[1] - 4
    with S.ctx:
        at = [S.sb(f"at{i}", [P, GT, 2], i32) for i in range(2)]
        got = [S.sb(f"got{i}", [P, GT, D]) for i in range(2)]
        mine = [S.sb(f"mine{i}", [P, GT]) for i in range(2)]
        pick = [[S.sb(f"pick{i}{h}", [P, GT, P], fp32r) for h in range(2)] for i in range(2)]
        column = S.sb("column", [P, 2])
        attr = [S.sb(f"attr{i}", [P, GT, AW]) for i in range(2)]
        attrT = [S.sb(f"attrT{i}", [AW, GT, P]) for i in range(2)]
        keyed = [S.sb(f"keyed{i}", [P, GT, D]) for i in range(2)]
        prod = [S.sb(f"prod{i}", [P, GT, D]) for i in range(2)]
        dots = [S.sb(f"dots{i}", [P, GT, HEADS]) for i in range(2)]
        We = S.sb("We", [AW, DH])
        T = S.ps("T", [AW, GT, 128])
        ep = [S.ps(f"ep{i}", [P, GT, 128]) for i in range(2)]
        places_row = S.ps("prow", [P, GT, 128])
        qx = [S.ps(f"qx{i}", [P, GT, D]) for i in range(2)]
        mine_ready, row_ready, picks_ready, q_ready, column_ready = (S.sem(x) for x in ("mi", "ro", "pi", "q", "co"))
        keys_done = S.sem("kd")
        at_ready, taken, turned, copied, ep_ready, loaded = (S.sem(x) for x in ("at", "tk", "tr", "cp", "ep", "ld"))
        gathered = [S.indirect(f"gat{i}") for i in range(2)]
        attr_in = [S.sem(f"attr{i}") for i in range(2)]
        with nc.Block() as block:

            @block.gpsimd
            def _(pool):
                for h in range(2):
                    pool.iota(column[:, h:h + 1], pattern=[[0, 1]], base=h * P, channel_multiplier=1,
                              allow_small_or_imprecise_dtypes=True).then_inc(column_ready, 1)

                def gather(g, slot, turn):
                    hold(K, pool, at_ready, g + 1)
                    hold(K, pool, keys_done, g - 1)
                    for j in range(GT):
                        pool.indirect_dma_start(got[slot][:, j, :], None, k,
                                                bass.IndirectOffsetOnAxis(ap=at[slot][:, j, 0:1], axis=0)).then_inc(gathered[slot], 16)

                skewed(pool, G, [(0, gather)])

            @block.sync
            def _(sp):
                sp.dma_start(We[:, :], a["L1_gnn_We"]).then_inc(loaded, 16)

                def load(g, slot, turn):
                    await_(sp, turned, g - 1)
                    sp.dma_start(attr[slot][:, :, :], K.rec[1][0:E, :].rearrange("(t p) c -> p t c", p=P)[:, bass.ds(g * GT, GT), 4:4 + AW]).then_inc(attr_in[slot], 16)

                skewed(sp, G, [(0, load)])

            @block.tensor
            def _(pe):
                pe.wait_ge(loaded, 16)

                def turn_(g, slot, turn):
                    pe.wait_ge(attr_in[slot], 16 * turn + 16)
                    hold(K, pe, copied, g)
                    for j in range(GT):
                        ins = pe.transpose(T[:, j, 0:P], attr[slot][:, j, :], K.ident[0:P, 0:P])
                    ins.then_inc(turned, 1)

                def multiply(g, slot, turn):
                    hold(K, pe, copied, g + 1)
                    hold(K, pe, keys_done, g - 1)
                    for j in range(GT):
                        ins = pe.matmul(ep[slot][:, j, 0:DH], attrT[slot][:, j, :], We[:, :], start=True, stop=True)
                    ins.then_inc(ep_ready, 1)

                def row(g, slot, turn):
                    hold(K, pe, mine_ready, g + 1)
                    hold(K, pe, picks_ready, g)
                    for j in range(GT):
                        ins = pe.matmul(places_row[:, j, 0:P], over(mine[slot][:, j:j + 1], [P, P]), K.ident[0:P, 0:P], start=True, stop=True)
                    ins.then_inc(row_ready, 1)

                def expand(g, slot, turn):
                    hold(K, pe, picks_ready, g + 1)
                    hold(K, pe, taken, g - 1)
                    word = pe.value_load(block_of[0:1, bass.ds(g, 1)], min_val=0, max_val=FIELD ** GT - 1)
                    for j in range(GT):
                        b = ((word >> (5 * j)) & (FIELD - 1)).with_bounds(min_val=0, max_val=NT - 1)
                        for h in range(2):
                            for x in range(2):
                                ins = pe.matmul(qx[slot][:, j, :], pick[slot][h][:, j, :], packed[x][:, bass.ds(b + h, 1), :].rearrange("p o n -> p (o n)"),
                                                start=(h == 0 and x == 0), stop=(h == 1 and x == 1))
                    ins.then_inc(q_ready, 1)

                skewed(pe, G, [(1, row), (2, expand), (1, multiply), (0, turn_)])

            @block.scalar
            def _(act):
                def copy(g, slot, turn):
                    hold(K, act, ep_ready, g - 1)
                    act.wait_ge(turned, g + 1)
                    act.activation(attrT[slot][:, :, :], T[:, :, 0:P], ACT.Copy).then_inc(copied, 1)

                def take(g, slot, turn):
                    hold(K, act, row_ready, g - 1)
                    act.activation(mine[slot][:, :], place[:, bass.ds(g * GT, GT)], ACT.Copy).then_inc(mine_ready, 1)

                skewed(act, G, [(0, take), (0, copy)])

            @block.vector
            def _(dve):
                link = S.link(dve, "l")

                def indices_(g, slot, turn):
                    hold(K, dve, gathered[slot], 64 * turn)
                    dve.tensor_copy(at[slot][:, :, :], K.idx[1][:, bass.ds(g * GT, GT), :]).then_inc(at_ready, 1)

                def pick_(g, slot, h):
                    ins = dve.tensor_scalar(pick[slot][h][:, :, :], places_row[:, :, 0:P], column[:, h:h + 1], None, ALU.is_equal)
                    if h == 1:
                        ins.then_inc(picks_ready, 1)

                def picks(g, slot, turn):
                    hold(K, dve, row_ready, g + 1)
                    hold(K, dve, q_ready, g - 1)
                    for h in range(2):
                        pick_(g, slot, h)

                def score(g, slot, turn):
                    more = not (isinstance(g, int) and g == G - 1)
                    link.restart()
                    dve.wait_ge(gathered[slot], 64 * turn + 64)
                    dve.wait_ge(ep_ready, g + 1)
                    dve.tensor_tensor(keyed[slot][:, :, :].rearrange("p j (h d) -> p j h d", d=DH),
                                      got[slot][:, :, :].rearrange("p j (h d) -> p j h d", d=DH),
                                      over(ep[slot][:, :, 0:DH].unsqueeze(2), [P, GT, HEADS, DH]), ALU.add).then_inc(keys_done, 1)
                    if more:
                        hold(K, dve, row_ready, g + 2)
                        hold(K, dve, q_ready, g)
                        pick_(g + 1, 1 - slot, 0)
                    hold(K, dve, q_ready, g + 1)
                    dve.wait_ge(keys_done, g + 1)
                    dve.tensor_tensor(prod[slot][:, :, :], keyed[slot][:, :, :], qx[slot][:, :, :], ALU.mult).then_inc(taken, 1)
                    if more:
                        pick_(g + 1, 1 - slot, 1)
                    dve.wait_ge(taken, g + 1)
                    link.mark(dve.reduce_sum(dots[slot][:, :, :], prod[slot][:, :, :].rearrange("p j (h d) -> p j h d", d=DH), AX.X))

                def scale(g, slot, turn):
                    dve.wait_ge(link.sem, link.n)
                    groups = bass.ds(g * GT, GT)
                    link(dve.scalar_tensor_tensor(K.scores[:, groups, :], dots[slot][:, :, :], DH ** -0.5,
                                                  over(K.fk[1][:, groups, 1:2], [P, GT, HEADS]), ALU.mult, ALU.mult))

                def first_picks(g, slot, turn):
                    if isinstance(g, int) and g == 0:
                        picks(g, slot, turn)

                dve.wait_ge(column_ready, 2)
                skewed(dve, G, [(0, indices_), (1, first_picks), (2, score), (2, scale)], peel=1)


def softmax_numerators(K, name):
    nc = K.nc
    S = Stage(K, name)
    PT = ET // SCAN
    L = PT * P
    C = SCAN * HEADS
    with S.ctx:
        s = S.sb("s", [C, L])
        key = S.sb("key", [C, L])
        pen = S.sb("pen", [C, L + 1])
        fwd = S.sb("fwd", [C, L])
        bwd = S.sb("bwd", [C, L])
        parted = S.sb("parted", [P, 2, PT, SCAN, HEADS])
        col = S.sb("col", [C, 4])
        rows = S.sb("rows", [1, 4, C])
        small = S.sb("small", [1, 8, C])
        back = S.sb("back", [C, 2])
        big = S.sb("big", [C, 1])
        zero = S.sb("zero", [C, L], u32)
        ps = [S.ps(f"ps{i}", [C, GT, 128]) for i in range(7)]
        bank = S.ps("bank", [C, 512])
        turned, copied, keys_turned, keys_copied = S.sem("t"), S.sem("c"), S.sem("kt"), S.sem("kc")
        cols_ready, rows_ready, edges_ready, edges_back, max_ready, exped = (S.sem(x) for x in ("co", "ro", "er", "eb", "mr", "ex"))
        out_turned, out_copied, parted_ready = S.sem("ot"), S.sem("oc"), S.sem("pr")
        where = [(j // GT, j % GT) for j in range(PT)]
        with nc.Block() as block:

            @block.tensor
            def _(pe):
                pe.wait_ge(parted_ready, 1)
                for x, (done, before) in enumerate(((turned, None), (keys_turned, copied))):
                    for j, (b, i) in enumerate(where):
                        if before is not None and i == 0:
                            pe.wait_ge(before, b + 1)
                        ins = pe.transpose(ps[b][:, i, 0:P], parted[:, x, j, :, :].rearrange("p c h -> p (c h)"), K.ident[0:P, 0:P])
                        if i == GT - 1 or j == PT - 1:
                            ins.then_inc(done, 1)
                pe.wait_ge(cols_ready, 1)
                for i in range(4):
                    ins = pe.matmul(bank[0:1, i * C:(i + 1) * C], col[:, i:i + 1], K.ident[:, :], start=True, stop=True)
                ins.then_inc(rows_ready, 1)
                pe.wait_ge(edges_ready, 1)
                for i in range(2):
                    ins = pe.matmul(bank[:, i:i + 1], small[0:1, 6 + i, :], K.ones[0:1, 0:1], start=True, stop=True)
                ins.then_inc(edges_back, 1)
                pe.wait_ge(exped, 1)
                for j, (b, i) in enumerate(where):
                    ins = pe.transpose(ps[b][0:P, i, :], fwd[:, j * P:(j + 1) * P], K.ident[:, :])
                    if i == GT - 1 or j == PT - 1:
                        ins.then_inc(out_turned, 1)

            @block.scalar
            def _(act):
                for dst, done, told in ((s, turned, copied), (key, keys_turned, keys_copied)):
                    for b in range(7):
                        n = min(GT, PT - b * GT)
                        act.wait_ge(done, b + 1)
                        act.activation(dst[:, b * GT * P:(b * GT + n) * P].rearrange("c (j e) -> c j e", e=P), ps[b][:, 0:n, 0:P], ACT.Copy).then_inc(told, 1)
                act.wait_ge(max_ready, 1)
                act.activation(fwd[:, :], s[:, :], ACT.Exp).then_inc(exped, 1)
                for j, (b, i) in enumerate(where):
                    if i == 0:
                        act.wait_ge(out_turned, b + 1)
                    act.activation(K.scores[:, j:ET:PT, :], ps[b][0:P, i, :].rearrange("p (c h) -> p c h", h=HEADS), ACT.Copy).then_inc(out_copied, 1)
                act.wait_ge(out_copied, PT)

            @block.vector
            def _(dve):
                link = S.link(dve, "l")
                dve.tensor_copy(parted[:, 0, :, :, :], K.scores[:, :, :].rearrange("p (c j) h -> p j c h", j=PT))
                dve.tensor_copy(parted[:, 1, :, :, :], over(K.fk[1][:, :, 0].rearrange("p (c j) -> p j c", j=PT).unsqueeze(3), [P, PT, SCAN, HEADS])).then_inc(parted_ready, 1)
                link(dve.memset(pen[:, :], -1e30))
                link(dve.memset(zero[:, :], 0))
                dve.wait_ge(keys_copied, 7)
                link(dve.tensor_tensor(pen[:, 1:L], key[:, 1:L], key[:, 0:L - 1], ALU.is_equal))
                link(dve.tensor_scalar(pen[:, 1:L], pen[:, 1:L], -1.0, 1e30, ALU.add, ALU.mult))
                link(dve.tensor_tensor_scan(fwd[:, :], pen[:, 0:L], s[:, :], -1e30, ALU.add, ALU.max))
                link(dve.tensor_tensor_scan(bwd[:, ::-1], pen[:, L:0:-1], s[:, ::-1], -1e30, ALU.add, ALU.max))
                dve.tensor_copy(col[:, 0:1], key[:, 0:1])
                dve.tensor_copy(col[:, 1:2], key[:, L - 1:L])
                dve.tensor_copy(col[:, 2:3], fwd[:, L - 1:L])
                dve.tensor_copy(col[:, 3:4], bwd[:, 0:1]).then_inc(cols_ready, 1)
                dve.wait_ge(rows_ready, 1)
                link(dve.tensor_copy(rows[:, :, :].rearrange("o i (h c) -> o i h c", h=HEADS),
                                     bank[0:1, :].rearrange("o (i c h) -> o i h c", i=4, h=HEADS)))
                first, last_, fend, bbeg = (rows[:, i, :].rearrange("o (h c) -> o h c", h=HEADS) for i in range(4))
                v = [small[:, i, :].rearrange("o (h c) -> o h c", h=HEADS) for i in range(8)]
                link(dve.memset(small[:, :, :], 0.0))
                link(dve.tensor_tensor(v[0][:, :, 1:SCAN], first[:, :, 1:SCAN], last_[:, :, 0:SCAN - 1], ALU.is_equal))
                link(dve.tensor_tensor(v[1][:, :, :], first, last_, ALU.is_equal))
                link(dve.tensor_tensor(v[2][:, :, :], v[1], v[0], ALU.mult))
                link(dve.tensor_tensor(v[3][:, :, 0:SCAN - 1], v[1][:, :, 0:SCAN - 1], v[0][:, :, 1:SCAN], ALU.mult))
                for i in (2, 3):
                    link(dve.tensor_scalar(small[:, i, :], small[:, i, :], -1.0, 1e30, ALU.add, ALU.mult))
                link(dve.tensor_tensor_scan(small[:, 4, :], small[:, 2, :], rows[:, 2, :], -1e30, ALU.add, ALU.max))
                link(dve.tensor_tensor_scan(small[:, 5, ::-1], small[:, 3, ::-1], rows[:, 3, ::-1], -1e30, ALU.add, ALU.max))
                link(dve.memset(small[:, 6:8, :], -1e30))
                into = [small[:, i, :].rearrange("o (c h) -> o h c", h=HEADS) for i in (6, 7)]
                link(dve.tensor_scalar(v[1][:, :, :], v[0], -1.0, 1e30, ALU.add, ALU.mult))
                link(dve.tensor_tensor(into[0][:, :, 1:SCAN], v[4][:, :, 0:SCAN - 1], v[0][:, :, 1:SCAN], ALU.mult))
                link(dve.tensor_tensor(into[0][:, :, 1:SCAN], into[0][:, :, 1:SCAN], v[1][:, :, 1:SCAN], ALU.add))
                link(dve.tensor_tensor(into[1][:, :, 0:SCAN - 1], v[5][:, :, 1:SCAN], v[0][:, :, 1:SCAN], ALU.mult))
                dve.tensor_tensor(into[1][:, :, 0:SCAN - 1], into[1][:, :, 0:SCAN - 1], v[1][:, :, 1:SCAN], ALU.add).then_inc(edges_ready, 1)
                link(dve.tensor_tensor(fwd[:, :], fwd[:, :], bwd[:, :], ALU.max))
                dve.wait_ge(edges_back, 1)
                link(dve.tensor_copy(back[:, :], bank[:, 0:2]))
                for i in range(2):
                    link(dve.tensor_scalar(bwd[:, :], key[:, :], col[:, i:i + 1], None, ALU.is_equal))
                    link(dve.tensor_scalar(pen[:, 0:L], bwd[:, :], -1.0, 1e30, ALU.add, ALU.mult))
                    link(dve.scalar_tensor_tensor(bwd[:, :], bwd[:, :], back[:, i:i + 1], pen[:, 0:L], ALU.mult, ALU.add))
                    link(dve.tensor_tensor(fwd[:, :], fwd[:, :], bwd[:, :], ALU.max))
                link(dve.tensor_scalar(bwd[:, :].bitcast(u32), fwd[:, :], FLT_MAX, None, ALU.is_gt))
                link(dve.copy_predicated(fwd[:, :], bwd[:, :].bitcast(u32), zero[:, :].bitcast(fp32)))
                link(dve.tensor_scalar(bwd[:, :].bitcast(u32), fwd[:, :], -FLT_MAX, None, ALU.is_lt))
                link(dve.copy_predicated(fwd[:, :], bwd[:, :].bitcast(u32), zero[:, :].bitcast(fp32)))
                dve.tensor_tensor(s[:, :], s[:, :], fwd[:, :], ALU.subtract).then_inc(max_ready, 1)


def attention_layer(K, a):
    nc = K.nc
    Kt, V = (K.dram(n, (N, D)) for n in ("aK", "aV"))
    normalise(K, "a0_", K.X, K.H)
    S = Stage(K, "as_")
    with S.ctx:
        K.scores = S.sb("scores", [P, ET, HEADS])
        SQ = Stage(K, "aq_")
        with SQ.ctx:
            packed = [SQ.sb(f"packed{x}", [P, NT + 1, D], fp32r) for x in "lr"]
            by_node = SQ.sb("by_node", [P, NT, 2])
            place = SQ.sb("place", [P, ET])
            block_of = SQ.sb("block_of", [P, G], i32)
            SN = Stage(K, "an_")
            with SN.ctx:
                H2 = SN.sb("H2", [P, NT, D])
                normalise(K, "a1_", K.H, H2, a["L1_gnn_ln1_g"], a["L1_gnn_ln1_b"])
                project(K, "a2_", H2, [a["L1_gnn_W" + c] for c in "kv"], [a["L1_gnn_b" + c] for c in "kv"], [Kt, V], head_bias=a["L1_gnn_be"])
                Q = H2
                project(K, "ap_", H2, [a["L1_gnn_Wq"]], [a["L1_gnn_bq"]], None, into=Q)
                pack(K, "ar_", 1, Q, by_node, packed)
            spread(K, "at_", 1, by_node, place)
            blocks(K, "au_", place, block_of)
            edge_scores(K, "a3_", a, packed, place, block_of, Kt)
        softmax_numerators(K, "a4_")
        edge_sums(K, "a5_", ATTEND, 1, [V], [0], D + HEADS)
    S = Stage(K, "ab_")
    with S.ctx:
        agg = S.sb("agg", [P, NT, D + HEADS])
        rec = S.sb("rec", [P, NT, HEADS])
        H2 = S.sb("H2", [P, NT, D])
        ab = S.sb("ab", [P, 2])
        done, loaded = S.sem("done"), S.sem("ld")
        collect(K, "a6_", 1, D + HEADS, agg)
        with nc.Block() as block:

            @block.sync
            def _(sp):
                sp.dma_start(ab[:, 0:1], a["L1_gnn_alpha"].partition_broadcast(P)).then_inc(loaded, 16)
                sp.wait_ge(loaded, 16)

            @block.vector
            def _(dve):
                link = S.link(dve, "l")
                link(dve.tensor_scalar(rec[:, :, :], agg[:, :, D:D + HEADS], 1e-30, None, ALU.max))
                link(dve.reciprocal(rec[:, :, :], rec[:, :, :]))
                for t in range(NT):
                    ins = dve.tensor_tensor(agg[:, t, 0:D].rearrange("p (h d) -> p h d", d=DH), agg[:, t, 0:D].rearrange("p (h d) -> p h d", d=DH),
                                            over(rec[:, t, :].unsqueeze(2), [P, HEADS, DH]), ALU.mult)
                link(ins)

        project(K, "a7_", agg, [a["L1_gnn_Wo"]], [a["L1_gnn_bo"]], None, into=H2)
        with nc.Block() as block:

            @block.vector
            def _(dve):
                link = S.link(dve, "l2")
                link(dve.scalar_tensor_tensor(K.H[:, :, :].rearrange("p t w -> p (t w)"), H2[:, :, :].rearrange("p t w -> p (t w)"), ab[:, 0:1],
                                              K.H[:, :, :].rearrange("p t w -> p (t w)"), ALU.mult, ALU.add))
                link(dve.tensor_tensor(K.X[:, :, :], K.X[:, :, :], K.H[:, :, :], ALU.add))

    S = Stage(K, "ac_")
    with S.ctx:
        ab = S.sb("ab", [P, 2])
        loaded = S.sem("ld")
        with nc.Block() as block:

            @block.sync
            def _(sp):
                sp.dma_start(ab[:, 1:2], a["L1_gnn_beta"].partition_broadcast(P)).then_inc(loaded, 16)
                sp.wait_ge(loaded, 16)

        normalise(K, "a8_", K.H, K.H, a["L1_gnn_ln2_g"], a["L1_gnn_ln2_b"])
        T = tuple(S.sb(f"T{i}", [128, 2, NT * 128], fp32r) for i in range(2))
        turn(K, "a9_", K.H, T)
        feed_forward(K, "aa_", [T], 8, a["L1_gnn_W1"], a["L1_gnn_b1"], a["L1_gnn_W2"], a["L1_gnn_b2"], ACT.Gelu, K.X, factor=ab[:, 1:2])


def switch_layer(K, a):
    nc = K.nc
    EX, F = 8, 8
    ROOM = -(-N * 125 // (100 * EX))
    SLOT = 512
    buf, ybuf = K.dram("buf", (EX * SLOT, D)), K.dram("ybuf", (EX * SLOT, D))
    normalise(K, "s0_", K.X, K.H)
    S = Stage(K, "s_")
    with S.ctx:
        logit = S.sb("logit", [P, NT, EX])
        row = S.sb("row", [P, 2, NT], i32)
        wt = S.sb("wt", [P, NT])
        S2 = Stage(K, "sa_")
        with S2.ctx:
            turn(K, "s1_", K.H, None, gate=(a["L1_ffn_gate_w"], a["L1_ffn_gate_b"], EX, logit))
        S2 = Stage(K, "sb_")
        with S2.ctx:
            prob = S2.sb("prob", [P, NT, EX])
            m = S2.sb("m", [P, 6, NT])
            top = S2.sb("top", [P, NT, 8])
            which = S2.sb("which", [P, NT, 8], u32)
            hot = S2.sb("hot", [P, NT, EX])
            incl = S2.sb("incl", [P, NT, EX])
            zeros = S2.sb("zeros", [128, 8, D])
            earlier = S2.ps("earlier", [P, 512])
            shifted, exped, counted, summed, zero_set = (S2.sem(x) for x in ("sh", "ex", "cn", "sm", "z"))
            row_ready, cleared, scattered = S2.sem("row"), S2.sem("clr"), S2.indirect("ind")
            wide = [P, NT, EX]
            with nc.Block() as block:

                @block.vector
                def _(dve):
                    link = S2.link(dve, "l")
                    dve.memset(zeros[:, :, :], 0.0).then_inc(zero_set, 1)
                    link(dve.reduce_max(m[:, 0, :], logit[:, :, :], AX.X))
                    dve.tensor_tensor(logit[:, :, :], logit[:, :, :], over(m[:, 0, :].unsqueeze(2), wide), ALU.subtract).then_inc(shifted, 1)
                    dve.wait_ge(exped, 1)
                    link(dve.reduce_sum(m[:, 1, :], prob[:, :, :], AX.X))
                    link(dve.reciprocal(m[:, 2, :], m[:, 1, :]))
                    link(dve.tensor_tensor(prob[:, :, :], prob[:, :, :], over(m[:, 2, :].unsqueeze(2), wide), ALU.mult))
                    for t in range(NT):
                        ins = dve.max(top[:, t, :], prob[:, t, :])
                    link(ins)
                    for t in range(NT):
                        ins = dve.max_index(which[:, t, :], top[:, t, :], prob[:, t, :])
                    link(ins)
                    link(dve.tensor_copy(m[:, 3, :], which[:, :, 0]))
                    link(dve.tensor_tensor(hot[:, :, :], over(K.iota64[0:P, 0:EX].unsqueeze(1), wide), over(m[:, 3, :].unsqueeze(2), wide), ALU.is_equal))
                    for e in range(EX):
                        ins = dve.tensor_tensor_scan(incl[:, :, e], hot[:, :, e], hot[:, :, e], 0.0, ALU.add, ALU.bypass)
                    ins.then_inc(counted, 1)
                    dve.wait_ge(summed, 1)
                    link(dve.tensor_tensor(prob[:, :, :], incl[:, :, :], over(earlier[:, 0:EX].unsqueeze(1), wide), ALU.add))
                    link(dve.tensor_tensor(prob[:, :, :], prob[:, :, :], hot[:, :, :], ALU.mult))
                    link(dve.reduce_sum(m[:, 4, :], prob[:, :, :], AX.X))
                    link(dve.tensor_scalar(m[:, 5, :], m[:, 4, :], float(ROOM), None, ALU.is_le))
                    link(dve.tensor_tensor(wt[:, :], m[:, 5, :], top[:, :, 0], ALU.mult))
                    link(dve.tensor_scalar(m[:, 4, :], m[:, 4, :], float(ROOM), -1.0, ALU.min, ALU.add))
                    link(dve.scalar_tensor_tensor(m[:, 4, :], m[:, 3, :], float(SLOT), m[:, 4, :], ALU.mult, ALU.add))
                    link(dve.tensor_copy(row[:, 0, :], m[:, 4, :]))
                    link(dve.tensor_scalar(m[:, 5, :], m[:, 5, :], -2.0 * EX * SLOT, 2.0 * EX * SLOT, ALU.mult, ALU.add))
                    dve.tensor_tensor(row[:, 1, :], m[:, 4, :], m[:, 5, :], ALU.add).then_inc(row_ready, 1)

                @block.scalar
                def _(act):
                    act.wait_ge(shifted, 1)
                    act.activation(prob[:, :, :], logit[:, :, :], ACT.Exp).then_inc(exped, 1)

                @block.tensor
                def _(pe):
                    pe.wait_ge(counted, 1)
                    pe.matmul(earlier[:, 0:EX], K.before[0:P, 0:P], incl[:, NT - 1, :], start=True, stop=True).then_inc(summed, 1)

                @block.sync
                def _(sp):
                    sp.wait_ge(zero_set, 1)
                    for i in range(EX * SLOT // 1024):
                        sp.dma_start(buf[i * 1024:(i + 1) * 1024, :].rearrange("(p j) n -> p j n", p=128), zeros[:, :, :]).then_inc(cleared, 16)

                @block.gpsimd
                def _(pool):
                    pool.wait_ge(cleared, 16 * (EX * SLOT // 1024))
                    pool.wait_ge(row_ready, 1)
                    for t in range(NT):
                        pool.indirect_dma_start(buf, bass.IndirectOffsetOnAxis(ap=row[:, 1, t:t + 1], axis=0), K.H[:, t, :], None,
                                                bounds_check=EX * SLOT - 1, oob_is_err=False).then_inc(scattered, 16)
                    pool.wait_ge(scattered, 16 * NT)

        switch_experts(K, "s3_", a, buf, ybuf, SLOT, EX, F)
        S2 = Stage(K, "sc_")
        with S2.ctx:
            y = S2.sb("y", [P, NT, D])
            odd = S2.sb("odd", [P, NT, D], u32)
            value = S2.sb("value", [P, 4])
            gathered = [S2.indirect(f"g{c}") for c in range(NT // CHUNK)]
            with nc.Block() as block:

                @block.gpsimd
                def _(pool):
                    for t in range(NT):
                        pool.indirect_dma_start(y[:, t, :], None, ybuf, bass.IndirectOffsetOnAxis(ap=row[:, 0, t:t + 1], axis=0)).then_inc(gathered[t // CHUNK], 16)

                @block.vector
                def _(dve):
                    link = S2.link(dve, "l")
                    for i, v in enumerate((0.0, 1e4, -1e4)):
                        link(dve.memset(value[:, i:i + 1], v))
                    for c in range(NT // CHUNK):
                        tiles = slice(c * CHUNK, (c + 1) * CHUNK)
                        dve.wait_ge(gathered[c], 16 * CHUNK)
                        link(dve.tensor_tensor(y[:, tiles, :], y[:, tiles, :], over(wt[:, tiles].unsqueeze(2), [P, CHUNK, D]), ALU.mult))
                        flat, mask = y[:, tiles, :].rearrange("p t w -> p (t w)"), odd[:, tiles, :].rearrange("p t w -> p (t w)")
                        for i in range(3):
                            if i == 0:
                                link(dve.tensor_tensor(mask, flat, flat, ALU.not_equal))
                            else:
                                link(dve.tensor_scalar(mask, flat, (FLT_MAX, -FLT_MAX)[i - 1], None, (ALU.is_gt, ALU.is_lt)[i - 1]))
                            link(dve.copy_predicated(flat, mask, over(value[:, i:i + 1], [P, CHUNK * D])))
                        link(dve.tensor_tensor(K.X[:, tiles, :], K.X[:, tiles, :], y[:, tiles, :], ALU.add))


def switch_experts(K, name, a, buf, ybuf, SLOT, EX, F):
    nc = K.nc
    S = Stage(K, name)
    R = SLOT // 128
    H = F * 128
    with S.ctx:
        w1 = [S.sb(f"w1{i}", [128, 2, H]) for i in range(2)]
        c1 = [S.sb(f"c1{i}", [128, F]) for i in range(2)]
        w2 = [S.sb(f"w2{i}", [128, F, D]) for i in range(2)]
        c2 = [S.sb(f"c2{i}", [1, 2 * D]) for i in range(2)]
        rows = [S.sb(f"rows{i}", [128, R, D]) for i in range(2)]
        rowsT = [S.sb(f"rowsT{i}", [128, 2, SLOT]) for i in range(2)]
        hid = [S.sb(f"hid{i}", [128, SLOT]) for i in range(2)]
        res = [S.sb(f"res{i}", [128, R, D]) for i in range(2)]
        T = S.ps("T", [128, 2, SLOT])
        hp = [S.ps(f"hp{i}", [128, SLOT]) for i in range(2)]
        y = S.ps("y", [128, R, D])
        loaded = [S.sem(f"ld{i}") for i in range(2)]
        stored = [S.sem(f"st{i}") for i in range(2)]
        turned, copied, h_done, h_used, y_done, ready = (S.sem(x) for x in ("tr", "cp", "hd", "hu", "yd", "rd"))
        with nc.Block() as block:

            @block.sync
            def _(sp):
                def load(e, slot, turn):
                    await_(sp, y_done, (e - 1) * F)
                    one = bass.ds(e, 1)
                    sp.dma_start(w1[slot][:, :, :], a["L1_ffn_w1"][one].rearrange("o (k p) f -> p (o k) f", p=128)).then_inc(loaded[slot], 16)
                    sp.dma_start(c1[slot][:, :], a["L1_ffn_b1"][one, :].rearrange("o (f p) -> p (o f)", p=128), allow_slow_non_contiguous=True).then_inc(loaded[slot], 16)
                    sp.dma_start(w2[slot][:, :, :], a["L1_ffn_w2"][one].rearrange("o (f p) n -> p (o f) n", p=128)).then_inc(loaded[slot], 16)
                    for h in range(2):
                        sp.dma_start(c2[slot][:, h * D:(h + 1) * D], a["L1_ffn_b2"][one, :]).then_inc(loaded[slot], 16)
                    sp.dma_start(rows[slot][:, :, :], buf[bass.ds(e * SLOT, SLOT), :].rearrange("(r p) n -> p r n", p=128)).then_inc(loaded[slot], 16)

                def store(e, slot, turn):
                    sp.wait_ge(ready, e + 1)
                    sp.dma_start(ybuf[bass.ds(e * SLOT, SLOT), :].rearrange("(r p) n -> p r n", p=128), res[slot][:, :, :]).then_inc(stored[slot], 16)

                skewed(sp, EX, [(2, store), (0, load)])
                for u in range(2):
                    sp.wait_ge(stored[u], 16 * (EX // 2))

            @block.tensor
            def _(pe):
                def turn_(e, slot, turn):
                    pe.wait_ge(loaded[slot], 96 * (turn + 1))
                    hold(K, pe, copied, e)
                    for k in range(2):
                        for r in range(R):
                            ins = pe.transpose(T[:, k, r * 128:(r + 1) * 128], rows[slot][:, r, k * 128:(k + 1) * 128], K.ident[:, :])
                    ins.then_inc(turned, 1)

                def expert(e, slot, turn):
                    hold(K, pe, copied, e + 1)

                    def hidden(f):
                        await_(pe, h_used, e * F + (f - 1))
                        for k in range(2):
                            ins = pe.matmul(hp[f % 2][:, :], w1[slot][:, k, f * 128:(f + 1) * 128], rowsT[slot][:, k, :], start=(k == 0), stop=(k == 1))
                        ins.then_inc(h_done, 1)

                    def outward(f):
                        pe.wait_ge(h_used, e * F + (f + 1))
                        if f == 0:
                            await_(pe, ready, e)
                            for b in range(2):
                                pe.matmul(y[:, 2 * b:2 * b + 2, :].rearrange("p j n -> p (j n)"), K.ones[0:1, 0:128], c2[slot][0:1, :], start=True, stop=True)
                        for r in range(R):
                            ins = pe.matmul(y[:, r, :], hid[f % 2][:, r * 128:(r + 1) * 128], w2[slot][:, f, :], start=False, stop=True, skip_group_check=True)
                        ins.then_inc(y_done, 1)

                    hidden(0)
                    for f in range(1, F):
                        hidden(f)
                        outward(f - 1)
                    outward(F - 1)

                skewed(pe, EX, [(1, expert), (0, turn_)])

            @block.scalar
            def _(act):
                def copy(e, slot, turn):
                    hold(K, act, y_done, (e - 1) * F)
                    act.wait_ge(turned, e + 1)
                    act.activation(rowsT[slot][:, :, :], T[:, :, :], ACT.Copy).then_inc(copied, 1)

                def expert(e, slot, turn):
                    for f in range(F):
                        if f == 0:
                            hold(K, act, loaded[slot], 96 * (turn + 1))
                        hold(K, act, y_done, e * F + (f - 1))
                        act.wait_ge(h_done, e * F + (f + 1))
                        act.activation(hid[f % 2][:, :], hp[f % 2][:, :], ACT.Relu, bias=c1[slot][:, f:f + 1]).then_inc(h_used, 1)

                skewed(act, EX, [(1, expert), (0, copy)])

            @block.vector
            def _(dve):
                def finish(e, slot, turn):
                    hold(K, dve, stored[slot], 16 * turn)
                    dve.wait_ge(y_done, (e + 1) * F)
                    dve.tensor_copy(res[slot][:, :, :], y[:, :, :]).then_inc(ready, 1)

                skewed(dve, EX, [(0, finish)])


def gat_layer(K, a):
    nc = K.nc
    normalise(K, "g0_", K.X, K.H)
    for layer in (1, 2):
        pre = f"g{layer}"
        table = K.dram(pre + "t", (N, D + 1))
        S = Stage(K, pre + "e_")
        with S.ctx:
            by_node = S.sb("by_node", [P, NT, 2])
            by_edge = S.sb("by_edge", [P, ET])
            project(K, pre + "a_", K.H, [a[f"L2_gnn_W{layer}"]], [None], [table], score=a[f"L2_gnn_a{layer}"], own=by_node)
            spread(K, pre + "d_", 0, by_node, by_edge)
            edge_sums(K, pre + "b_", GAT, 0, [table], [1], D + 1, own=by_edge)
        S = Stage(K, pre + "_")
        with S.ctx:
            agg = S.sb("agg", [P, NT, D + 1])
            rec = S.sb("rec", [P, NT])
            neg = S.sb("neg", [P, NT, D])
            negative, exped = S.sem("neg"), S.sem("ex")
            collect(K, pre + "c_", 0, D + 1, agg)
            with nc.Block() as block:

                @block.vector
                def _(dve):
                    link = S.link(dve, "l")
                    link(dve.reciprocal(rec[:, :], agg[:, :, D]))
                    link(dve.tensor_tensor(K.H[:, :, :], agg[:, :, 0:D], over(rec[:, :].unsqueeze(2), [P, NT, D]), ALU.mult))
                    flat = K.H[:, :, :].rearrange("p t w -> p (t w)")
                    nflat = neg[:, :, :].rearrange("p t w -> p (t w)")
                    dve.tensor_scalar(nflat, flat, 0.0, None, ALU.min).then_inc(negative, 1)
                    dve.wait_ge(exped, 1)
                    link(dve.tensor_scalar(nflat, nflat, -1.0, None, ALU.add))
                    link(dve.scalar_tensor_tensor(flat, flat, 0.0, nflat, ALU.max, ALU.add))
                    if layer == 2:
                        link(dve.tensor_tensor(K.X[:, :, :], K.X[:, :, :], K.H[:, :, :], ALU.add))

                @block.scalar
                def _(act):
                    act.wait_ge(negative, 1)
                    act.activation(neg[:, :, :], neg[:, :, :], ACT.Exp).then_inc(exped, 1)


def depth_layer(K, a):
    nc = K.nc
    SELECTED = N // 2 - 1
    wrow = K.dram("wrow", (N,))
    normalise(K, "d0_", K.X, K.H)
    S = Stage(K, "d_")
    with S.ctx:
        T = tuple(S.sb(f"T{i}", [128, 2, NT * 128], fp32r) for i in range(2))
        w = S.sb("w", [P, NT, 1])
        wts = S.sb("wts", [P, NT, 1])
        turn(K, "d1_", K.H, T, gate=(a["L2_ffn_wr"], a["L2_ffn_br"], 1, w))
        S2 = Stage(K, "da_")
        with S2.ctx:
            row = S2.sb("row", [P, N])
            order = S2.sb("order", [P, N + NT])
            junk = S2.sb("junk", [P, N])
            junk2 = S2.sb("junk2", [P, N])
            minus = S2.sb("minus", [P, NT])
            v = S2.sb("v", [P, 6, NT])
            whole = S2.sb("whole", [P, NT], i32)
            stored, loaded, masks, minus_ready, signs = (S2.sem(x) for x in ("st", "ld", "m", "mi", "si"))
            with nc.Block() as block:

                @block.sync
                def _(sp):
                    sp.dma_start(wrow.rearrange("(p t) -> p t", t=NT), w[:, :, 0]).then_inc(stored, 16)
                    sp.wait_ge(stored, 16)
                    sp.dma_start(row[:, :], wrow.partition_broadcast(P)).then_inc(loaded, 16)

                @block.gpsimd
                def _(pool):
                    pool.memset(order[:, :], 1.0).then_inc(masks, 1)
                    pool.wait_ge(masks, 1)
                    pool.affine_select(out=order[:, :], in_=order[:, :], compare_op=ALU.is_gt, fill=1.0 / FAR, base=NT - 1,
                                       pattern=[[-1, N + NT]], channel_multiplier=NT).then_inc(masks, 1)

                @block.scalar
                def _(act):
                    link = S2.link(act, "la")
                    act.wait_ge(minus_ready, 1)
                    act.wait_ge(loaded, 16)
                    for t in range(NT):
                        link(act.activation(junk2[:, :], row[:, :], ACT.Sign, bias=minus[:, t:t + 1], accum_out=v[:, 0, t:t + 1]))
                    act.sem_inc(signs, 1)

                @block.vector
                def _(dve):
                    link = S2.link(dve, "l")
                    dve.tensor_scalar(minus[:, :], w[:, :, 0], -1.0, None, ALU.mult).then_inc(minus_ready, 1)
                    dve.wait_ge(loaded, 16)
                    dve.wait_ge(masks, 2)
                    for t in range(NT):
                        link(dve.scalar_tensor_tensor(junk[:, :], row[:, :], w[:, t, 0:1], order[:, NT - 1 - t:NT - 1 - t + N],
                                                      ALU.is_equal, ALU.mult, accum_out=v[:, 1, t:t + 1]))
                    sign, ties, sooner, later, t1, rank = (v[:, i, :] for i in range(6))
                    link(dve.tensor_copy(whole[:, :], ties))
                    link(dve.tensor_copy(sooner, whole[:, :]))
                    link(dve.tensor_tensor(t1, sooner, ties, ALU.is_gt))
                    link(dve.tensor_tensor(sooner, sooner, t1, ALU.subtract))
                    link(dve.tensor_tensor(later, ties, sooner, ALU.subtract))
                    link(dve.tensor_scalar(later, later, -float(FAR), float(N), ALU.mult, ALU.add))
                    link(dve.tensor_tensor(rank, later, sooner, ALU.add))
                    dve.wait_ge(signs, 1)
                    link(dve.tensor_tensor(rank, rank, sign, ALU.add))
                    link(dve.scalar_tensor_tensor(wts[:, :, 0], rank, 2.0 * SELECTED, w[:, :, 0], ALU.is_lt, ALU.mult))

        add_into(K, "d2_", K.X, K.H)
        feed_forward(K, "d3_", [T], 8, a["L2_ffn_w1"], a["L2_ffn_b1"], a["L2_ffn_w2"], a["L2_ffn_b2"], ACT.Gelu_apprx_tanh, K.X, by_tile=wts)


def conv_layer(K, a):
    nc = K.nc
    WT, table = K.dram("WT", (D, D)), K.dram("cT", (N, D + 1))
    normalise(K, "v0_", K.X, K.H)
    S = Stage(K, "va_")
    with S.ctx:
        w = S.sb("w", [128, 2, D])
        wt = S.sb("wt", [128, 2, D])
        ps = S.ps("ps", [128, 2, D])
        loaded, turned, copied, stored = (S.sem(x) for x in ("ld", "tr", "cp", "st"))
        with nc.Block() as block:

            @block.sync
            def _(sp):
                sp.dma_start(w[:, :, :], a["L3_gnn_W"].rearrange("(k p) i -> p k i", p=128)).then_inc(loaded, 16)
                sp.wait_ge(copied, 1)
                sp.dma_start(WT.rearrange("(k p) o -> p k o", p=128), wt[:, :, :]).then_inc(stored, 16)
                sp.wait_ge(stored, 16)

            @block.tensor
            def _(pe):
                pe.wait_ge(loaded, 16)
                for k in range(2):
                    for o in range(2):
                        ins = pe.transpose(ps[:, k, o * 128:(o + 1) * 128], w[:, o, k * 128:(k + 1) * 128], K.ident[:, :])
                ins.then_inc(turned, 1)

            @block.scalar
            def _(act):
                act.wait_ge(turned, 1)
                act.activation(wt[:, :, :], ps[:, :, :], ACT.Copy).then_inc(copied, 1)

    project(K, "v1_", K.H, [WT], [a["L3_gnn_b"]], [table])
    edge_sums(K, "v2_", COPY, 1, [table], [0], D + 1)
    S = Stage(K, "vb_")
    with S.ctx:
        agg = S.sb("agg", [P, NT, D + 1])
        rec = S.sb("rec", [P, NT])
        collect(K, "v3_", 1, D + 1, agg)
        with nc.Block() as block:

            @block.vector
            def _(dve):
                link = S.link(dve, "l")
                link(dve.tensor_scalar(rec[:, :], agg[:, :, D], 1.0, None, ALU.add))
                link(dve.reciprocal(rec[:, :], rec[:, :]))
                link(dve.tensor_tensor(K.H[:, :, :], agg[:, :, 0:D], over(rec[:, :].unsqueeze(2), [P, NT, D]), ALU.mult))
                link(dve.tensor_tensor(K.X[:, :, :], K.X[:, :, :], K.H[:, :, :], ALU.add))


def mixture_layer(K, a):
    nc = K.nc
    EX = 8
    CAPACITY = float(-(-N * 125 // (100 * EX)))
    normalise(K, "x0_", K.X, K.H)
    S = Stage(K, "x_")
    with S.ctx:
        T = tuple(S.sb(f"T{i}", [128, 2, NT * 128], fp32r) for i in range(2))
        which = S.sb("which", [P, 8], u32)
        w2 = S.sb("w2", [P, 2])
        S2 = Stage(K, "xa_")
        with S2.ctx:
            mean = S2.sb("mean", [128, 2])
            Wr = S2.sb("Wr", [128, 2, EX])
            br = S2.sb("br", [P, EX])
            v = S2.sb("v", [P, 8, EX])
            c = S2.sb("c", [P, 8])
            top = S2.sb("top", [P, 8])
            ps = [S2.ps(f"ps{i}", [128, 512]) for i in range(3)]
            loaded, summed, mean_ready, routed = (S2.sem(x) for x in ("ld", "sm", "mn", "rt"))
            shifted, exped = S2.sem("sh"), S2.sem("ex")
            with nc.Block() as block:

                @block.sync
                def _(sp):
                    sp.dma_start(Wr[:, :, :], a["L3_ffn_Wr"].rearrange("(k p) n -> p k n", p=128)).then_inc(loaded, 16)
                    sp.dma_start(br[:, :], a["L3_ffn_br"].partition_broadcast(P)).then_inc(loaded, 16)

                @block.tensor
                def _(pe):
                    pe.wait_ge(loaded, 32)
                    for k in range(2):
                        for t in range(NT):
                            ins = pe.matmul(ps[k][:, 0:1], K.H[:, t, k * 128:(k + 1) * 128], K.ones[0:P, 0:1], start=(t == 0), stop=(t == NT - 1))
                    ins.then_inc(summed, 1)
                    pe.wait_ge(mean_ready, 1)
                    for k in range(2):
                        ins = pe.matmul(ps[2][0:P, 0:EX], over(mean[:, k:k + 1], [128, P]), Wr[:, k, :], start=(k == 0), stop=(k == 1))
                    ins.then_inc(routed, 1)

                @block.scalar
                def _(act):
                    for i in range(2):
                        act.wait_ge(shifted, i + 1)
                        act.activation(v[:, 2, :], v[:, 1, :], ACT.Exp, accum_out=c[:, 1:2]).then_inc(exped, 1)
                    act.wait_ge(shifted, 3)
                    act.activation(c[:, 4:5], c[:, 3:4], ACT.Exp).then_inc(exped, 1)

                @block.vector
                def _(dve):
                    link = S2.link(dve, "l")
                    dve.wait_ge(summed, 1)
                    dve.tensor_scalar(mean[:, 0:1], ps[0][:, 0:1], 1.0 / N, None, ALU.mult)
                    dve.tensor_scalar(mean[:, 1:2], ps[1][:, 0:1], 1.0 / N, None, ALU.mult).then_inc(mean_ready, 1)
                    dve.wait_ge(routed, 1)
                    link(dve.tensor_tensor(v[:, 0, :], ps[2][0:P, 0:EX], br[:, :], ALU.add))

                    def softmax(i):
                        link(dve.reduce_max(c[:, 0:1], v[:, 0, :], AX.X))
                        dve.tensor_scalar(v[:, 1, :], v[:, 0, :], c[:, 0:1], None, ALU.subtract).then_inc(shifted, 1)
                        dve.wait_ge(exped, i + 1)
                        link(dve.reciprocal(c[:, 2:3], c[:, 1:2]))
                        link(dve.tensor_scalar(v[:, 3, :], v[:, 2, :], c[:, 2:3], None, ALU.mult))

                    softmax(0)
                    link(dve.tensor_scalar(v[:, 4, :], v[:, 3, :], float(N), None, ALU.mult))
                    link(dve.reciprocal(v[:, 5, :], v[:, 4, :]))
                    link(dve.tensor_scalar(v[:, 6, :], v[:, 4, :], CAPACITY, None, ALU.is_gt))
                    link(dve.scalar_tensor_tensor(v[:, 5, :], v[:, 5, :], CAPACITY, v[:, 6, :], ALU.mult, ALU.mult))
                    link(dve.tensor_scalar(v[:, 6, :], v[:, 6, :], -1.0, 1.0, ALU.mult, ALU.add))
                    link(dve.tensor_tensor(v[:, 5, :], v[:, 5, :], v[:, 6, :], ALU.add))
                    link(dve.tensor_tensor(v[:, 0, :], v[:, 3, :], v[:, 5, :], ALU.mult))
                    softmax(1)
                    link(dve.max(top[:, :], v[:, 3, :]))
                    link(dve.max_index(which[:, :], top[:, :], v[:, 3, :]))
                    dve.tensor_tensor(c[:, 3:4], top[:, 1:2], top[:, 0:1], ALU.subtract).then_inc(shifted, 1)
                    dve.wait_ge(exped, 3)
                    link(dve.tensor_scalar(c[:, 5:6], c[:, 4:5], 1.0, None, ALU.add))
                    link(dve.reciprocal(w2[:, 0:1], c[:, 5:6]))
                    link(dve.tensor_tensor(w2[:, 1:2], c[:, 4:5], w2[:, 0:1], ALU.mult))

        turn(K, "x1_", K.H, T)
        for i in range(2):
            feed_forward(K, f"x2{i}_", [T], 4, a["L3_ffn_W1"], a["L3_ffn_b1"], a["L3_ffn_W2"], a["L3_ffn_b2"], ACT.Gelu, K.H,
                         factor=w2[:, i:i + 1], chosen=which[0:1, i:i + 1])
    normalise(K, "x3_", K.H, K.H, a["L3_ffn_gamma"], a["L3_ffn_beta"])
    add_into(K, "x4_", K.X, K.H)


def store_result(K, out):
    stored = K.nc.alloc_semaphore("result")
    with K.nc.Block() as block:

        @block.sync
        def _(sp):
            sp.dma_start(nodes(out), K.X[:, :, :]).then_inc(stored, 16)
            sp.wait_ge(stored, 16)


def build(nc, a, out):
    K = Kernel()
    K.nc = nc
    shared(K, lambda name, shape, dt=fp32: nc.dram_tensor(name, shape, dt, kind="Internal").ap())
    constants(K, a)
    sort_edges(K, a)
    indices(K, 0)
    message_layer(K, a)
    top2_layer(K, a)
    indices(K, 1)
    attention_layer(K, a)
    switch_layer(K, a)
    gat_layer(K, a)
    depth_layer(K, a)
    conv_layer(K, a)
    mixture_layer(K, a)
    store_result(K, out)


def kernel(**inputs):
    import concourse.bacc as bacc
    from concourse.bass_utils import run_bass_kernel_spmd as run

    nc = bacc.Bacc("TRN2", target_bir_lowering=False, num_devices=1)
    arrays, a = {}, {}
    for name, value in inputs.items():
        if name == "L2_ffn_attention_mask":
            continue
        v = np.ascontiguousarray(value)
        arrays["in_" + name] = v
        a[name] = nc.dram_tensor("in_" + name, v.shape, mybir.dt.from_np(v.dtype), kind="ExternalInput").ap()
    out = nc.dram_tensor("out", (N, D), fp32, kind="ExternalOutput").ap()
    build(nc, a, out)
    return run(nc, [arrays], core_ids=[0]).results[0]["out"]
```
